# Optimizing a Trainium2 kernel written in Bass

```python
import numpy as np
import jax
import jax.numpy as jnp

def _softmax(x, axis=-1):
    return jax.nn.softmax(x, axis=axis)

def _gelu(x):
    return jax.nn.gelu(x, approximate=True)

def _silu(x):
    return jax.nn.silu(x)

def _sigmoid(x):
    return jax.nn.sigmoid(x)

def _layernorm(x, axis=-1, eps=1e-05):
    m = jnp.mean(x, axis=axis, keepdims=True)
    v = jnp.var(x, axis=axis, keepdims=True)
    return (x - m) / jnp.sqrt(v + eps)

def _scatter_add(tgt, idx, src, axis=0):
    return tgt.at[idx].add(src)

def _segment_sum(src, seg, n):
    return jax.ops.segment_sum(src, seg, n)
kernel_name = 'mk_gnn_preln_d2_gnn_r8_2a1bb1'

def setup_inputs(seed: int=0):
    np.random.seed(seed)
    _w = jnp.asarray

    def _rec_inputs():
        import jax
        import jax.numpy as jnp
        _gk = jax.random.key(seed)
        x = -6.415e-05 + 1 * jax.random.normal(jax.random.fold_in(_gk, 1), (6250, 256), jnp.float32)
        src = jax.random.randint(jax.random.fold_in(_gk, 2), (100000,), 0, 6250, jnp.int32)
        dst = jax.random.randint(jax.random.fold_in(_gk, 3), (100000,), 0, 6250, jnp.int32)
        _o = jnp.argsort(dst, stable=True)
        src = src[_o]
        dst = dst[_o]
        edge_type_16 = jax.random.randint(jax.random.fold_in(_gk, 12), (100000,), 0, 16, jnp.int32)
        edge_weight1 = jax.random.uniform(jax.random.fold_in(_gk, 13), (100000, 1), jnp.float32, 0.0, 1)
        return (x, src, dst, edge_type_16, edge_weight1)
    x, src, dst, edge_type_16, edge_weight1 = _rec_inputs()

    def _L0_gnn_setup():
        import jax, jax.numpy as jnp
        import numpy as np
        N = 5000
        E = 80000
        D = 256
        H = 8
        DH = D // H
        DFF = 4 * D
        SCALE = D ** (-0.5)
        EPS = 1e-05

        def layernorm(x, g, b):
            mu = jnp.mean(x, axis=-1, keepdims=True)
            var = jnp.mean(jnp.square(x - mu), axis=-1, keepdims=True)
            return (x - mu) * jax.lax.rsqrt(var + EPS) * g + b
        key = jax.random.key(seed)
        ks = jax.random.split(key, 12)
        inv = 1.0 / np.sqrt(D)
        invf = 1.0 / np.sqrt(DFF)
        return {'triplet_h': jax.random.normal(ks[0], (N, D), dtype=jnp.float32), 'src': jax.random.randint(ks[1], (E,), 0, N, dtype=jnp.int32), 'dst': jax.random.randint(ks[2], (E,), 0, N, dtype=jnp.int32), 'Wqkv': jax.random.uniform(ks[3], (D, 3 * D), jnp.float32, -inv, inv), 'bqkv': jax.random.uniform(ks[4], (3 * D,), jnp.float32, -inv, inv), 'ln_attn_g': jnp.ones((D,), jnp.float32), 'ln_attn_b': jnp.zeros((D,), jnp.float32), 'ln_res_g': jnp.ones((D,), jnp.float32), 'ln_res_b': jnp.zeros((D,), jnp.float32), 'W_in': jax.random.uniform(ks[5], (D, DFF), jnp.float32, -inv, inv), 'b_in': jax.random.uniform(ks[6], (DFF,), jnp.float32, -inv, inv), 'W_out': jax.random.uniform(ks[7], (DFF, D), jnp.float32, -invf, invf), 'b_out': jax.random.uniform(ks[8], (D,), jnp.float32, -invf, invf)}
    _L0_gnn_all = _L0_gnn_setup()
    _L0_gnn_in = {k: v for k, v in _L0_gnn_all.items() if k in ('Wqkv', 'bqkv', 'ln_attn_g', 'ln_attn_b', 'ln_res_g', 'ln_res_b', 'W_in', 'b_in', 'W_out', 'b_out')}
    del _L0_gnn_all

    def _L1_gnn_setup():
        import jax, jax.numpy as jnp
        import numpy as np
        N_NODES = 6250
        N_EDGES = 100000
        NUM_RELS = 16
        FEAT = 256
        OUT = 256
        key = jax.random.key(seed)
        ks = jax.random.split(key, 7)
        h = jax.random.normal(ks[0], (N_NODES, FEAT), dtype=jnp.float32)
        norm = jax.random.uniform(ks[1], (N_EDGES, 1), dtype=jnp.float32)
        weight = jax.random.normal(ks[2], (NUM_RELS, FEAT, OUT), dtype=jnp.float32) * 0.05
        gate_weight = jax.random.normal(ks[3], (NUM_RELS, FEAT, 1), dtype=jnp.float32) * 0.05
        src = jax.random.randint(ks[4], (N_EDGES,), 0, N_NODES)
        dst = jax.random.randint(ks[5], (N_EDGES,), 0, N_NODES)
        rel_type = jax.random.randint(ks[6], (N_EDGES,), 0, NUM_RELS)
        return {'h': h, 'norm': norm, 'weight': weight, 'gate_weight': gate_weight, 'src': src, 'dst': dst, 'rel_type': rel_type}
    _L1_gnn_all = _L1_gnn_setup()
    _L1_gnn_in = {k: v for k, v in _L1_gnn_all.items() if k in ('weight', 'gate_weight')}
    del _L1_gnn_all
    return {'x': x, 'src': src, 'dst': dst, 'edge_type_16': edge_type_16, 'edge_weight1': edge_weight1, 'L0_gnn_Wqkv': _L0_gnn_in['Wqkv'], 'L0_gnn_bqkv': _L0_gnn_in['bqkv'], 'L0_gnn_ln_attn_g': _L0_gnn_in['ln_attn_g'], 'L0_gnn_ln_attn_b': _L0_gnn_in['ln_attn_b'], 'L0_gnn_ln_res_g': _L0_gnn_in['ln_res_g'], 'L0_gnn_ln_res_b': _L0_gnn_in['ln_res_b'], 'L0_gnn_W_in': _L0_gnn_in['W_in'], 'L0_gnn_b_in': _L0_gnn_in['b_in'], 'L0_gnn_W_out': _L0_gnn_in['W_out'], 'L0_gnn_b_out': _L0_gnn_in['b_out'], 'L1_gnn_weight': _L1_gnn_in['weight'], 'L1_gnn_gate_weight': _L1_gnn_in['gate_weight']}

def reference(x, src, dst, edge_type_16, edge_weight1, L0_gnn_Wqkv, L0_gnn_bqkv, L0_gnn_ln_attn_g, L0_gnn_ln_attn_b, L0_gnn_ln_res_g, L0_gnn_ln_res_b, L0_gnn_W_in, L0_gnn_b_in, L0_gnn_W_out, L0_gnn_b_out, L1_gnn_weight, L1_gnn_gate_weight):
    import jax
    import jax.numpy as jnp

    def _L0_gnn_ref(triplet_h, src, dst, Wqkv, bqkv, ln_attn_g, ln_attn_b, ln_res_g, ln_res_b, W_in, b_in, W_out, b_out):
        import jax, jax.numpy as jnp
        import numpy as np
        N = 5000
        E = 80000
        D = 256
        H = 8
        DH = D // H
        DFF = 4 * D
        SCALE = D ** (-0.5)
        EPS = 1e-05

        def layernorm(x, g, b):
            mu = jnp.mean(x, axis=-1, keepdims=True)
            var = jnp.mean(jnp.square(x - mu), axis=-1, keepdims=True)
            return (x - mu) * jax.lax.rsqrt(var + EPS) * g + b
        n = triplet_h.shape[0]
        h = layernorm(triplet_h, ln_attn_g, ln_attn_b)
        qkv = (h @ Wqkv + bqkv).reshape(n, 3, H, DH)
        q = qkv[:, 0] * SCALE
        k = qkv[:, 1]
        v = qkv[:, 2]
        scores = jnp.einsum('ehd,ehd->eh', q[src], k[dst])
        m = jax.ops.segment_max(scores, dst, num_segments=n)
        e = jnp.exp(scores - m[dst])
        s = jax.ops.segment_sum(e, dst, num_segments=n)
        sa = e / s[dst]
        he = (v[src] * sa[:, :, None]).reshape(-1, D)
        agg = jax.ops.segment_sum(he, dst, num_segments=n)
        x = triplet_h + agg
        y = layernorm(x, ln_res_g, ln_res_b)
        y = jax.nn.gelu(y @ W_in + b_in, approximate=False) @ W_out + b_out
        return x + y

    def _L1_gnn_ref(h, norm, weight, gate_weight, src, dst, rel_type):
        import jax, jax.numpy as jnp
        import numpy as np
        N_NODES = 6250
        N_EDGES = 100000
        NUM_RELS = 16
        FEAT = 256
        OUT = 256
        n_nodes = h.shape[0]
        all_msg = jnp.einsum('nf,rfo->rno', h, weight)
        msg = all_msg[rel_type, src] * norm
        all_gate = jnp.einsum('nf,rf->rn', h, gate_weight[..., 0])
        gate = jax.nn.sigmoid(all_gate[rel_type, src])[:, None]
        msg = msg * gate
        agg = jax.ops.segment_sum(msg, dst, num_segments=n_nodes)
        return jax.nn.relu(agg)
    h = jnp.maximum(_layernorm(x, axis=-1), 0.0)
    x = x + _L0_gnn_ref(h, src, dst, L0_gnn_Wqkv, L0_gnn_bqkv, L0_gnn_ln_attn_g, L0_gnn_ln_attn_b, L0_gnn_ln_res_g, L0_gnn_ln_res_b, L0_gnn_W_in, L0_gnn_b_in, L0_gnn_W_out, L0_gnn_b_out)
    h = jnp.maximum(_layernorm(x, axis=-1), 0.0)
    x = x + _L1_gnn_ref(h, edge_weight1, L1_gnn_weight, L1_gnn_gate_weight, src, dst, edge_type_16)
    return x

_drawn_inputs = setup_inputs


def setup_inputs(seed=0):
    import zlib

    import numpy as np

    out = dict(_drawn_inputs(seed))
    spreads = {'L0_gnn_ln_attn_g': (1.0, 0.6),
     'L0_gnn_ln_attn_b': (0.0, 0.1),
     'L0_gnn_ln_res_g': (1.0, 0.6),
     'L0_gnn_ln_res_b': (0.0, 0.669)}
    factors = {'L0_gnn_b_in': 7.386, 'L0_gnn_b_out': 5.453}
    for name, (base, spread) in spreads.items():
        noise = np.random.default_rng([zlib.crc32(name.encode()), seed]).standard_normal(out[name].shape)
        drawn = base * np.exp(spread * noise) if base else spread * noise
        out[name] = jnp.asarray(drawn.astype(out[name].dtype))
    for name, factor in factors.items():
        out[name] = (out[name] * factor).astype(out[name].dtype)
    return out
```

```python
from contextlib import ExitStack

import concourse.bass as bass
from concourse import mybir

F32 = mybir.dt.float32
BF16 = mybir.dt.bfloat16
I32 = mybir.dt.int32
ALU = mybir.AluOpType
ACT = mybir.ActivationFunctionType
AX_X = mybir.AxisListType.X

P = 128
NODES, FEAT = 6250, 256
EDGES = 100000
HEADS = 8
HEAD_DIM = FEAT // HEADS
DFF = 4 * FEAT
RELS = 16
EPS = 1e-5
ATT_SCALE = float(FEAT) ** -0.5
KC = FEAT // P
FFC = DFF // P

NODE_TILES = -(-NODES // P)
NODES_PAD = NODE_TILES * P
LAST_ROWS = NODES - (NODE_TILES - 1) * P
GROUP = 7
GROUPS = NODE_TILES // GROUP
EDGE_TILES = -(-EDGES // P)
IC = 112
ICN = 7
EDGE_TILES_PAD = IC * ICN
EDGES_PAD = EDGE_TILES_PAD * P
UNROLL = 16
HALF = UNROLL // 2
STEPS = 832
assert EDGE_TILES + NODE_TILES - 1 <= STEPS and STEPS % UNROLL == 0
ROUNDS = STEPS // UNROLL
SH = STEPS // 2
DST_PAD = 6400
NOT_LAST = 4096
CHUNKS = P // HEADS
CHUNK_STEPS = STEPS // CHUNKS
CHUNK = CHUNK_STEPS * P
BIG = 1.0e30
AGGW = FEAT + HEADS
BLOCKS = STEPS // 16
ACC_RING = 8
PAIRS = RELS // 2


def gnn_program(nc, x, src, dst, rel, norm, wqkv, bqkv, g_attn, b_attn, g_res, b_res,
                w_in, b_in, w_out, b_out, w_rel, w_gate, out):
    def dram(name, shape, dt=F32):
        return nc.dram_tensor(name, shape, dt, kind="Internal").ap()

    h0_d = dram("h0_d", [NODES_PAD, FEAT])
    q_d = dram("q_d", [NODES_PAD, FEAT])
    v_d = dram("v_d", [NODES_PAD, FEAT])
    x1_d = dram("x1_d", [NODES_PAD, FEAT])
    msg_d = dram("msg_d", [NODES_PAD * RELS, FEAT])
    agg_d = dram("agg_d", [NODES_PAD, AGGW])
    agg1_d = dram("agg1_d", [NODES_PAD, FEAT])
    scores_d = dram("scores_d", [STEPS * HEADS, P])
    probs_d = dram("probs_d", [STEPS * HEADS, P])
    key_d = dram("key_d", [STEPS * P + 2 * P])

    with ExitStack() as whole:
        def sb(ctx, name, shape, dt=F32):
            return ctx.enter_context(nc.sbuf_tensor(name, shape, dt))

        def ps(ctx, name, shape, dt=F32):
            return ctx.enter_context(nc.psum_tensor(name, shape, dt))

        def sem(name):
            return whole.enter_context(nc.semaphore(name))

        iota_n = sb(whole, "iota_n", [P, P])
        ident = sb(whole, "ident", [P, P])
        ident_b = sb(whole, "ident_b", [P, P], BF16)
        part = sb(whole, "part", [P, 1])
        ones = sb(whole, "ones", [P, P])
        neg_half = sb(whole, "neg_half", [P, GROUP])
        dloc = sb(whole, "dloc", [P, STEPS + 2])
        keep = sb(whole, "keep", [P, STEPS])
        norm_s = sb(whole, "norm_s", [P, STEPS])
        src_i = sb(whole, "src_i", [P, STEPS], I32)
        msg_i = sb(whole, "msg_i", [P, STEPS], I32)
        tile_i = sb(whole, "tile_i", [P, STEPS], I32)
        store_i = sb(whole, "store_i", [P, STEPS], I32)
        idx_now = sb(whole, "idx_now", [P, 2, HALF], I32)

        build_steps(nc, sb, ps, sem, src, dst, rel, norm, key_d, iota_n, ident, ident_b, part, ones,
                    neg_half, dloc, keep, norm_s, src_i, msg_i, tile_i, store_i)
        with ExitStack() as att:
            k_all = sb(att, "k_all", [P, (NODE_TILES + 1) * FEAT])
            node_inputs(nc, sb, ps, sem, x, wqkv, bqkv, g_attn, b_attn, ident, neg_half,
                        h0_d, q_d, v_d, k_all)
            edge_scores(nc, sb, ps, sem, q_d, scores_d, k_all, iota_n, ident, ident_b, dloc, src_i, tile_i, idx_now)
        softmax_numerators(nc, sb, ps, sem, scores_d, probs_d, key_d, ident, ones)
        edge_sum(nc, sb, ps, sem, "att", v_d, agg_d, AGGW, probs_d, iota_n, ident, dloc, None, keep,
                 src_i, store_i, idx_now)
        node_update(nc, sb, ps, sem, x, g_res, b_res, w_in, b_in, w_out, b_out, w_rel, w_gate, ident,
                    neg_half, h0_d, agg_d, x1_d, msg_d)
        edge_sum(nc, sb, ps, sem, "rel", msg_d, agg1_d, FEAT, None, iota_n, ident, dloc, norm_s, keep,
                 msg_i, store_i, idx_now)
        finish(nc, sb, sem, x1_d, agg1_d, out)


def build_steps(nc, sb, ps, sem, src, dst, rel, norm, key_d, iota_n, ident, ident_b, part, ones,
                neg_half, dloc, keep, norm_s, src_i, msg_i, tile_i, store_i):
    loaded = sem("steps_loaded")
    consts = sem("consts_made")
    dve_did = sem("steps_dve")
    pe_did = sem("steps_pe")
    sel_free = sem("steps_sel_free")
    key_out = sem("key_out")
    with ExitStack() as ctx:
        cols_i = sb(ctx, "cols_i", [IC, 3, ICN, P], I32)
        cols = sb(ctx, "cols", [IC, 4, ICN, P])
        last_i = sb(ctx, "last_i", [1, EDGE_TILES_PAD], I32)
        last_f = sb(ctx, "last_f", [1, EDGE_TILES_PAD])
        step_no = sb(ctx, "step_no", [P, STEPS])
        bound = sb(ctx, "bound", [P, 1])
        full = sb(ctx, "full", [P, 1])
        pos = sb(ctx, "pos", [P, 1])
        scratch = sb(ctx, "steps_scratch", [P, STEPS])
        before = sb(ctx, "before", [P, STEPS])
        node_tile = sb(ctx, "node_tile", [P, STEPS + 1])
        edge_tile = sb(ctx, "edge_tile", [P, STEPS])
        part_c = sb(ctx, "part_c", [P, ICN])
        sel = sb(ctx, "sel", [IC, 2, STEPS])
        src_f = sb(ctx, "src_f", [P, STEPS])
        valid = sb(ctx, "valid", [P, STEPS])
        key = sb(ctx, "key", [P, STEPS])
        key_t = sb(ctx, "key_t", [P, ICN, P])
        guard = sb(ctx, "guard", [1, 2 * P])
        pb = [ps(ctx, f"steps_ps{b}", [P, 512]) for b in range(8)]

        with nc.Block() as block:
            @block.sync
            def _(sp):
                for n, a in enumerate((src, dst, rel)):
                    sp.dma_start(cols_i[:, n], a.rearrange("(c i p) -> i c p", i=IC, p=P)).then_inc(loaded, 16)
                sp.dma_start(cols[:, 3], norm.rearrange("(c i p) -> i c p", i=IC, p=P)).then_inc(loaded, 16)
                with nc.allow_non_contiguous_dma("one dst of each edge tile"):
                    sp.dma_start(last_i[:], dst.rearrange("(a i p) -> a i p", a=1, p=P)[:, :, P - 1]).then_inc(loaded, 16)
                sp.wait_ge(dve_did, 30)
                kd = key_d[P:P + STEPS * P].rearrange("(s p) -> s p", p=P)
                for c in range(ICN):
                    n = min(P, STEPS - c * P)
                    sp.dma_start(kd[c * P:c * P + n, :], key_t[0:n, c, :]).then_inc(key_out, 16)
                gd = key_d[:].rearrange("(a n) -> a n", a=1)
                sp.dma_start(gd[:, 0:P], guard[:, 0:P]).then_inc(key_out, 16)
                sp.dma_start(gd[:, P + STEPS * P:], guard[:, P:]).then_inc(key_out, 16)
                sp.wait_ge(key_out, 16 * (ICN + 2))

            @block.gpsimd
            def _(pool):
                nc.gpsimd.iota(iota_n[:], [[1, P]], base=0, channel_multiplier=0,
                               allow_small_or_imprecise_dtypes=True).then_inc(consts, 1)
                nc.gpsimd.iota(step_no[:], [[1, STEPS]], base=0, channel_multiplier=0,
                               allow_small_or_imprecise_dtypes=True).then_inc(consts, 1)
                nc.gpsimd.iota(part[:], [[1, 1]], base=0, channel_multiplier=1,
                               allow_small_or_imprecise_dtypes=True).then_inc(consts, 1)
                nc.gpsimd.iota(bound[:], [[1, 1]], base=P, channel_multiplier=P,
                               allow_small_or_imprecise_dtypes=True).then_inc(consts, 1)
                nc.gpsimd.iota(part_c[:], [[IC, ICN]], base=0, channel_multiplier=1,
                               allow_small_or_imprecise_dtypes=True).then_inc(consts, 1)
                nc.gpsimd.memset(ones[:], 1.0).then_inc(consts, 1)
                nc.gpsimd.memset(neg_half[:], -0.5).then_inc(consts, 1)
                nc.gpsimd.memset(guard[:], -2.0).then_inc(consts, 1)

            @block.vector
            def _(dve):
                done = [0]

                def did(ins):
                    done[0] += 1
                    ins.then_inc(dve_did, 1)
                    dve.wait_ge(dve_did, done[0])
                    return done[0]

                dve.wait_ge(consts, 8)
                nc.vector.memset(dloc[:, STEPS:], -1.0)
                did(nc.vector.tensor_scalar(ident[:], iota_n[:], part[:], None, ALU.is_equal))
                did(nc.vector.tensor_copy(ident_b[:], ident[:]))
                dve.wait_ge(loaded, 80)
                did(nc.vector.tensor_copy(last_f[:], last_i[:]))
                did(nc.vector.tensor_copy(cols[:, 0:3], cols_i[:]))
                n = EDGE_TILES_PAD // 2
                dve.wait_ge(pe_did, 2)
                did(nc.vector.tensor_scalar(scratch[:, 0:n], pb[0][:, 0:n], bound[:], 0.0, ALU.is_lt, ALU.add,
                                            accum_out=full[:]))
                did(nc.vector.tensor_scalar(scratch[:, 0:n], pb[1][:, 0:n], bound[:], full[:], ALU.is_lt, ALU.add,
                                            accum_out=pos[:]))
                did(nc.vector.tensor_tensor(pos[:], pos[:], part[:], ALU.add))
                did(nc.vector.tensor_scalar(before[:], step_no[:], pos[:], None, ALU.is_gt))
                dve.wait_ge(pe_did, 4)
                did(nc.vector.tensor_copy(node_tile[:, 0:SH], pb[2][:, 0:SH]))
                did(nc.vector.tensor_copy(node_tile[:, SH:STEPS], pb[3][:, 0:SH]))
                did(nc.vector.tensor_copy(node_tile[:, STEPS:], node_tile[:, STEPS - 1:STEPS]))
                did(nc.vector.tensor_tensor(edge_tile[:], step_no[:], node_tile[:, 0:STEPS], ALU.subtract))
                for c in range(ICN):
                    if c >= 2:
                        dve.wait_ge(sel_free, c - 1)
                    did(nc.vector.tensor_scalar(sel[:, c % 2], edge_tile[0:IC, :], part_c[0:IC, c:c + 1], None,
                                                ALU.is_equal))
                dve.wait_ge(pe_did, 5)
                for h in range(2):
                    a, b = h * SH, (h + 1) * SH
                    nc.vector.tensor_copy(src_f[:, a:b], pb[h][:, 0:SH])
                    nc.vector.tensor_copy(src_i[:, a:b], pb[h][:, 0:SH])
                    nc.vector.scalar_tensor_tensor(out=dloc[:, a:b], in0=node_tile[:, a:b], scalar=-float(P),
                                                   in1=pb[2 + h][:, 0:SH], op0=ALU.mult, op1=ALU.add)
                    nc.vector.tensor_copy(scratch[:, a:b], pb[4 + h][:, 0:SH])
                    did(nc.vector.tensor_copy(norm_s[:, a:b], pb[6 + h][:, 0:SH]))
                did(nc.vector.scalar_tensor_tensor(out=msg_i[:], in0=src_f[:], scalar=float(RELS), in1=scratch[:],
                                                   op0=ALU.mult, op1=ALU.add))
                nc.vector.tensor_copy(tile_i[:], node_tile[:, 0:STEPS])
                did(nc.vector.tensor_tensor(before[:], node_tile[:, 1:], node_tile[:, 0:STEPS], ALU.is_equal))
                nc.vector.memset(keep[:, 0:1], 0.0)
                nc.vector.tensor_copy(keep[:, 1:], before[:, 0:STEPS - 1])
                did(nc.vector.scalar_tensor_tensor(out=store_i[:], in0=before[:], scalar=float(NOT_LAST),
                                                   in1=node_tile[:, 0:STEPS], op0=ALU.mult, op1=ALU.add))
                did(nc.vector.tensor_scalar(valid[:], dloc[:, 0:STEPS], 0.0, None, ALU.is_ge))
                did(nc.vector.scalar_tensor_tensor(out=valid[:], in0=dloc[:, 0:STEPS], scalar=float(P), in1=valid[:],
                                                   op0=ALU.is_lt, op1=ALU.mult))
                did(nc.vector.scalar_tensor_tensor(out=key[:], in0=node_tile[:, 0:STEPS], scalar=float(P), in1=dloc[:, 0:STEPS],
                                                   op0=ALU.mult, op1=ALU.add))
                did(nc.vector.scalar_tensor_tensor(out=key[:], in0=key[:], scalar=1.0, in1=valid[:],
                                                   op0=ALU.add, op1=ALU.mult))
                did(nc.vector.tensor_scalar(key[:], key[:], -1.0, None, ALU.add))
                dve.wait_ge(pe_did, 6)
                for c in range(ICN):
                    n = min(P, STEPS - c * P)
                    last = nc.vector.tensor_copy(key_t[0:n, c, :], pb[c // 4][0:n, (c % 4) * P:(c % 4 + 1) * P])
                did(last)

            @block.tensor
            def _(pe):
                n = EDGE_TILES_PAD // 2
                pe.wait_ge(dve_did, 3)
                for h in range(2):
                    nc.tensor.matmul(pb[h][:, 0:n], ones[0:1, :], last_f[:, h * n:(h + 1) * n],
                                     start=True, stop=True).then_inc(pe_did, 1)
                pe.wait_ge(dve_did, 8)
                for h in range(2):
                    nc.tensor.matmul(pb[2 + h][:, 0:SH], ones[0:NODE_TILES, :], before[0:NODE_TILES, h * SH:(h + 1) * SH],
                                     start=True, stop=True).then_inc(pe_did, 1)
                for c in range(ICN):
                    pe.wait_ge(dve_did, 13 + c)
                    for n in range(4):
                        for h in range(2):
                            mm = nc.tensor.matmul(pb[2 * n + h][:, 0:SH], cols[:, n, c, :],
                                                  sel[:, c % 2, h * SH:(h + 1) * SH],
                                                  start=(c == 0), stop=(c == ICN - 1))
                    mm.then_inc(sel_free, 1)
                pe.nop()
                pe.wait_ge(sel_free, ICN)
                pe.sem_inc(pe_did, 1)
                pe.wait_ge(dve_did, 29)
                for c in range(ICN):
                    n = min(P, STEPS - c * P)
                    tr = nc.tensor.transpose(pb[c // 4][0:n, (c % 4) * P:(c % 4 + 1) * P], key[:, c * P:c * P + n], ident[:])
                tr.then_inc(pe_did, 1)


def node_inputs(nc, sb, ps, sem, x, wqkv, bqkv, g_attn, b_attn, ident, neg_half, h0_d, q_d, v_d, k_all):
    w_ld = sem("in_w")
    x_ld = [sem(f"in_x{i}") for i in range(2)]
    x_free = sem("in_x_free")
    stat = sem("in_stat")
    rstd_ok = sem("in_rstd")
    h0_ok = sem("in_h0")
    hn_ok = sem("in_hn")
    tr_ok = sem("in_tr")
    ht_ok = sem("in_ht")
    mm_ok = sem("in_mm")
    ev_ok = sem("in_ev")
    st_h0 = sem("in_st_h0")
    st_qv = sem("in_st_qv")
    own = sem("in_own")
    with ExitStack() as ctx:
        wq = sb(ctx, "wq", [P, KC, 3 * FEAT])
        bias = sb(ctx, "qkv_bias", [P, 3 * FEAT])
        gb = sb(ctx, "attn_gb", [P, 2, KC])
        xg = sb(ctx, "xg", [P, 2, GROUP, FEAT])
        h0 = sb(ctx, "h0", [P, GROUP, FEAT])
        hn = sb(ctx, "hn", [P, GROUP, FEAT])
        hT = sb(ctx, "hT", [P, 2, KC, P])
        qv = sb(ctx, "qv", [P, 2, GROUP, FEAT])
        st6 = sb(ctx, "st6", [P, GROUP, 6])
        mv = sb(ctx, "mv", [P, 2, GROUP, 2])
        veps = sb(ctx, "veps", [P, 2, GROUP])
        rstd = sb(ctx, "rstd", [P, 2, GROUP])
        shift = sb(ctx, "shift", [P, GROUP])
        tr_ps = [ps(ctx, f"in_tr{i}", [P, KC, P]) for i in range(2)]
        qk_ps = [ps(ctx, f"in_qk{i}", [P, 512]) for i in range(2)]
        v_ps = [ps(ctx, f"in_v{i}", [P, FEAT]) for i in range(2)]
        rows = lambda d: d.rearrange("(g t p) f -> g p t f", t=GROUP, p=P)

        with nc.Block() as block:
            @block.sync
            def _(sp):
                def store(g):
                    sp.wait_ge(h0_ok, g + 1)
                    sp.dma_start(rows(h0_d)[g], h0[:]).then_inc(st_h0, 16)
                    sp.wait_ge(ev_ok, GROUP * (g + 1))
                    sp.dma_start(rows(q_d)[g], qv[:, 0]).then_inc(st_qv, 16)
                    sp.dma_start(rows(v_d)[g], qv[:, 1]).then_inc(st_qv, 16)

                sp.dma_start(wq[:], wqkv.rearrange("(k p) n -> p k n", p=P)).then_inc(w_ld, 16)
                sp.dma_start(bias[:], bqkv.rearrange("(a n) -> a n", a=1).to_broadcast([P, 3 * FEAT])).then_inc(w_ld, 16)
                with nc.allow_non_contiguous_dma("two columns of LN parameters"):
                    sp.dma_start(gb[:, 0], g_attn.rearrange("(k p) -> p k", p=P)).then_inc(w_ld, 16)
                    sp.dma_start(gb[:, 1], b_attn.rearrange("(k p) -> p k", p=P)).then_inc(w_ld, 16)
                for g in range(GROUPS):
                    if g >= 2:
                        sp.wait_ge(h0_ok, g - 1)
                    sp.dma_start(xg[:, g % 2], rows(x)[g]).then_inc(x_ld[g % 2], 16)
                    if g >= 1:
                        store(g - 1)
                store(GROUPS - 1)
                sp.wait_ge(st_h0, 16 * GROUPS)
                sp.wait_ge(st_qv, 32 * GROUPS)

            @block.vector
            def _(dve):
                n = [0]

                def own_wait(ins):
                    n[0] += 1
                    ins.then_inc(own, 1)
                    dve.wait_ge(own, n[0])

                def stats(g, which, data):
                    for t in range(GROUP):
                        last = nc.vector.bn_stats(st6[:, t, :], data[:, t, :])
                    own_wait(last)
                    for t in range(GROUP):
                        last = nc.vector.bn_aggr(mv[:, which, t, :], st6[:, t, :])
                    own_wait(last)
                    nc.vector.tensor_scalar(veps[:, which, :], mv[:, which, :, 1], EPS, None, ALU.add).then_inc(stat, 1)

                dve.wait_ge(w_ld, 64)
                own_wait(nc.vector.memset(k_all[:, NODE_TILES * FEAT:], 0.0))
                for g in range(GROUPS):
                    dve.wait_ge(x_ld[g % 2], 16 * (g // 2 + 1))
                    stats(g, 0, xg[:, g % 2])
                    dve.wait_ge(rstd_ok, 2 * g + 1)
                    if g >= 1:
                        dve.wait_ge(h0_ok, g)
                    nc.vector.scalar_tensor_tensor(out=shift[:], in0=mv[:, 0, :, 0], scalar=-1.0, in1=rstd[:, 0, :],
                                                   op0=ALU.mult, op1=ALU.mult).then_inc(stat, 1)
                    dve.wait_ge(h0_ok, g + 1)
                    stats(g, 1, h0)
                    dve.wait_ge(rstd_ok, 2 * g + 2)
                    if g >= 1:
                        dve.wait_ge(tr_ok, GROUP * g)
                    for t in range(GROUP):
                        nc.vector.tensor_scalar(hn[:, t, :], h0[:, t, :], mv[:, 1, t, 0:1], rstd[:, 1, t:t + 1],
                                                ALU.subtract, ALU.mult).then_inc(hn_ok, 1)
                    if g >= 1:
                        dve.wait_ge(st_qv, 32 * g)
                    for t in range(GROUP):
                        n_t = GROUP * g + t
                        dve.wait_ge(mm_ok, n_t + 1)
                        nc.vector.tensor_tensor(qv[:, 0, t, :], qk_ps[n_t % 2][:, 0:FEAT], bias[:, 0:FEAT], ALU.add)
                        nc.vector.tensor_tensor(k_all[:, n_t * FEAT:(n_t + 1) * FEAT], qk_ps[n_t % 2][:, FEAT:], bias[:, FEAT:2 * FEAT], ALU.add)
                        nc.vector.tensor_tensor(qv[:, 1, t, :], v_ps[n_t % 2][:], bias[:, 2 * FEAT:], ALU.add).then_inc(ev_ok, 1)

            @block.gpsimd
            def _(pool):
                for g in range(GROUPS):
                    for which in range(2):
                        pool.wait_ge(stat, 3 * g + 1 + 2 * which)
                        nc.gpsimd.tensor_tensor(rstd[:, which, :], veps[:, which, :], neg_half[:], ALU.pow).then_inc(rstd_ok, 1)

            @block.scalar
            def _(act):
                act.wait_ge(w_ld, 64)
                for g in range(GROUPS):
                    act.wait_ge(stat, 3 * g + 2)
                    if g >= 1:
                        act.wait_ge(st_h0, 16 * g)
                        act.wait_ge(hn_ok, GROUP * g)
                    for t in range(GROUP):
                        last = nc.scalar.activation(h0[:, t, :], xg[:, g % 2, t, :], ACT.Relu,
                                                    scale=rstd[:, 0, t:t + 1], bias=shift[:, t:t + 1])
                    last.then_inc(h0_ok, 1)
                    for t in range(GROUP):
                        n_t = GROUP * g + t
                        act.wait_ge(tr_ok, n_t + 1)
                        if n_t >= 2:
                            act.wait_ge(mm_ok, n_t - 1)
                        for k in range(KC):
                            last = nc.scalar.activation(hT[:, n_t % 2, k, :], tr_ps[n_t % 2][:, k, :], ACT.Identity,
                                                        scale=gb[:, 0, k:k + 1], bias=gb[:, 1, k:k + 1])
                        last.then_inc(ht_ok, 1)

            @block.tensor
            def _(pe):
                def products(m):
                    pe.wait_ge(ht_ok, m + 1)
                    if m >= 2:
                        pe.wait_ge(ev_ok, m - 1)
                    for k in range(KC):
                        nc.tensor.matmul(qk_ps[m % 2][:], hT[:, m % 2, k, :], wq[:, k, 0:512], start=(k == 0), stop=(k == KC - 1))
                    for k in range(KC):
                        last = nc.tensor.matmul(v_ps[m % 2][:], hT[:, m % 2, k, :], wq[:, k, 512:], start=(k == 0), stop=(k == KC - 1))
                    last.then_inc(mm_ok, 1)

                pe.wait_ge(w_ld, 64)
                for g in range(GROUPS):
                    for t in range(GROUP):
                        n_t = GROUP * g + t
                        pe.wait_ge(hn_ok, n_t + 1)
                        if n_t >= 2:
                            pe.wait_ge(ht_ok, n_t - 1)
                        for k in range(KC):
                            last = nc.tensor.transpose(tr_ps[n_t % 2][:, k, :], hn[:, t, k * P:(k + 1) * P], ident[:])
                        last.then_inc(tr_ok, 1)
                        if t >= 1:
                            products(n_t - 1)
                    products(GROUP * g + GROUP - 1)


def load_indices(sp, idx_now, idx_all, columns, half, idx_ld):
    sp.dma_start(idx_now[:, half, :], idx_all[:, columns]).then_inc(idx_ld[half], 16)


def gather_rows(nc, pool, t0, b, rows, table, idx_now, got, used, idx_ld, turn, rounds_done):
    if b % HALF == 0:
        pool.wait_ge(idx_ld[b // HALF], rounds_done)
        pool.sem_inc(turn, 1)
    pool.wait_ge(used, t0 + (b + 1))
    pool.sem_inc(turn, 1)
    nc.gpsimd.indirect_dma_start(rows[:, b, :], None, table,
                                 bass.IndirectOffsetOnAxis(ap=idx_now[:, b // HALF, b % HALF:b % HALF + 1], axis=0)
                                 ).then_inc(got[b], 16)


def edge_scores(nc, sb, ps, sem, q_d, scores_d, k_all, iota_n, ident, ident_b, dloc, src_i, tile_i, idx_now):
    idx_ld = [sem(f"sc_idx{h}") for h in range(2)]
    got = [sem(f"sc_got{b}") for b in range(UNROLL)]
    used = sem("sc_used")
    turn = sem("sc_turn")
    hot_ok, turned, hott_ok, expanded, prod_ok = (sem(f"sc_{n}") for n in ("hot", "turned", "hott", "exp", "prod"))
    t_ok, c_ok, st = sem("sc_t"), sem("sc_c"), [sem(f"sc_st{i}") for i in range(4)]
    with ExitStack() as ctx:
        rows = sb(ctx, "q_rows", [P, UNROLL, FEAT])
        scores = sb(ctx, "scores", [P, STEPS * HEADS])
        hot = sb(ctx, "hot_b", [P, 2, P], BF16)
        hot_t = sb(ctx, "hot_t", [P, 2, P])
        prod = sb(ctx, "prod", [P, 2, HEADS, HEAD_DIM])
        turned_sb = sb(ctx, "scores_t", [P, 4, P])
        hot_ps = [ps(ctx, f"hot_ps{i}", [P, P], BF16) for i in range(2)]
        k_ps = [ps(ctx, f"k_ps{i}", [P, FEAT]) for i in range(4)]
        out_ps = [ps(ctx, f"sco_ps{i}", [P, P]) for i in range(2)]

        with nc.Block() as block:
            @block.sync
            def _(sp):
                for h in range(2):
                    load_indices(sp, idx_now, src_i, slice(h * HALF, (h + 1) * HALF), h, idx_ld)
                with sp.Fori(0, ROUNDS - 1) as round_no:
                    t0 = sp.snap(round_no * UNROLL)
                    for h in range(2):
                        sp.wait_ge(used, t0 + (UNROLL + HALF * (h + 1)))
                        load_indices(sp, idx_now, src_i, bass.ds(t0 + (UNROLL + HALF * h), HALF), h, idx_ld)
                for n in range(BLOCKS):
                    sp.wait_ge(c_ok, n + 1)
                    sp.dma_start(scores_d[n * P:(n + 1) * P, :], turned_sb[:, n % 4, :]).then_inc(st[n % 4], 16)
                for n in range(4):
                    sp.wait_ge(st[n], 16 * (BLOCKS // 4))

            @block.gpsimd
            def _(pool):
                with pool.Fori(0, ROUNDS) as round_no:
                    t0 = pool.snap(round_no * UNROLL)
                    for b in range(UNROLL):
                        gather_rows(nc, pool, t0, b, rows, q_d, idx_now, got, used, idx_ld, turn, t0 + 16)

            @block.scalar
            def _(act):
                act.sem_inc(hott_ok, 2)
                with act.Fori(0, ROUNDS) as round_no:
                    t0 = act.snap(round_no * UNROLL)
                    for b in range(UNROLL):
                        act.wait_ge(turned, t0 + (b + 1))
                        act.wait_ge(expanded, t0 + (b + 1))
                        nc.scalar.copy(hot_t[:, b % 2, :], hot_ps[b % 2][:]).then_inc(hott_ok, 1)
                for n in range(BLOCKS):
                    act.wait_ge(t_ok, n + 1)
                    if n >= 4:
                        act.wait_ge(st[n % 4], 16 * (n // 4))
                    nc.scalar.copy(turned_sb[:, n % 4, :], out_ps[n % 2][:]).then_inc(c_ok, 1)

            @block.tensor
            def _(pe):
                pe.sem_inc(expanded, 2)
                with pe.Fori(0, ROUNDS) as round_no:
                    t0 = pe.snap(round_no * UNROLL)
                    tiles = [pe.value_load(tile_i[0:1, bass.ds(t0 + b, 1)], min_val=0, max_val=NODE_TILES)
                             for b in range(UNROLL)]

                    def turn_hot(b):
                        pe.wait_ge(hot_ok, t0 + (b + 1))
                        pe.wait_ge(hott_ok, t0 + (b + 1))
                        nc.tensor.transpose(hot_ps[b % 2][:], hot[:, b % 2, :], ident_b[:]).then_inc(turned, 1)

                    def expand(b):
                        pe.wait_ge(hott_ok, t0 + (b + 3))
                        pe.wait_ge(prod_ok, t0 + (b + 1))
                        nc.tensor.matmul(k_ps[b % 4][:], hot_t[:, b % 2, :], k_all[:, bass.ds(tiles[b] * FEAT, FEAT)],
                                         start=True, stop=True).then_inc(expanded, 1)

                    turn_hot(0)
                    for b in range(1, UNROLL):
                        turn_hot(b)
                        expand(b - 1)
                    expand(UNROLL - 1)
                for n in range(BLOCKS):
                    if n == 0:
                        pe.wait_ge(used, STEPS + UNROLL)
                    if n >= 2:
                        pe.wait_ge(c_ok, n - 1)
                    nc.tensor.transpose(out_ps[n % 2][:], scores[:, n * P:(n + 1) * P],
                                        ident[:]).then_inc(t_ok, 1)

            @block.vector
            def _(dve):
                dve.sem_inc(prod_ok, 4)
                dve.sem_inc(used, UNROLL)

                def make_hot(column, slot):
                    nc.vector.tensor_scalar(hot[:, slot, :], iota_n[:], column, None, ALU.is_equal).then_inc(hot_ok, 1)

                make_hot(dloc[:, 0:1], 0)
                make_hot(dloc[:, 1:2], 1)
                with dve.Fori(0, ROUNDS) as round_no:
                    t0 = dve.snap(round_no * UNROLL)
                    for b in range(UNROLL):
                        dve.wait_ge(got[b], t0 + 16)
                        dve.wait_ge(expanded, t0 + (b + 3))
                        nc.vector.tensor_tensor(prod[:, b % 2].rearrange("p h d -> p (h d)"), rows[:, b, :], k_ps[b % 4][:],
                                                ALU.mult).then_inc(prod_ok, 1)
                        dve.wait_ge(turned, t0 + (b + 1))
                        make_hot(dloc[:, bass.ds(t0 + (b + 2), 1)], b % 2)
                        dve.wait_ge(prod_ok, t0 + (b + 5))
                        nc.vector.tensor_reduce(scores[:, bass.ds((t0 + b) * HEADS, HEADS)], prod[:, b % 2], AX_X, ALU.add).then_inc(used, 1)


def softmax_numerators(nc, sb, ps, sem, scores_d, probs_d, key_d, ident, ones):
    ld, dve_did, pe_did, exp_ok, st = (sem(f"sm_{n}") for n in ("ld", "dve", "pe", "exp", "st"))
    with ExitStack() as ctx:
        s = sb(ctx, "sm_s", [P, CHUNK])
        key = sb(ctx, "sm_key", [P, CHUNK + 2])
        brk = sb(ctx, "sm_brk", [P, CHUNK + 1], BF16)
        fwd = sb(ctx, "sm_fwd", [P, CHUNK])
        bwd = sb(ctx, "sm_bwd", [P, CHUNK])
        ends = sb(ctx, "sm_ends", [P, 4])
        rows_sb = sb(ctx, "sm_rows", [1, 4, P])
        carry = sb(ctx, "sm_carry", [1, 2, P])
        carry_c = sb(ctx, "sm_carry_c", [P, 2])
        row_ps = ps(ctx, "sm_row_ps", [1, 4 * P])
        col_ps = ps(ctx, "sm_col_ps", [P, 2])

        def by_head(d, h):
            return d.rearrange("(c s h) p -> h c s p", h=HEADS, c=CHUNKS)[h]

        with nc.Block() as block:
            @block.sync
            def _(sp):
                with nc.allow_non_contiguous_dma("runs of one step and head"):
                    for h in range(HEADS):
                        r = slice(h * CHUNKS, (h + 1) * CHUNKS)
                        sp.dma_start(key[r, :], bass.AP(key_d.tensor, P - 1, [[CHUNK, CHUNKS], [1, CHUNK + 2]])).then_inc(ld, 16)
                        sp.dma_start(s[r, :].rearrange("c (s p) -> c s p", p=P), by_head(scores_d, h)).then_inc(ld, 16)
                    sp.wait_ge(exp_ok, 1)
                    for h in range(HEADS):
                        r = slice(h * CHUNKS, (h + 1) * CHUNKS)
                        sp.dma_start(by_head(probs_d, h), s[r, :].rearrange("c (s p) -> c s p", p=P)).then_inc(st, 16)
                    sp.wait_ge(st, 16 * HEADS)

            @block.vector
            def _(dve):
                done = [0]

                def did(ins):
                    done[0] += 1
                    ins.then_inc(dve_did, 1)
                    dve.wait_ge(dve_did, done[0])

                dve.wait_ge(ld, 32 * HEADS)
                did(nc.vector.tensor_tensor(brk[:], key[:, 1:], key[:, 0:CHUNK + 1], ALU.not_equal))
                did(nc.vector.tensor_scalar(brk[:], brk[:], -BIG, None, ALU.mult))
                did(nc.vector.tensor_tensor_scan(fwd[:], brk[:, 0:CHUNK], s[:], -BIG, ALU.add, ALU.max))
                did(nc.vector.tensor_tensor_scan(bwd[:, ::-1], brk[:, CHUNK:0:-1], s[:, ::-1], -BIG, ALU.add, ALU.max))
                nc.vector.tensor_copy(ends[:, 0:1], fwd[:, CHUNK - 1:])
                nc.vector.tensor_copy(ends[:, 2:3], bwd[:, 0:1])
                nc.vector.tensor_tensor(ends[:, 1:2], key[:, 0:1], key[:, CHUNK:CHUNK + 1], ALU.not_equal)
                did(nc.vector.tensor_tensor(ends[:, 3:4], key[:, 1:2], key[:, CHUNK + 1:], ALU.not_equal))
                dve.wait_ge(pe_did, 1)
                did(nc.vector.tensor_copy(rows_sb[:].rearrange("a n p -> a (n p)"), row_ps[:]))
                for n in (1, 3):
                    last = nc.vector.tensor_scalar(rows_sb[:, n, :], rows_sb[:, n, :], -BIG, None, ALU.mult)
                did(last)
                nc.vector.memset(carry[:], -BIG)
                did(nc.vector.tensor_copy(ends[:, 0:1], ends[:, 0:1]))
                did(nc.vector.tensor_tensor_scan(carry[:, 0, 1:], rows_sb[:, 1, 0:P - 1], rows_sb[:, 0, 0:P - 1], -BIG,
                                                 ALU.add, ALU.max))
                did(nc.vector.tensor_tensor_scan(carry[:, 1, P - 2::-1], rows_sb[:, 3, P - 1:0:-1], rows_sb[:, 2, P - 1:0:-1],
                                                 -BIG, ALU.add, ALU.max))
                dve.wait_ge(pe_did, 2)
                did(nc.vector.tensor_copy(carry_c[:], col_ps[:]))
                did(nc.vector.tensor_tensor_scan(fwd[:], brk[:, 0:CHUNK], s[:], carry_c[:, 0:1], ALU.add, ALU.max))
                did(nc.vector.tensor_tensor_scan(bwd[:, ::-1], brk[:, CHUNK:0:-1], s[:, ::-1], carry_c[:, 1:2], ALU.add, ALU.max))
                did(nc.vector.tensor_tensor(fwd[:], fwd[:], bwd[:], ALU.max))
                did(nc.vector.tensor_tensor(s[:], s[:], fwd[:], ALU.subtract))
                assert done[0] == SM_DVE

            @block.tensor
            def _(pe):
                pe.wait_ge(dve_did, 5)
                for n in range(4):
                    last = nc.tensor.transpose(row_ps[:, n * P:(n + 1) * P], ends[:, n:n + 1], ident[:])
                last.then_inc(pe_did, 1)
                pe.wait_ge(dve_did, 10)
                for n in range(2):
                    last = nc.tensor.matmul(col_ps[:, n:n + 1], carry[:, n, :], ones[0:1, 0:1], start=True, stop=True)
                last.then_inc(pe_did, 1)

            @block.scalar
            def _(act):
                act.wait_ge(dve_did, SM_DVE)
                nc.scalar.activation(s[:], s[:], ACT.Exp, scale=ATT_SCALE).then_inc(exp_ok, 1)


SM_DVE = 15


def edge_sum(nc, sb, ps, sem, name, table, sums_d, width, probs_d, iota_n, ident, dloc, norm_s, keep,
             row_i, store_i, idx_now):
    idx_ld = [sem(f"{name}_idx{h}") for h in range(2)]
    got = [sem(f"{name}_got{b}") for b in range(UNROLL)]
    att = probs_d is not None
    summed = sem(f"{name}_sum")
    used = sem(f"{name}_used") if att else summed
    credit = 4 if att else UNROLL
    turn = sem(f"{name}_turn")
    hot_ok, acc_ok, acc_free, acc_st = (sem(f"{name}_{n}") for n in ("hot", "acc", "accf", "accs"))
    den_ok, p_tr, p_ok = (sem(f"{name}_{n}") for n in ("den", "ptr", "pok"))
    p_ld = [sem(f"{name}_pld{i}") for i in range(4)]
    with ExitStack() as ctx:
        rows = sb(ctx, f"{name}_rows", [P, UNROLL, FEAT])
        hot = sb(ctx, f"{name}_hot", [P, 4, P])
        acc = sb(ctx, f"{name}_acc", [P, ACC_RING, width])
        if att:
            probs = sb(ctx, "probs", [P, STEPS * HEADS])
            probs_t = sb(ctx, "probs_t", [P, 4, P])
            val = sb(ctx, "val", [P, 4, AGGW])
        sum_ps = [ps(ctx, f"{name}_ps{i}", [P, width]) for i in range(4)]
        turn_ps = [ps(ctx, f"{name}_tps{i}", [P, P]) for i in range(2)]

        with nc.Block() as block:
            @block.sync
            def _(sp):
                for h in range(2):
                    load_indices(sp, idx_now, row_i, slice(h * HALF, (h + 1) * HALF), h, idx_ld)
                if att:
                    for n in range(BLOCKS):
                        if n >= 4:
                            sp.wait_ge(p_tr, n - 3)
                        sp.dma_start(probs_t[:, n % 4, :], probs_d[n * P:(n + 1) * P, :]).then_inc(p_ld[n % 4], 16)

                sp.sem_inc(acc_free, ACC_RING)

                def store_ended(t0, b):
                    code = sp.value_load(store_i[0:1, bass.ds(t0 + b, 1)], min_val=0, max_val=NOT_LAST + NODE_TILES)
                    sp.wait_ge(acc_ok, t0 + (b + 2))
                    sp.sem_inc(turn, 1)
                    with sp.If(code < NODE_TILES):
                        tile = nc.s_assert_within(
                            code, 0, NODE_TILES - 1,
                            skip_runtime_bounds_check_because="this branch is taken only for codes below NODE_TILES")
                        sp.dma_start(sums_d[bass.ds(tile * P, P), :], acc[:, b % ACC_RING, :]).then_inc(acc_st, 16)
                        sp.wait_ge(acc_st, tile * 16 + 16)
                        sp.sem_inc(turn, 1)
                    sp.sem_inc(acc_free, 1)

                with sp.Fori(0, ROUNDS - 1) as round_no:
                    t0 = sp.snap(round_no * UNROLL)
                    for b in range(UNROLL):
                        store_ended(t0, b)
                        if b % HALF == HALF - 1:
                            load_indices(sp, idx_now, row_i, bass.ds(t0 + (UNROLL + b + 1 - HALF), HALF), b // HALF, idx_ld)
                for b in range(UNROLL):
                    store_ended(STEPS - UNROLL, b)
                sp.wait_ge(acc_st, 16 * NODE_TILES)

            @block.gpsimd
            def _(pool):
                with pool.Fori(0, ROUNDS) as round_no:
                    t0 = pool.snap(round_no * UNROLL)
                    for b in range(UNROLL):
                        gather_rows(nc, pool, t0, b, rows, table, idx_now, got, used, idx_ld, turn, t0 + 16)

            @block.scalar
            def _(act):
                if att:
                    for n in range(BLOCKS):
                        act.wait_ge(p_tr, n + 1)
                        nc.scalar.copy(probs[:, n * P:(n + 1) * P],
                                       turn_ps[n % 2][:]).then_inc(p_ok, 1)
                    with act.Fori(0, ROUNDS) as round_no:
                        t0 = act.snap(round_no * UNROLL)
                        for b in range(UNROLL):
                            act.wait_ge(summed, t0 + (b + 1))
                            nc.scalar.copy(val[:, b % 4, FEAT:], probs[:, bass.ds((t0 + b) * HEADS, HEADS)]
                                           ).then_inc(den_ok, 1)

            @block.tensor
            def _(pe):
                if att:
                    for n in range(BLOCKS):
                        pe.wait_ge(p_ld[n % 4], 16 * (n // 4 + 1))
                        if n >= 2:
                            pe.wait_ge(p_ok, n - 1)
                        nc.tensor.transpose(turn_ps[n % 2][:], probs_t[:, n % 4, :], ident[:]).then_inc(p_tr, 1)
                pe.sem_inc(summed, credit)
                with pe.Fori(0, ROUNDS) as round_no:
                    t0 = pe.snap(round_no * UNROLL)
                    for b in range(UNROLL):
                        pe.wait_ge(hot_ok, t0 + (b + 1))
                        if b >= 4:
                            pe.wait_ge(acc_ok, t0 + (b - 2))
                        if att:
                            pe.wait_ge(used, t0 + (b + 1 + UNROLL))
                            pe.wait_ge(den_ok, t0 + (b + 1))
                            moving = val[:, b % 4, :]
                        else:
                            pe.wait_ge(got[b], t0 + 16)
                            moving = rows[:, b, :]
                        nc.tensor.matmul(sum_ps[b % 4][:], hot[:, b % 4, :], moving, start=True, stop=True).then_inc(summed, 1)

            @block.vector
            def _(dve):
                if att:
                    dve.sem_inc(used, UNROLL)
                nc.vector.memset(acc[:], 0.0).then_inc(acc_ok, 1)
                if att:
                    dve.wait_ge(p_ok, BLOCKS)

                def feed(t0, b):
                    column = dloc[:, bass.ds(t0 + b, 1)]
                    dve.wait_ge(summed, t0 + (b - 3 + credit))
                    if att:
                        nc.vector.tensor_scalar(hot[:, b % 4, :], iota_n[:], column, None, ALU.is_equal).then_inc(hot_ok, 1)
                        dve.wait_ge(got[b], t0 + 16)
                        weights = probs[:, bass.ds((t0 + b) * HEADS, HEADS)]
                        nc.vector.tensor_tensor(val[:, b % 4, 0:FEAT].rearrange("p (h d) -> p h d", h=HEADS),
                                                rows[:, b, :].rearrange("p (h d) -> p h d", h=HEADS),
                                                weights.rearrange("p (h o) -> p h o", o=1).to_broadcast([P, HEADS, HEAD_DIM]),
                                                ALU.mult).then_inc(used, 1)
                    else:
                        nc.vector.tensor_scalar(hot[:, b % 4, :], iota_n[:], column, norm_s[:, bass.ds(t0 + b, 1)],
                                                ALU.is_equal, ALU.mult).then_inc(hot_ok, 1)

                def accumulate(t0, b):
                    dve.wait_ge(summed, t0 + (b + 1 + credit))
                    dve.wait_ge(acc_free, t0 + (b + 1))
                    dve.wait_ge(acc_ok, t0 + (b + 1))
                    nc.vector.scalar_tensor_tensor(out=acc[:, b % ACC_RING, :], in0=acc[:, (b - 1) % ACC_RING, :],
                                                   scalar=keep[:, bass.ds(t0 + b, 1)], in1=sum_ps[b % 4][:],
                                                   op0=ALU.mult, op1=ALU.add).then_inc(acc_ok, 1)

                with dve.Fori(0, ROUNDS) as round_no:
                    t0 = dve.snap(round_no * UNROLL)
                    for b in range(UNROLL):
                        feed(t0, b)
                        if b >= 2:
                            accumulate(t0, b - 2)
                    accumulate(t0, UNROLL - 2)
                    accumulate(t0, UNROLL - 1)


def node_update(nc, sb, ps, sem, x, g_res, b_res, w_in, b_in, w_out, b_out, w_rel, w_gate, ident,
                neg_half, h0_d, agg_d, x1_d, msg_d):
    w_ld, in_ld = sem("up_w"), sem("up_in")
    own = sem("up_own")
    stat, rstd_ok = sem("up_stat"), sem("up_rstd")
    yn_ok, tr_ok, yt_ok = sem("up_yn"), sem("up_tr"), sem("up_yt")
    hid_mm, hid_ok, out_mm, x1_ok, x1_st = (sem(f"up_{n}") for n in ("hmm", "hid", "omm", "x1", "x1s"))
    h1_ok, h1t_ok, gate_mm, gate_ok = (sem(f"up_{n}") for n in ("h1", "h1t", "gmm", "gate"))
    msg_mm, ev_act, ev_dve = (sem(f"up_{n}") for n in ("msg", "eva", "evd"))
    msg_st = [sem(f"up_mst{i}") for i in range(2)]
    NC_ = GROUP * P
    HN = NC_ // 2
    with ExitStack() as ctx:
        win = sb(ctx, "win", [P, KC, DFF])
        wout = sb(ctx, "wout", [P, FFC, FEAT])
        wrel = sb(ctx, "wrel", [P, KC, RELS, FEAT])
        wgate = sb(ctx, "wgate", [P, KC, RELS])
        bin_c = sb(ctx, "bin_c", [P, FFC])
        bout = sb(ctx, "bout", [P, FEAT])
        gb = sb(ctx, "res_gb", [P, 2, KC])
        agg = sb(ctx, "up_agg", [P, GROUP, AGGW])
        h0 = sb(ctx, "up_h0", [P, GROUP, FEAT])
        xg = sb(ctx, "up_x", [P, GROUP, FEAT])
        den = sb(ctx, "up_den", [P, GROUP, HEADS])
        x2 = sb(ctx, "up_x2", [P, GROUP, FEAT])
        res = sb(ctx, "up_res", [P, GROUP, FEAT])
        yT = sb(ctx, "up_yT", [P, KC, NC_])
        hid = sb(ctx, "up_hid", [P, FFC, NC_])
        x1 = sb(ctx, "up_x1", [P, GROUP, FEAT])
        h1T = sb(ctx, "up_h1T", [P, KC, NC_])
        gate = sb(ctx, "up_gate", [P, GROUP, RELS])
        msg = sb(ctx, "up_msg", [P, 2, RELS * FEAT])
        st6 = sb(ctx, "up_st6", [P, GROUP, 6])
        mv = sb(ctx, "up_mv", [P, 2, GROUP, 2])
        veps = sb(ctx, "up_veps", [P, 2, GROUP])
        rstd = sb(ctx, "up_rstd_t", [P, 2, GROUP])
        tr_ps = [ps(ctx, f"up_tr{i}", [P, KC, P]) for i in range(2)]
        gate_ps = tr_ps[0][:].rearrange("p k n -> p (k n)")[:, 0:GROUP * RELS]
        mm_ps = [ps(ctx, f"up_mm{i}", [P, 512]) for i in range(6)]
        rows = lambda d: d.rearrange("(g t p) f -> g p t f", t=GROUP, p=P)

        with nc.Block() as block:
            @block.sync
            def _(sp):
                sp.dma_start(win[:], w_in.rearrange("(k p) n -> p k n", p=P)).then_inc(w_ld, 16)
                sp.dma_start(wout[:], w_out.rearrange("(k p) n -> p k n", p=P)).then_inc(w_ld, 16)
                for k in range(KC):
                    sp.dma_start(wrel[:, k], w_rel.rearrange("r (k p) n -> k p r n", p=P)[k]).then_inc(w_ld, 16)
                sp.dma_start(bout[:], b_out.rearrange("(a n) -> a n", a=1).to_broadcast([P, FEAT])).then_inc(w_ld, 16)
                with nc.allow_non_contiguous_dma("small columns of parameters"):
                    for k in range(KC):
                        sp.dma_start(wgate[:, k], w_gate.rearrange("r (k p) a -> k p (r a)", p=P)[k]).then_inc(w_ld, 16)
                    sp.dma_start(bin_c[:], b_in.rearrange("(k p) -> p k", p=P)).then_inc(w_ld, 16)
                    sp.dma_start(gb[:, 0], g_res.rearrange("(k p) -> p k", p=P)).then_inc(w_ld, 16)
                    sp.dma_start(gb[:, 1], b_res.rearrange("(k p) -> p k", p=P)).then_inc(w_ld, 16)
                for g in range(GROUPS):
                    if g >= 1:
                        sp.wait_ge(yn_ok, GROUP * g)
                    sp.dma_start(agg[:], rows(agg_d)[g]).then_inc(in_ld, 16)
                    sp.dma_start(h0[:], rows(h0_d)[g]).then_inc(in_ld, 16)
                    sp.dma_start(xg[:], rows(x)[g]).then_inc(in_ld, 16)
                    sp.wait_ge(x1_ok, GROUP * (g + 1))
                    sp.dma_start(rows(x1_d)[g], x1[:]).then_inc(x1_st, 16)
                    for t in range(GROUP):
                        n_t = GROUP * g + t
                        sp.wait_ge(ev_act, PAIRS * (n_t + 1))
                        sp.wait_ge(ev_dve, (PAIRS // 2) * (n_t + 1))
                        sp.dma_start(msg_d[n_t * P * RELS:(n_t + 1) * P * RELS, :].rearrange("(p r) f -> p (r f)", r=RELS),
                                     msg[:, n_t % 2, :]).then_inc(msg_st[n_t % 2], 16)
                sp.wait_ge(x1_st, 16 * GROUPS)
                for n in range(2):
                    sp.wait_ge(msg_st[n], 16 * ((NODE_TILES + 1 - n) // 2))

            @block.vector
            def _(dve):
                n = [0]

                def own_wait(ins):
                    n[0] += 1
                    ins.then_inc(own, 1)
                    dve.wait_ge(own, n[0])

                def stats(g, which, data):
                    for t in range(GROUP):
                        last = nc.vector.bn_stats(st6[:, t, :], data[:, t, :])
                    own_wait(last)
                    for t in range(GROUP):
                        last = nc.vector.bn_aggr(mv[:, which, t, :], st6[:, t, :])
                    own_wait(last)
                    nc.vector.tensor_scalar(veps[:, which, :], mv[:, which, :, 1], EPS, None, ALU.add).then_inc(stat, 1)

                dve.wait_ge(w_ld, 16 * 10)
                for g in range(GROUPS):
                    dve.wait_ge(in_ld, 48 * (g + 1))
                    own_wait(nc.vector.tensor_scalar(den[:], agg[:, :, FEAT:], 1e-30, None, ALU.max))
                    own_wait(nc.vector.reciprocal(den[:], den[:]))
                    for t in range(GROUP):
                        last = nc.vector.tensor_tensor(x2[:, t, :].rearrange("p (h d) -> p h d", h=HEADS),
                                                       agg[:, t, 0:FEAT].rearrange("p (h d) -> p h d", h=HEADS),
                                                       den[:, t, :].rearrange("p (h o) -> p h o", o=1).to_broadcast([P, HEADS, HEAD_DIM]),
                                                       ALU.mult)
                    own_wait(last)
                    own_wait(nc.vector.tensor_tensor(x2[:], x2[:], h0[:], ALU.add))
                    for t in range(GROUP):
                        last = nc.vector.tensor_tensor(res[:, t, :], xg[:, t, :], bout[:], ALU.add)
                    own_wait(last)
                    own_wait(nc.vector.tensor_tensor(res[:], res[:], x2[:], ALU.add))
                    stats(g, 0, x2)
                    dve.wait_ge(rstd_ok, 2 * g + 1)
                    for t in range(GROUP):
                        nc.vector.tensor_scalar(x2[:, t, :], x2[:, t, :], mv[:, 0, t, 0:1], rstd[:, 0, t:t + 1],
                                                ALU.subtract, ALU.mult).then_inc(yn_ok, 1)
                    if g >= 1:
                        dve.wait_ge(x1_st, 16 * g)
                    for t in range(GROUP):
                        dve.wait_ge(out_mm, GROUP * g + t + 1)
                        nc.vector.tensor_tensor(x1[:, t, :], mm_ps[t % 6][:, 0:FEAT], res[:, t, :], ALU.add).then_inc(x1_ok, 1)
                    dve.wait_ge(x1_ok, GROUP * (g + 1))
                    stats(g, 1, x1)
                    dve.wait_ge(rstd_ok, 2 * g + 2)
                    for t in range(GROUP):
                        nc.vector.tensor_scalar(x2[:, t, :], x1[:, t, :], mv[:, 1, t, 0:1], rstd[:, 1, t:t + 1],
                                                ALU.subtract, ALU.mult).then_inc(h1_ok, 1)
                    dve.wait_ge(gate_ok, g + 1)
                    for t in range(GROUP):
                        n_t = GROUP * g + t
                        if n_t >= 2:
                            dve.wait_ge(msg_st[n_t % 2], 16 * (n_t // 2))
                        for c in range(0, PAIRS, 2):
                            dve.wait_ge(msg_mm, PAIRS * n_t + c + 1)
                            nc.vector.tensor_tensor(
                                msg[:, n_t % 2, c * 512:(c + 1) * 512].rearrange("p (r f) -> p r f", r=2),
                                mm_ps[(PAIRS * n_t + c) % 6][:].rearrange("p (r f) -> p r f", r=2),
                                gate[:, t, 2 * c:2 * c + 2].rearrange("p (r o) -> p r o", o=1).to_broadcast([P, 2, FEAT]),
                                ALU.mult).then_inc(ev_dve, 1)

            @block.gpsimd
            def _(pool):
                for n in range(2 * GROUPS):
                    pool.wait_ge(stat, n + 1)
                    nc.gpsimd.tensor_tensor(rstd[:, n % 2, :], veps[:, n % 2, :], neg_half[:], ALU.pow).then_inc(rstd_ok, 1)

            @block.scalar
            def _(act):
                act.wait_ge(w_ld, 16 * 10)
                for g in range(GROUPS):
                    for t in range(GROUP):
                        act.wait_ge(tr_ok, 2 * GROUP * g + t + 1)
                        for k in range(KC):
                            last = nc.scalar.activation(yT[:, k, t * P:(t + 1) * P], tr_ps[t % 2][:, k, :], ACT.Identity,
                                                        scale=gb[:, 0, k:k + 1], bias=gb[:, 1, k:k + 1])
                        last.then_inc(yt_ok, 1)
                    for m in range(2 * FFC):
                        act.wait_ge(hid_mm, 2 * FFC * g + m + 1)
                        nc.scalar.activation(hid[:, m // 2, (m % 2) * HN:(m % 2 + 1) * HN], mm_ps[m % 6][:, 0:HN], ACT.Gelu,
                                             bias=bin_c[:, m // 2:m // 2 + 1]).then_inc(hid_ok, 1)
                    for t in range(GROUP):
                        act.wait_ge(tr_ok, GROUP * (2 * g + 1) + t + 1)
                        nc.scalar.activation(h1T[:, :, t * P:(t + 1) * P], tr_ps[(t + 1) % 2][:], ACT.Relu).then_inc(h1t_ok, 1)
                    act.wait_ge(gate_mm, g + 1)
                    if g >= 1:
                        act.wait_ge(ev_dve, (PAIRS // 2) * GROUP * g)
                        act.wait_ge(ev_act, PAIRS * GROUP * g)
                    nc.scalar.activation(gate[:].rearrange("p t r -> p (t r)"), gate_ps, ACT.Sigmoid).then_inc(gate_ok, 1)
                    act.wait_ge(gate_ok, g + 1)
                    for t in range(GROUP):
                        n_t = GROUP * g + t
                        if n_t >= 2:
                            act.wait_ge(msg_st[n_t % 2], 16 * (n_t // 2))
                        for c in range(1, PAIRS, 2):
                            act.wait_ge(msg_mm, PAIRS * n_t + c + 1)
                            for r in range(2):
                                nc.scalar.mul(msg[:, n_t % 2, c * 512 + r * FEAT:c * 512 + (r + 1) * FEAT],
                                              mm_ps[(PAIRS * n_t + c) % 6][:, r * FEAT:(r + 1) * FEAT],
                                              gate[:, t, 2 * c + r:2 * c + r + 1]).then_inc(ev_act, 1)

            @block.tensor
            def _(pe):
                pe.wait_ge(w_ld, 16 * 10)
                for g in range(GROUPS):
                    for t in range(GROUP):
                        pe.wait_ge(yn_ok, GROUP * g + t + 1)
                        if t >= 2:
                            pe.wait_ge(yt_ok, GROUP * g + t - 1)
                        elif g >= 1:
                            pe.wait_ge(gate_ok, g)
                        for k in range(KC):
                            last = nc.tensor.transpose(tr_ps[t % 2][:, k, :], x2[:, t, k * P:(k + 1) * P], ident[:])
                        last.then_inc(tr_ok, 1)
                    if g >= 1:
                        pe.wait_ge(ev_act, PAIRS * GROUP * g)
                        pe.wait_ge(ev_dve, (PAIRS // 2) * GROUP * g)
                    pe.wait_ge(yt_ok, GROUP * (g + 1))
                    for m in range(2 * FFC):
                        if m >= 6:
                            pe.wait_ge(hid_ok, 2 * FFC * g + m - 5)
                        for k in range(KC):
                            last = nc.tensor.matmul(mm_ps[m % 6][:, 0:HN], win[:, k, (m // 2) * P:(m // 2 + 1) * P],
                                                    yT[:, k, (m % 2) * HN:(m % 2 + 1) * HN], start=(k == 0), stop=(k == KC - 1))
                        last.then_inc(hid_mm, 1)
                    pe.wait_ge(hid_ok, 2 * FFC * (g + 1))
                    for t in range(GROUP):
                        if t >= 6:
                            pe.wait_ge(x1_ok, GROUP * g + t - 5)
                        for m in range(FFC):
                            last = nc.tensor.matmul(mm_ps[t % 6][:, 0:FEAT], hid[:, m, t * P:(t + 1) * P], wout[:, m, :],
                                                    start=(m == 0), stop=(m == FFC - 1))
                        last.then_inc(out_mm, 1)
                    for t in range(GROUP):
                        pe.wait_ge(h1_ok, GROUP * g + t + 1)
                        if t >= 2:
                            pe.wait_ge(h1t_ok, GROUP * g + t - 1)
                        for k in range(KC):
                            last = nc.tensor.transpose(tr_ps[(t + 1) % 2][:, k, :], x2[:, t, k * P:(k + 1) * P], ident[:])
                        last.then_inc(tr_ok, 1)
                    pe.wait_ge(h1t_ok, GROUP * (g + 1))
                    for t in range(GROUP):
                        for k in range(KC):
                            last = nc.tensor.matmul(gate_ps[:, t * RELS:(t + 1) * RELS], h1T[:, k, t * P:(t + 1) * P], wgate[:, k, :],
                                                    start=(k == 0), stop=(k == KC - 1))
                    last.then_inc(gate_mm, 1)
                    for t in range(GROUP):
                        n_t = GROUP * g + t
                        for c in range(PAIRS):
                            m = PAIRS * n_t + c
                            if c >= 6 or t >= 1:
                                old = m - 6
                                if old % 2 == 0:
                                    pe.wait_ge(ev_dve, old // 2 + 1)
                                else:
                                    pe.wait_ge(ev_act, old + 1)
                            else:
                                pe.wait_ge(x1_ok, GROUP * (g + 1))
                            for k in range(KC):
                                last = nc.tensor.matmul(mm_ps[m % 6][:], h1T[:, k, t * P:(t + 1) * P],
                                                        wrel[:, k, 2 * c:2 * c + 2, :].rearrange("p r f -> p (r f)"),
                                                        start=(k == 0), stop=(k == KC - 1))
                            last.then_inc(msg_mm, 1)


def finish(nc, sb, sem, x1_d, agg1_d, out):
    ld, dve_did, st = [sem(f"fin_ld{i}") for i in range(2)], sem("fin_dve"), sem("fin_st")
    with ExitStack() as ctx:
        a = sb(ctx, "fin_a", [P, GROUPS, GROUP, FEAT])
        b = sb(ctx, "fin_b", [P, 2, GROUP, FEAT])
        rows = lambda d: d.rearrange("(g t p) f -> g p t f", t=GROUP, p=P)
        with nc.Block() as block:
            @block.sync
            def _(sp):
                def load(g):
                    sp.dma_start(a[:, g], rows(x1_d)[g]).then_inc(ld[g % 2], 16)
                    sp.dma_start(b[:, g % 2], rows(agg1_d)[g]).then_inc(ld[g % 2], 16)

                def store(g):
                    sp.wait_ge(dve_did, g + 1)
                    last = g == GROUPS - 1
                    tiles = GROUP - 1 if last else GROUP
                    r0 = g * GROUP * P
                    sp.dma_start(out[r0:r0 + tiles * P, :].rearrange("(t p) f -> p t f", p=P), a[:, g, 0:tiles]).then_inc(st, 16)
                    if last:
                        sp.dma_start(out[NODES - LAST_ROWS:, :], a[0:LAST_ROWS, g, tiles]).then_inc(st, 16)

                load(0)
                load(1)
                for g in range(GROUPS):
                    store(g)
                    if g + 2 < GROUPS:
                        load(g + 2)
                sp.wait_ge(st, 16 * (GROUPS + 1))

            @block.vector
            def _(dve):
                for g in range(GROUPS):
                    dve.wait_ge(ld[g % 2], 32 * (g // 2 + 1))
                    nc.vector.scalar_tensor_tensor(out=a[:, g], in0=b[:, g % 2], scalar=0.0, in1=a[:, g],
                                                   op0=ALU.max, op1=ALU.add).then_inc(dve_did, 1)


_OUT = ((NODES, FEAT), "float32")
_NAMES = ["x", "src", "dst", "edge_type_16", "edge_weight1", "L0_gnn_Wqkv", "L0_gnn_bqkv", "L0_gnn_ln_attn_g",
          "L0_gnn_ln_attn_b", "L0_gnn_ln_res_g", "L0_gnn_ln_res_b", "L0_gnn_W_in", "L0_gnn_b_in", "L0_gnn_W_out",
          "L0_gnn_b_out", "L1_gnn_weight", "L1_gnn_gate_weight"]


def kernel(**inputs):
    import numpy as _np
    import concourse.bacc as _bacc
    from concourse import mybir as _mybir
    from concourse.bass_utils import run_bass_kernel_spmd as _run

    nc = _bacc.Bacc("TRN2", target_bir_lowering=False, num_devices=1)
    arrays, args = {}, []
    for name in _NAMES:
        a = _np.asarray(inputs[name])
        if name == "x":
            a = _np.pad(a, ((0, NODES_PAD - NODES), (0, 0)))
        if name in ("src", "edge_type_16"):
            a = _np.pad(a, (0, EDGES_PAD - EDGES))
        if name == "dst":
            a = _np.pad(a, (0, EDGES_PAD - EDGES), constant_values=DST_PAD)
        if name == "edge_weight1":
            a = _np.pad(a.reshape(EDGES), (0, EDGES_PAD - EDGES))
        a = _np.ascontiguousarray(a)
        arrays[f"in_{name}_dram"] = a
        args.append(nc.dram_tensor(f"in_{name}_dram", a.shape, _mybir.dt.from_np(a.dtype), kind="ExternalInput").ap())
    args.append(nc.dram_tensor("out_0_dram", _OUT[0], _mybir.dt.from_np(_np.dtype(_OUT[1])), kind="ExternalOutput").ap())
    gnn_program(nc, *args)
    r = _run(nc, [arrays], core_ids=[0])
    return r.results[0]["out_0_dram"]
```

```python
from contextlib import ExitStack

import concourse.bass as bass
from concourse import mybir

F32 = mybir.dt.float32
BF16 = mybir.dt.bfloat16
I32 = mybir.dt.int32
ALU = mybir.AluOpType
ACT = mybir.ActivationFunctionType
AX_X = mybir.AxisListType.X

P = 128
NODES, FEAT = 6250, 256
EDGES = 100000
HEADS = 8
HEAD_DIM = FEAT // HEADS
DFF = 4 * FEAT
RELS = 16
EPS = 1e-5
ATT_SCALE = float(FEAT) ** -0.5
KC = FEAT // P
FFC = DFF // P

NODE_TILES = -(-NODES // P)
NODES_PAD = NODE_TILES * P
LAST_ROWS = NODES - (NODE_TILES - 1) * P
GROUP = 7
GROUPS = NODE_TILES // GROUP
EDGE_TILES = -(-EDGES // P)
IC = 112
ICN = 7
EDGE_TILES_PAD = IC * ICN
EDGES_PAD = EDGE_TILES_PAD * P
UNROLL = 16
AHEAD = 4
HALF = UNROLL // 2
STEPS = 832
assert EDGE_TILES + NODE_TILES - 1 <= STEPS and STEPS % UNROLL == 0
ROUNDS = STEPS // UNROLL
SH = STEPS // 2
DST_PAD = 6400
NOT_LAST = 4096
QUAD = 4
CHUNKS = P // HEADS
CHUNK_STEPS = STEPS // CHUNKS
CHUNK = CHUNK_STEPS * P
BIG = 1.0e30
AGGW = FEAT + HEADS
BLOCKS = STEPS // 16
ACC_RING = 8
PAIRS = RELS // 2


def gnn_program(nc, x, src, dst, rel, norm, wqkv, bqkv, g_attn, b_attn, g_res, b_res,
                w_in, b_in, w_out, b_out, w_rel, w_gate, out):
    def dram(name, shape, dt=F32):
        return nc.dram_tensor(name, shape, dt, kind="Internal").ap()

    h0_d = dram("h0_d", [NODES_PAD, FEAT])
    q_d = dram("q_d", [NODES_PAD, FEAT])
    v_d = dram("v_d", [NODES_PAD, FEAT])
    x1_d = dram("x1_d", [NODES_PAD, FEAT])
    msg_d = dram("msg_d", [NODES_PAD * RELS, FEAT])
    agg_d = dram("agg_d", [NODES_PAD, AGGW])
    agg1_d = dram("agg1_d", [NODES_PAD, FEAT])
    scores_d = dram("scores_d", [STEPS * HEADS, P])
    probs_d = dram("probs_d", [(STEPS + UNROLL) * HEADS, P])
    key_d = dram("key_d", [STEPS * P + 2 * P])

    with ExitStack() as whole:
        def sb(ctx, name, shape, dt=F32):
            return ctx.enter_context(nc.sbuf_tensor(name, shape, dt))

        def ps(ctx, name, shape, dt=F32):
            return ctx.enter_context(nc.psum_tensor(name, shape, dt))

        def sem(name):
            return whole.enter_context(nc.semaphore(name))

        iota_n = sb(whole, "iota_n", [P, P])
        ident = sb(whole, "ident", [P, P])
        ident_b = sb(whole, "ident_b", [P, P], BF16)
        part = sb(whole, "part", [P, 1])
        ones = sb(whole, "ones", [P, P])
        neg_half = sb(whole, "neg_half", [P, GROUP])
        dloc = sb(whole, "dloc", [P, STEPS + AHEAD])
        keep = sb(whole, "keep", [P, STEPS])
        norm_s = sb(whole, "norm_s", [P, STEPS])
        src_i = sb(whole, "src_i", [P, STEPS], I32)
        msg_i = sb(whole, "msg_i", [P, STEPS], I32)
        tile_i = sb(whole, "tile_i", [P, STEPS], I32)
        ends_i = sb(whole, "ends_i", [P, STEPS // QUAD], I32)
        store_i = sb(whole, "store_i", [P, STEPS], I32)
        idx_now = sb(whole, "idx_now", [P, 2, HALF], I32)

        build_steps(nc, sb, ps, sem, src, dst, rel, norm, key_d, iota_n, ident, ident_b, part, ones,
                    neg_half, dloc, keep, norm_s, src_i, msg_i, tile_i, store_i, ends_i)
        with ExitStack() as att:
            k_all = sb(att, "k_all", [P, (NODE_TILES + 1) * FEAT])
            node_inputs(nc, sb, ps, sem, x, wqkv, bqkv, g_attn, b_attn, ident, neg_half,
                        h0_d, q_d, v_d, k_all)
            edge_scores(nc, sb, ps, sem, q_d, scores_d, k_all, iota_n, ident, ident_b, dloc, src_i, tile_i, idx_now)
        softmax_numerators(nc, sb, ps, sem, scores_d, probs_d, key_d, ident, ones)
        edge_sum(nc, sb, ps, sem, "att", v_d, agg_d, AGGW, probs_d, iota_n, ident, dloc, None, keep,
                 src_i, store_i, ends_i, idx_now)
        node_update(nc, sb, ps, sem, x, g_res, b_res, w_in, b_in, w_out, b_out, w_rel, w_gate, ident,
                    neg_half, h0_d, agg_d, x1_d, msg_d)
        edge_sum(nc, sb, ps, sem, "rel", msg_d, agg1_d, FEAT, None, iota_n, ident, dloc, norm_s, keep,
                 msg_i, store_i, ends_i, idx_now)
        finish(nc, sb, sem, x1_d, agg1_d, out)


def build_steps(nc, sb, ps, sem, src, dst, rel, norm, key_d, iota_n, ident, ident_b, part, ones,
                neg_half, dloc, keep, norm_s, src_i, msg_i, tile_i, store_i, ends_i):
    loaded = sem("steps_loaded")
    consts = sem("consts_made")
    dve_did = sem("steps_dve")
    pe_did = sem("steps_pe")
    sel_free = sem("steps_sel_free")
    key_out = sem("key_out")
    with ExitStack() as ctx:
        cols_i = sb(ctx, "cols_i", [IC, 3, ICN, P], I32)
        cols = sb(ctx, "cols", [IC, 4, ICN, P])
        last_i = sb(ctx, "last_i", [1, EDGE_TILES_PAD], I32)
        last_f = sb(ctx, "last_f", [1, EDGE_TILES_PAD])
        step_no = sb(ctx, "step_no", [P, STEPS])
        bound = sb(ctx, "bound", [P, 1])
        full = sb(ctx, "full", [P, 1])
        pos = sb(ctx, "pos", [P, 1])
        scratch = sb(ctx, "steps_scratch", [P, STEPS])
        before = sb(ctx, "before", [P, STEPS])
        node_tile = sb(ctx, "node_tile", [P, STEPS + QUAD])
        edge_tile = sb(ctx, "edge_tile", [P, STEPS])
        part_c = sb(ctx, "part_c", [P, ICN])
        sel = sb(ctx, "sel", [IC, 2, STEPS])
        src_f = sb(ctx, "src_f", [P, STEPS])
        valid = sb(ctx, "valid", [P, STEPS])
        key = sb(ctx, "key", [P, STEPS])
        key_t = sb(ctx, "key_t", [P, ICN, P])
        guard = sb(ctx, "guard", [1, 2 * P])
        pb = [ps(ctx, f"steps_ps{b}", [P, 512]) for b in range(8)]

        with nc.Block() as block:
            @block.sync
            def _(sp):
                for n, a in enumerate((src, dst, rel)):
                    sp.dma_start(cols_i[:, n], a.rearrange("(c i p) -> i c p", i=IC, p=P)).then_inc(loaded, 16)
                sp.dma_start(cols[:, 3], norm.rearrange("(c i p) -> i c p", i=IC, p=P)).then_inc(loaded, 16)
                with nc.allow_non_contiguous_dma("one dst of each edge tile"):
                    sp.dma_start(last_i[:], dst.rearrange("(a i p) -> a i p", a=1, p=P)[:, :, P - 1]).then_inc(loaded, 16)
                sp.wait_ge(dve_did, 30)
                kd = key_d[P:P + STEPS * P].rearrange("(s p) -> s p", p=P)
                for c in range(ICN):
                    n = min(P, STEPS - c * P)
                    sp.dma_start(kd[c * P:c * P + n, :], key_t[0:n, c, :]).then_inc(key_out, 16)
                gd = key_d[:].rearrange("(a n) -> a n", a=1)
                sp.dma_start(gd[:, 0:P], guard[:, 0:P]).then_inc(key_out, 16)
                sp.dma_start(gd[:, P + STEPS * P:], guard[:, P:]).then_inc(key_out, 16)
                sp.wait_ge(key_out, 16 * (ICN + 2))

            @block.gpsimd
            def _(pool):
                nc.gpsimd.iota(iota_n[:], [[1, P]], base=0, channel_multiplier=0,
                               allow_small_or_imprecise_dtypes=True).then_inc(consts, 1)
                nc.gpsimd.iota(step_no[:], [[1, STEPS]], base=0, channel_multiplier=0,
                               allow_small_or_imprecise_dtypes=True).then_inc(consts, 1)
                nc.gpsimd.iota(part[:], [[1, 1]], base=0, channel_multiplier=1,
                               allow_small_or_imprecise_dtypes=True).then_inc(consts, 1)
                nc.gpsimd.iota(bound[:], [[1, 1]], base=P, channel_multiplier=P,
                               allow_small_or_imprecise_dtypes=True).then_inc(consts, 1)
                nc.gpsimd.iota(part_c[:], [[IC, ICN]], base=0, channel_multiplier=1,
                               allow_small_or_imprecise_dtypes=True).then_inc(consts, 1)
                nc.gpsimd.memset(ones[:], 1.0).then_inc(consts, 1)
                nc.gpsimd.memset(neg_half[:], -0.5).then_inc(consts, 1)
                nc.gpsimd.memset(guard[:], -2.0).then_inc(consts, 1)

            @block.vector
            def _(dve):
                done = [0]

                def did(ins):
                    done[0] += 1
                    ins.then_inc(dve_did, 1)
                    dve.wait_ge(dve_did, done[0])
                    return done[0]

                dve.wait_ge(consts, 8)
                nc.vector.memset(dloc[:, STEPS:], -1.0)
                did(nc.vector.tensor_scalar(ident[:], iota_n[:], part[:], None, ALU.is_equal))
                did(nc.vector.tensor_copy(ident_b[:], ident[:]))
                dve.wait_ge(loaded, 80)
                did(nc.vector.tensor_copy(last_f[:], last_i[:]))
                did(nc.vector.tensor_copy(cols[:, 0:3], cols_i[:]))
                n = EDGE_TILES_PAD // 2
                dve.wait_ge(pe_did, 2)
                did(nc.vector.tensor_scalar(scratch[:, 0:n], pb[0][:, 0:n], bound[:], 0.0, ALU.is_lt, ALU.add,
                                            accum_out=full[:]))
                did(nc.vector.tensor_scalar(scratch[:, 0:n], pb[1][:, 0:n], bound[:], full[:], ALU.is_lt, ALU.add,
                                            accum_out=pos[:]))
                did(nc.vector.tensor_tensor(pos[:], pos[:], part[:], ALU.add))
                did(nc.vector.tensor_scalar(before[:], step_no[:], pos[:], None, ALU.is_gt))
                dve.wait_ge(pe_did, 4)
                did(nc.vector.tensor_copy(node_tile[:, 0:SH], pb[2][:, 0:SH]))
                did(nc.vector.tensor_copy(node_tile[:, SH:STEPS], pb[3][:, 0:SH]))
                did(nc.vector.tensor_copy(node_tile[:, STEPS:], node_tile[:, STEPS - 1:STEPS].to_broadcast([P, QUAD])))
                did(nc.vector.tensor_tensor(edge_tile[:], step_no[:], node_tile[:, 0:STEPS], ALU.subtract))
                for c in range(ICN):
                    if c >= 2:
                        dve.wait_ge(sel_free, c - 1)
                    did(nc.vector.tensor_scalar(sel[:, c % 2], edge_tile[0:IC, :], part_c[0:IC, c:c + 1], None,
                                                ALU.is_equal))
                dve.wait_ge(pe_did, 5)
                for h in range(2):
                    a, b = h * SH, (h + 1) * SH
                    nc.vector.tensor_copy(src_f[:, a:b], pb[h][:, 0:SH])
                    nc.vector.tensor_copy(src_i[:, a:b], pb[h][:, 0:SH])
                    nc.vector.scalar_tensor_tensor(out=dloc[:, a:b], in0=node_tile[:, a:b], scalar=-float(P),
                                                   in1=pb[2 + h][:, 0:SH], op0=ALU.mult, op1=ALU.add)
                    nc.vector.tensor_copy(scratch[:, a:b], pb[4 + h][:, 0:SH])
                    did(nc.vector.tensor_copy(norm_s[:, a:b], pb[6 + h][:, 0:SH]))
                did(nc.vector.scalar_tensor_tensor(out=msg_i[:], in0=src_f[:], scalar=float(RELS), in1=scratch[:],
                                                   op0=ALU.mult, op1=ALU.add))
                nc.vector.tensor_copy(tile_i[:], node_tile[:, 0:STEPS])
                quad = node_tile[:].rearrange("p (n q) -> p n q", q=QUAD)
                nc.vector.tensor_tensor(ends_i[:], quad[:, 1:, 0], quad[:, 0:STEPS // QUAD, 0], ALU.not_equal)
                did(nc.vector.tensor_tensor(before[:], node_tile[:, 1:STEPS + 1], node_tile[:, 0:STEPS], ALU.is_equal))
                nc.vector.memset(keep[:, 0:1], 0.0)
                nc.vector.tensor_copy(keep[:, 1:], before[:, 0:STEPS - 1])
                did(nc.vector.scalar_tensor_tensor(out=store_i[:], in0=before[:], scalar=float(NOT_LAST),
                                                   in1=node_tile[:, 0:STEPS], op0=ALU.mult, op1=ALU.add))
                did(nc.vector.tensor_scalar(valid[:], dloc[:, 0:STEPS], 0.0, None, ALU.is_ge))
                did(nc.vector.scalar_tensor_tensor(out=valid[:], in0=dloc[:, 0:STEPS], scalar=float(P), in1=valid[:],
                                                   op0=ALU.is_lt, op1=ALU.mult))
                did(nc.vector.scalar_tensor_tensor(out=key[:], in0=node_tile[:, 0:STEPS], scalar=float(P), in1=dloc[:, 0:STEPS],
                                                   op0=ALU.mult, op1=ALU.add))
                did(nc.vector.scalar_tensor_tensor(out=key[:], in0=key[:], scalar=1.0, in1=valid[:],
                                                   op0=ALU.add, op1=ALU.mult))
                did(nc.vector.tensor_scalar(key[:], key[:], -1.0, None, ALU.add))
                dve.wait_ge(pe_did, 6)
                for c in range(ICN):
                    n = min(P, STEPS - c * P)
                    last = nc.vector.tensor_copy(key_t[0:n, c, :], pb[c // 4][0:n, (c % 4) * P:(c % 4 + 1) * P])
                did(last)

            @block.tensor
            def _(pe):
                n = EDGE_TILES_PAD // 2
                pe.wait_ge(dve_did, 3)
                for h in range(2):
                    nc.tensor.matmul(pb[h][:, 0:n], ones[0:1, :], last_f[:, h * n:(h + 1) * n],
                                     start=True, stop=True).then_inc(pe_did, 1)
                pe.wait_ge(dve_did, 8)
                for h in range(2):
                    nc.tensor.matmul(pb[2 + h][:, 0:SH], ones[0:NODE_TILES, :], before[0:NODE_TILES, h * SH:(h + 1) * SH],
                                     start=True, stop=True).then_inc(pe_did, 1)
                for c in range(ICN):
                    pe.wait_ge(dve_did, 13 + c)
                    for n in range(4):
                        for h in range(2):
                            mm = nc.tensor.matmul(pb[2 * n + h][:, 0:SH], cols[:, n, c, :],
                                                  sel[:, c % 2, h * SH:(h + 1) * SH],
                                                  start=(c == 0), stop=(c == ICN - 1))
                    mm.then_inc(sel_free, 1)
                pe.nop()
                pe.wait_ge(sel_free, ICN)
                pe.sem_inc(pe_did, 1)
                pe.wait_ge(dve_did, 29)
                for c in range(ICN):
                    n = min(P, STEPS - c * P)
                    tr = nc.tensor.transpose(pb[c // 4][0:n, (c % 4) * P:(c % 4 + 1) * P], key[:, c * P:c * P + n], ident[:])
                tr.then_inc(pe_did, 1)


def node_inputs(nc, sb, ps, sem, x, wqkv, bqkv, g_attn, b_attn, ident, neg_half, h0_d, q_d, v_d, k_all):
    w_ld = sem("in_w")
    x_ld = [sem(f"in_x{i}") for i in range(2)]
    x_free = sem("in_x_free")
    stat = sem("in_stat")
    rstd_ok = sem("in_rstd")
    h0_ok = sem("in_h0")
    hn_ok = sem("in_hn")
    tr_ok = sem("in_tr")
    ht_ok = sem("in_ht")
    mm_ok = sem("in_mm")
    ev_ok = sem("in_ev")
    st_h0 = sem("in_st_h0")
    st_qv = sem("in_st_qv")
    own = sem("in_own")
    with ExitStack() as ctx:
        wq = sb(ctx, "wq", [P, KC, 3 * FEAT])
        bias = sb(ctx, "qkv_bias", [P, 3 * FEAT])
        gb = sb(ctx, "attn_gb", [P, 2, KC])
        xg = sb(ctx, "xg", [P, 2, GROUP, FEAT])
        h0 = sb(ctx, "h0", [P, GROUP, FEAT])
        hn = sb(ctx, "hn", [P, GROUP, FEAT])
        hT = sb(ctx, "hT", [P, 2, KC, P])
        qv = sb(ctx, "qv", [P, 2, GROUP, FEAT])
        st6 = sb(ctx, "st6", [P, GROUP, 6])
        mv = sb(ctx, "mv", [P, 2, GROUP, 2])
        veps = sb(ctx, "veps", [P, 2, GROUP])
        rstd = sb(ctx, "rstd", [P, 2, GROUP])
        shift = sb(ctx, "shift", [P, GROUP])
        tr_ps = [ps(ctx, f"in_tr{i}", [P, KC, P]) for i in range(2)]
        qk_ps = [ps(ctx, f"in_qk{i}", [P, 512]) for i in range(2)]
        v_ps = [ps(ctx, f"in_v{i}", [P, FEAT]) for i in range(2)]
        rows = lambda d: d.rearrange("(g t p) f -> g p t f", t=GROUP, p=P)

        with nc.Block() as block:
            @block.sync
            def _(sp):
                def store(g):
                    sp.wait_ge(h0_ok, g + 1)
                    sp.dma_start(rows(h0_d)[g], h0[:]).then_inc(st_h0, 16)
                    sp.wait_ge(ev_ok, GROUP * (g + 1))
                    sp.dma_start(rows(q_d)[g], qv[:, 0]).then_inc(st_qv, 16)
                    sp.dma_start(rows(v_d)[g], qv[:, 1]).then_inc(st_qv, 16)

                sp.dma_start(wq[:], wqkv.rearrange("(k p) n -> p k n", p=P)).then_inc(w_ld, 16)
                sp.dma_start(bias[:], bqkv.rearrange("(a n) -> a n", a=1).to_broadcast([P, 3 * FEAT])).then_inc(w_ld, 16)
                with nc.allow_non_contiguous_dma("two columns of LN parameters"):
                    sp.dma_start(gb[:, 0], g_attn.rearrange("(k p) -> p k", p=P)).then_inc(w_ld, 16)
                    sp.dma_start(gb[:, 1], b_attn.rearrange("(k p) -> p k", p=P)).then_inc(w_ld, 16)
                for g in range(GROUPS):
                    if g >= 2:
                        sp.wait_ge(h0_ok, g - 1)
                    sp.dma_start(xg[:, g % 2], rows(x)[g]).then_inc(x_ld[g % 2], 16)
                    if g >= 1:
                        store(g - 1)
                store(GROUPS - 1)
                sp.wait_ge(st_h0, 16 * GROUPS)
                sp.wait_ge(st_qv, 32 * GROUPS)

            @block.vector
            def _(dve):
                n = [0]

                def own_wait(ins):
                    n[0] += 1
                    ins.then_inc(own, 1)
                    dve.wait_ge(own, n[0])

                def stats(g, which, data):
                    for t in range(GROUP):
                        last = nc.vector.bn_stats(st6[:, t, :], data[:, t, :])
                    own_wait(last)
                    for t in range(GROUP):
                        last = nc.vector.bn_aggr(mv[:, which, t, :], st6[:, t, :])
                    own_wait(last)
                    nc.vector.tensor_scalar(veps[:, which, :], mv[:, which, :, 1], EPS, None, ALU.add).then_inc(stat, 1)

                dve.wait_ge(w_ld, 64)
                own_wait(nc.vector.memset(k_all[:, NODE_TILES * FEAT:], 0.0))
                for g in range(GROUPS):
                    dve.wait_ge(x_ld[g % 2], 16 * (g // 2 + 1))
                    stats(g, 0, xg[:, g % 2])
                    dve.wait_ge(rstd_ok, 2 * g + 1)
                    if g >= 1:
                        dve.wait_ge(h0_ok, g)
                    nc.vector.scalar_tensor_tensor(out=shift[:], in0=mv[:, 0, :, 0], scalar=-1.0, in1=rstd[:, 0, :],
                                                   op0=ALU.mult, op1=ALU.mult).then_inc(stat, 1)
                    dve.wait_ge(h0_ok, g + 1)
                    stats(g, 1, h0)
                    dve.wait_ge(rstd_ok, 2 * g + 2)
                    if g >= 1:
                        dve.wait_ge(tr_ok, GROUP * g)
                    for t in range(GROUP):
                        nc.vector.tensor_scalar(hn[:, t, :], h0[:, t, :], mv[:, 1, t, 0:1], rstd[:, 1, t:t + 1],
                                                ALU.subtract, ALU.mult).then_inc(hn_ok, 1)
                    if g >= 1:
                        dve.wait_ge(st_qv, 32 * g)
                    for t in range(GROUP):
                        n_t = GROUP * g + t
                        dve.wait_ge(mm_ok, n_t + 1)
                        nc.vector.tensor_tensor(qv[:, 0, t, :], qk_ps[n_t % 2][:, 0:FEAT], bias[:, 0:FEAT], ALU.add)
                        nc.vector.tensor_tensor(k_all[:, n_t * FEAT:(n_t + 1) * FEAT], qk_ps[n_t % 2][:, FEAT:], bias[:, FEAT:2 * FEAT], ALU.add)
                        nc.vector.tensor_tensor(qv[:, 1, t, :], v_ps[n_t % 2][:], bias[:, 2 * FEAT:], ALU.add).then_inc(ev_ok, 1)

            @block.gpsimd
            def _(pool):
                for g in range(GROUPS):
                    for which in range(2):
                        pool.wait_ge(stat, 3 * g + 1 + 2 * which)
                        nc.gpsimd.tensor_tensor(rstd[:, which, :], veps[:, which, :], neg_half[:], ALU.pow).then_inc(rstd_ok, 1)

            @block.scalar
            def _(act):
                act.wait_ge(w_ld, 64)
                for g in range(GROUPS):
                    act.wait_ge(stat, 3 * g + 2)
                    if g >= 1:
                        act.wait_ge(st_h0, 16 * g)
                        act.wait_ge(hn_ok, GROUP * g)
                    for t in range(GROUP):
                        last = nc.scalar.activation(h0[:, t, :], xg[:, g % 2, t, :], ACT.Relu,
                                                    scale=rstd[:, 0, t:t + 1], bias=shift[:, t:t + 1])
                    last.then_inc(h0_ok, 1)
                    for t in range(GROUP):
                        n_t = GROUP * g + t
                        act.wait_ge(tr_ok, n_t + 1)
                        if n_t >= 2:
                            act.wait_ge(mm_ok, n_t - 1)
                        for k in range(KC):
                            last = nc.scalar.activation(hT[:, n_t % 2, k, :], tr_ps[n_t % 2][:, k, :], ACT.Identity,
                                                        scale=gb[:, 0, k:k + 1], bias=gb[:, 1, k:k + 1])
                        last.then_inc(ht_ok, 1)

            @block.tensor
            def _(pe):
                def products(m):
                    pe.wait_ge(ht_ok, m + 1)
                    if m >= 2:
                        pe.wait_ge(ev_ok, m - 1)
                    for k in range(KC):
                        nc.tensor.matmul(qk_ps[m % 2][:], hT[:, m % 2, k, :], wq[:, k, 0:512], start=(k == 0), stop=(k == KC - 1))
                    for k in range(KC):
                        last = nc.tensor.matmul(v_ps[m % 2][:], hT[:, m % 2, k, :], wq[:, k, 512:], start=(k == 0), stop=(k == KC - 1))
                    last.then_inc(mm_ok, 1)

                pe.wait_ge(w_ld, 64)
                for g in range(GROUPS):
                    for t in range(GROUP):
                        n_t = GROUP * g + t
                        pe.wait_ge(hn_ok, n_t + 1)
                        if n_t >= 2:
                            pe.wait_ge(ht_ok, n_t - 1)
                        for k in range(KC):
                            last = nc.tensor.transpose(tr_ps[n_t % 2][:, k, :], hn[:, t, k * P:(k + 1) * P], ident[:])
                        last.then_inc(tr_ok, 1)
                        if t >= 1:
                            products(n_t - 1)
                    products(GROUP * g + GROUP - 1)


def load_indices(eng, idx_now, idx_all, columns, half, idx_ld):
    eng.dma_start(idx_now[:, half, :], idx_all[:, columns]).then_inc(idx_ld[half], 16)


def next_indices(eng, idx_now, idx_all, t0, half, got, idx_ld):
    for b in range(half * HALF, (half + 1) * HALF):
        eng.wait_ge(got[b], t0 + 16)
    load_indices(eng, idx_now, idx_all, bass.ds(t0 + (UNROLL + HALF * half), HALF), half, idx_ld)


def gather_rows(nc, pool, t0, b, rows, table, idx_now, got, used, idx_ld, turn):
    if b % HALF == 0:
        pool.wait_ge(idx_ld[b // HALF], t0 + 16)
        pool.sem_inc(turn, 1)
    pool.wait_ge(used, t0 + (b + 1))
    pool.sem_inc(turn, 1)
    nc.gpsimd.indirect_dma_start(rows[:, b, :], None, table,
                                 bass.IndirectOffsetOnAxis(ap=idx_now[:, b // HALF, b % HALF:b % HALF + 1], axis=0)
                                 ).then_inc(got[b], 16)


def edge_scores(nc, sb, ps, sem, q_d, scores_d, k_all, iota_n, ident, ident_b, dloc, src_i, tile_i, idx_now):
    idx_ld = [sem(f"sc_idx{h}") for h in range(2)]
    got = [sem(f"sc_got{b}") for b in range(UNROLL)]
    used = sem("sc_used")
    turn = sem("sc_turn")
    hot_ok, turned, hott_ok, expanded, prod_ok = (sem(f"sc_{n}") for n in ("hot", "turned", "hott", "exp", "prod"))
    t_ok, c_ok, st = sem("sc_t"), sem("sc_c"), [sem(f"sc_st{i}") for i in range(4)]
    SLOTS = 4
    with ExitStack() as ctx:
        rows = sb(ctx, "q_rows", [P, UNROLL, FEAT])
        scores = sb(ctx, "scores", [P, STEPS * HEADS])
        hot = sb(ctx, "hot_b", [P, 2 * SLOTS, P], BF16)
        hot_t = sb(ctx, "hot_t", [P, SLOTS, P])
        prod = sb(ctx, "prod", [P, 2, HEADS, HEAD_DIM])
        turned_sb = sb(ctx, "scores_t", [P, 4, P])
        hot_ps = [ps(ctx, f"hot_ps{i}", [P, P], BF16) for i in range(2)]
        k_ps = [ps(ctx, f"k_ps{i}", [P, FEAT]) for i in range(SLOTS)]
        out_ps = [ps(ctx, f"sco_ps{i}", [P, P]) for i in range(2)]

        with nc.Block() as block:
            @block.sync
            def _(sp):
                for h in range(2):
                    load_indices(sp, idx_now, src_i, slice(h * HALF, (h + 1) * HALF), h, idx_ld)
                with sp.Fori(0, ROUNDS - 1) as round_no:
                    t0 = sp.snap(round_no * UNROLL)
                    for h in range(2):
                        next_indices(sp, idx_now, src_i, t0, h, got, idx_ld)
                for n in range(BLOCKS):
                    sp.wait_ge(c_ok, n + 1)
                    sp.dma_start(scores_d[n * P:(n + 1) * P, :], turned_sb[:, n % 4, :]).then_inc(st[n % 4], 16)
                for n in range(4):
                    sp.wait_ge(st[n], 16 * (BLOCKS // 4))

            @block.gpsimd
            def _(pool):
                with pool.Fori(0, ROUNDS) as round_no:
                    t0 = pool.snap(round_no * UNROLL)
                    for b in range(UNROLL):
                        gather_rows(nc, pool, t0, b, rows, q_d, idx_now, got, used, idx_ld, turn)

            @block.scalar
            def _(act):
                act.sem_inc(hott_ok, SLOTS)
                with act.Fori(0, ROUNDS) as round_no:
                    t0 = act.snap(round_no * UNROLL)
                    for b in range(UNROLL):
                        act.wait_ge(turned, t0 + (b + 1))
                        act.wait_ge(expanded, t0 + (b + 1))
                        nc.scalar.copy(hot_t[:, b % SLOTS, :], hot_ps[b % 2][:]).then_inc(hott_ok, 1)
                for n in range(BLOCKS):
                    act.wait_ge(t_ok, n + 1)
                    if n >= 4:
                        act.wait_ge(st[n % 4], 16 * (n // 4))
                    nc.scalar.copy(turned_sb[:, n % 4, :], out_ps[n % 2][:]).then_inc(c_ok, 1)

            @block.tensor
            def _(pe):
                pe.sem_inc(expanded, SLOTS)

                def turn_hot(slot):
                    nc.tensor.transpose(hot_ps[slot % 2][:], hot[:, slot % (2 * SLOTS), :], ident_b[:]).then_inc(turned, 1)

                pe.wait_ge(hot_ok, 2)
                turn_hot(0)
                turn_hot(1)
                with pe.Fori(0, ROUNDS) as round_no:
                    t0 = pe.snap(round_no * UNROLL)
                    for b in range(UNROLL):
                        tile = pe.value_load(tile_i[0:1, bass.ds(t0 + b, 1)], min_val=0, max_val=NODE_TILES)
                        pe.wait_ge(hot_ok, t0 + (b + 3))
                        pe.wait_ge(hott_ok, t0 + (b + 1 + SLOTS))
                        turn_hot(b + 2)
                        nc.tensor.matmul(k_ps[b % SLOTS][:], hot_t[:, b % SLOTS, :], k_all[:, bass.ds(tile * FEAT, FEAT)],
                                         start=True, stop=True).then_inc(expanded, 1)
                for n in range(BLOCKS):
                    if n == 0:
                        pe.wait_ge(used, STEPS + UNROLL)
                    if n >= 2:
                        pe.wait_ge(c_ok, n - 1)
                    nc.tensor.transpose(out_ps[n % 2][:], scores[:, n * P:(n + 1) * P], ident[:]).then_inc(t_ok, 1)

            @block.vector
            def _(dve):
                dve.sem_inc(prod_ok, SLOTS)
                dve.sem_inc(used, UNROLL)

                def make_hot(column, slot):
                    nc.vector.tensor_scalar(hot[:, slot % (2 * SLOTS), :], iota_n[:], column, None, ALU.is_equal).then_inc(hot_ok, 1)

                for n in range(AHEAD):
                    make_hot(dloc[:, n:n + 1], n)
                with dve.Fori(0, ROUNDS) as round_no:
                    t0 = dve.snap(round_no * UNROLL)
                    for b in range(UNROLL):
                        dve.wait_ge(got[b], t0 + 16)
                        dve.wait_ge(expanded, t0 + (b + 1 + SLOTS))
                        nc.vector.tensor_tensor(prod[:, b % 2].rearrange("p h d -> p (h d)"), rows[:, b, :], k_ps[b % SLOTS][:],
                                                ALU.mult).then_inc(prod_ok, 1)
                        make_hot(dloc[:, bass.ds(t0 + (b + AHEAD), 1)], b + AHEAD)
                        dve.wait_ge(prod_ok, t0 + (b + 1 + SLOTS))
                        nc.vector.tensor_reduce(scores[:, bass.ds((t0 + b) * HEADS, HEADS)], prod[:, b % 2], AX_X, ALU.add).then_inc(used, 1)


def softmax_numerators(nc, sb, ps, sem, scores_d, probs_d, key_d, ident, ones):
    ld, dve_did, pe_did, exp_ok, st, zero_ok = (sem(f"sm_{n}") for n in ("ld", "dve", "pe", "exp", "st", "zero"))
    with ExitStack() as ctx:
        s = sb(ctx, "sm_s", [P, CHUNK])
        key = sb(ctx, "sm_key", [P, CHUNK + 2])
        brk = sb(ctx, "sm_brk", [P, CHUNK + 1], BF16)
        fwd = sb(ctx, "sm_fwd", [P, CHUNK])
        bwd = sb(ctx, "sm_bwd", [P, CHUNK])
        ends = sb(ctx, "sm_ends", [P, 4])
        rows_sb = sb(ctx, "sm_rows", [1, 4, P])
        carry = sb(ctx, "sm_carry", [1, 2, P])
        carry_c = sb(ctx, "sm_carry_c", [P, 2])
        zeros = sb(ctx, "sm_zeros", [P, P])
        row_ps = ps(ctx, "sm_row_ps", [1, 4 * P])
        col_ps = ps(ctx, "sm_col_ps", [P, 2])

        def by_head(d, h):
            return d.rearrange("(c s h) p -> h c s p", h=HEADS, c=CHUNKS)[h]

        with nc.Block() as block:
            @block.sync
            def _(sp):
                with nc.allow_non_contiguous_dma("runs of one step and head"):
                    for h in range(HEADS):
                        r = slice(h * CHUNKS, (h + 1) * CHUNKS)
                        sp.dma_start(key[r, :], bass.AP(key_d.tensor, P - 1, [[CHUNK, CHUNKS], [1, CHUNK + 2]])).then_inc(ld, 16)
                        sp.dma_start(s[r, :].rearrange("c (s p) -> c s p", p=P), by_head(scores_d, h)).then_inc(ld, 16)
                    sp.wait_ge(zero_ok, 1)
                    sp.dma_start(probs_d[STEPS * HEADS:, :], zeros[:]).then_inc(st, 16)
                    sp.wait_ge(exp_ok, 1)
                    for h in range(HEADS):
                        r = slice(h * CHUNKS, (h + 1) * CHUNKS)
                        sp.dma_start(by_head(probs_d[0:STEPS * HEADS, :], h), s[r, :].rearrange("c (s p) -> c s p", p=P)).then_inc(st, 16)
                    sp.wait_ge(st, 16 * (HEADS + 1))

            @block.gpsimd
            def _(pool):
                nc.gpsimd.memset(zeros[:], 0.0).then_inc(zero_ok, 1)

            @block.vector
            def _(dve):
                done = [0]

                def did(ins):
                    done[0] += 1
                    ins.then_inc(dve_did, 1)
                    dve.wait_ge(dve_did, done[0])

                dve.wait_ge(ld, 32 * HEADS)
                did(nc.vector.tensor_tensor(brk[:], key[:, 1:], key[:, 0:CHUNK + 1], ALU.not_equal))
                did(nc.vector.tensor_scalar(brk[:], brk[:], -BIG, None, ALU.mult))
                did(nc.vector.tensor_tensor_scan(fwd[:], brk[:, 0:CHUNK], s[:], -BIG, ALU.add, ALU.max))
                did(nc.vector.tensor_tensor_scan(bwd[:, ::-1], brk[:, CHUNK:0:-1], s[:, ::-1], -BIG, ALU.add, ALU.max))
                nc.vector.tensor_copy(ends[:, 0:1], fwd[:, CHUNK - 1:])
                nc.vector.tensor_copy(ends[:, 2:3], bwd[:, 0:1])
                nc.vector.tensor_tensor(ends[:, 1:2], key[:, 0:1], key[:, CHUNK:CHUNK + 1], ALU.not_equal)
                did(nc.vector.tensor_tensor(ends[:, 3:4], key[:, 1:2], key[:, CHUNK + 1:], ALU.not_equal))
                dve.wait_ge(pe_did, 1)
                did(nc.vector.tensor_copy(rows_sb[:].rearrange("a n p -> a (n p)"), row_ps[:]))
                for n in (1, 3):
                    last = nc.vector.tensor_scalar(rows_sb[:, n, :], rows_sb[:, n, :], -BIG, None, ALU.mult)
                did(last)
                nc.vector.memset(carry[:], -BIG)
                did(nc.vector.tensor_copy(ends[:, 0:1], ends[:, 0:1]))
                did(nc.vector.tensor_tensor_scan(carry[:, 0, 1:], rows_sb[:, 1, 0:P - 1], rows_sb[:, 0, 0:P - 1], -BIG,
                                                 ALU.add, ALU.max))
                did(nc.vector.tensor_tensor_scan(carry[:, 1, P - 2::-1], rows_sb[:, 3, P - 1:0:-1], rows_sb[:, 2, P - 1:0:-1],
                                                 -BIG, ALU.add, ALU.max))
                dve.wait_ge(pe_did, 2)
                did(nc.vector.tensor_copy(carry_c[:], col_ps[:]))
                did(nc.vector.tensor_tensor_scan(fwd[:], brk[:, 0:CHUNK], s[:], carry_c[:, 0:1], ALU.add, ALU.max))
                did(nc.vector.tensor_tensor_scan(bwd[:, ::-1], brk[:, CHUNK:0:-1], s[:, ::-1], carry_c[:, 1:2], ALU.add, ALU.max))
                did(nc.vector.tensor_tensor(fwd[:], fwd[:], bwd[:], ALU.max))
                did(nc.vector.tensor_tensor(s[:], s[:], fwd[:], ALU.subtract))
                assert done[0] == SM_DVE

            @block.tensor
            def _(pe):
                pe.wait_ge(dve_did, 5)
                for n in range(4):
                    last = nc.tensor.transpose(row_ps[:, n * P:(n + 1) * P], ends[:, n:n + 1], ident[:])
                last.then_inc(pe_did, 1)
                pe.wait_ge(dve_did, 10)
                for n in range(2):
                    last = nc.tensor.matmul(col_ps[:, n:n + 1], carry[:, n, :], ones[0:1, 0:1], start=True, stop=True)
                last.then_inc(pe_did, 1)

            @block.scalar
            def _(act):
                act.wait_ge(dve_did, SM_DVE)
                nc.scalar.activation(s[:], s[:], ACT.Exp, scale=ATT_SCALE).then_inc(exp_ok, 1)


SM_DVE = 15


def edge_sum(nc, sb, ps, sem, name, table, sums_d, width, probs_d, iota_n, ident, dloc, norm_s, keep,
             row_i, store_i, ends_i, idx_now):
    idx_ld = [sem(f"{name}_idx{h}") for h in range(2)]
    got = [sem(f"{name}_got{b}") for b in range(UNROLL)]
    att = probs_d is not None
    summed = sem(f"{name}_sum")
    used = sem(f"{name}_used") if att else summed
    credit = 4 if att else UNROLL
    turn = sem(f"{name}_turn")
    hot_ok, acc_ok, acc_free, acc_st = (sem(f"{name}_{n}") for n in ("hot", "acc", "accf", "accs"))
    den_ok, p_ld, p_tr, p_ok = (sem(f"{name}_{n}") for n in ("den", "pld", "ptr", "pok"))
    with ExitStack() as ctx:
        rows = sb(ctx, f"{name}_rows", [P, UNROLL, FEAT])
        hot = sb(ctx, f"{name}_hot", [P, 4, P])
        acc = sb(ctx, f"{name}_acc", [P, ACC_RING, width])
        if att:
            probs = sb(ctx, "probs", [P, (STEPS + UNROLL) * HEADS])
            probs_t = sb(ctx, "probs_t", [P, P])
            val = sb(ctx, "val", [P, 4, AGGW])
        sum_ps = [ps(ctx, f"{name}_ps{i}", [P, width]) for i in range(4)]
        turn_ps = ps(ctx, f"{name}_tps", [P, P])

        with nc.Block() as block:
            @block.sync
            def _(sp):

                sp.sem_inc(acc_free, ACC_RING)

                def store_ended(t0, b):
                    code = sp.value_load(store_i[0:1, bass.ds(t0 + b, 1)], min_val=0, max_val=NOT_LAST + NODE_TILES)
                    sp.wait_ge(acc_ok, t0 + (b + 2))
                    sp.sem_inc(turn, 1)
                    with sp.If(code < NODE_TILES):
                        tile = nc.s_assert_within(
                            code, 0, NODE_TILES - 1,
                            skip_runtime_bounds_check_because="this branch is taken only for codes below NODE_TILES")
                        sp.dma_start(sums_d[bass.ds(tile * P, P), :], acc[:, b % ACC_RING, :]).then_inc(acc_st, 16)
                        sp.wait_ge(acc_st, tile * 16 + 16)
                        sp.sem_inc(turn, 1)
                    sp.sem_inc(acc_free, 1)

                with sp.Fori(0, ROUNDS) as round_no:
                    t0 = sp.snap(round_no * UNROLL)
                    for b in range(0, UNROLL, QUAD):
                        any_ends = sp.value_load(ends_i[0:1, bass.ds(round_no * (UNROLL // QUAD) + b // QUAD, 1)],
                                                 min_val=0, max_val=1)
                        with sp.If(any_ends > 0):
                            for q in range(QUAD):
                                store_ended(t0, b + q)
                        with sp.Else():
                            sp.wait_ge(acc_ok, t0 + (b + QUAD + 1))
                            sp.sem_inc(acc_free, QUAD)
                sp.wait_ge(acc_st, 16 * NODE_TILES)

            @block.gpsimd
            def _(pool):
                with pool.Fori(0, ROUNDS) as round_no:
                    t0 = pool.snap(round_no * UNROLL)
                    for b in range(UNROLL):
                        gather_rows(nc, pool, t0, b, rows, table, idx_now, got, used, idx_ld, turn)

            @block.scalar
            def _(act):
                for h in range(2):
                    load_indices(act, idx_now, row_i, slice(h * HALF, (h + 1) * HALF), h, idx_ld)

                def load_numerators(row):
                    act.dma_start(probs_t[:], probs_d[row, :]).then_inc(p_ld, 16)

                def copy_numerators(n, columns):
                    act.wait_ge(p_tr, n + 1)
                    nc.scalar.copy(probs[:, columns], turn_ps[:]).then_inc(p_ok, 1)

                if att:
                    load_numerators(slice(0, P))
                    copy_numerators(0, slice(0, P))
                    load_numerators(slice(P, 2 * P))

                def numerators(t0, b):
                    act.wait_ge(summed, t0 + (b + 1))
                    nc.scalar.copy(val[:, b % 4, FEAT:], probs[:, bass.ds((t0 + b) * HEADS, HEADS)]).then_inc(den_ok, 1)

                with act.Fori(0, ROUNDS - 1) as round_no:
                    t0 = act.snap(round_no * UNROLL)
                    for h in range(2):
                        if att:
                            if h == 0:
                                act.wait_ge(p_ok, round_no + 1)
                            else:
                                copy_numerators(round_no + 1, bass.ds(round_no * P + P, P))
                                load_numerators(bass.ds(round_no * P + 2 * P, P))
                            for b in range(h * HALF, (h + 1) * HALF):
                                numerators(t0, b)
                        next_indices(act, idx_now, row_i, t0, h, got, idx_ld)
                if att:
                    act.wait_ge(p_ok, ROUNDS)
                    for b in range(UNROLL):
                        numerators(STEPS - UNROLL, b)

            @block.tensor
            def _(pe):
                def turn_numerators(n):
                    pe.wait_ge(p_ld, (n + 1) * 16)
                    nc.tensor.transpose(turn_ps[:], probs_t[:], ident[:]).then_inc(p_tr, 1)

                if att:
                    turn_numerators(0)
                pe.sem_inc(summed, credit)
                with pe.Fori(0, ROUNDS) as round_no:
                    t0 = pe.snap(round_no * UNROLL)
                    for b in range(UNROLL):
                        if att and b == 2:
                            pe.wait_ge(p_ok, round_no + 1)
                            turn_numerators(round_no + 1)
                        pe.wait_ge(hot_ok, t0 + (b + 1))
                        if b >= 4:
                            pe.wait_ge(acc_ok, t0 + (b - 2))
                        if att:
                            pe.wait_ge(used, t0 + (b + 1 + UNROLL))
                            pe.wait_ge(den_ok, t0 + (b + 1))
                            moving = val[:, b % 4, :]
                        else:
                            pe.wait_ge(got[b], t0 + 16)
                            moving = rows[:, b, :]
                        nc.tensor.matmul(sum_ps[b % 4][:], hot[:, b % 4, :], moving, start=True, stop=True).then_inc(summed, 1)

            @block.vector
            def _(dve):
                if att:
                    dve.sem_inc(used, UNROLL)
                nc.vector.memset(acc[:], 0.0).then_inc(acc_ok, 1)

                def feed(t0, b):
                    column = dloc[:, bass.ds(t0 + b, 1)]
                    dve.wait_ge(summed, t0 + (b - 3 + credit))
                    if att:
                        nc.vector.tensor_scalar(hot[:, b % 4, :], iota_n[:], column, None, ALU.is_equal).then_inc(hot_ok, 1)
                        dve.wait_ge(got[b], t0 + 16)
                        weights = probs[:, bass.ds((t0 + b) * HEADS, HEADS)]
                        nc.vector.tensor_tensor(val[:, b % 4, 0:FEAT].rearrange("p (h d) -> p h d", h=HEADS),
                                                rows[:, b, :].rearrange("p (h d) -> p h d", h=HEADS),
                                                weights.rearrange("p (h o) -> p h o", o=1).to_broadcast([P, HEADS, HEAD_DIM]),
                                                ALU.mult).then_inc(used, 1)
                    else:
                        nc.vector.tensor_scalar(hot[:, b % 4, :], iota_n[:], column, norm_s[:, bass.ds(t0 + b, 1)],
                                                ALU.is_equal, ALU.mult).then_inc(hot_ok, 1)

                def accumulate(t0, b):
                    dve.wait_ge(summed, t0 + (b + 1 + credit))
                    dve.wait_ge(acc_free, t0 + (b + 1))
                    dve.wait_ge(acc_ok, t0 + (b + 1))
                    nc.vector.scalar_tensor_tensor(out=acc[:, b % ACC_RING, :], in0=acc[:, (b - 1) % ACC_RING, :],
                                                   scalar=keep[:, bass.ds(t0 + b, 1)], in1=sum_ps[b % 4][:],
                                                   op0=ALU.mult, op1=ALU.add).then_inc(acc_ok, 1)

                with dve.Fori(0, ROUNDS) as round_no:
                    t0 = dve.snap(round_no * UNROLL)
                    if att:
                        dve.wait_ge(p_ok, round_no + 1)
                    for b in range(UNROLL):
                        feed(t0, b)
                        if b >= 2:
                            accumulate(t0, b - 2)
                    accumulate(t0, UNROLL - 2)
                    accumulate(t0, UNROLL - 1)


def node_update(nc, sb, ps, sem, x, g_res, b_res, w_in, b_in, w_out, b_out, w_rel, w_gate, ident,
                neg_half, h0_d, agg_d, x1_d, msg_d):
    w_ld, in_ld = sem("up_w"), sem("up_in")
    own = sem("up_own")
    stat, rstd_ok = [sem(f"up_stat{i}") for i in range(2)], [sem(f"up_rstd{i}") for i in range(2)]
    yn_ok, tr_ok, yt_ok = sem("up_yn"), sem("up_tr"), sem("up_yt")
    hid_mm, hid_ok, out_mm, x1_ok, x1_st = (sem(f"up_{n}") for n in ("hmm", "hid", "omm", "x1", "x1s"))
    h1_ok, h1t_ok, gate_mm, gate_ok = (sem(f"up_{n}") for n in ("h1", "h1t", "gmm", "gate"))
    msg_mm, ev_act, ev_dve = (sem(f"up_{n}") for n in ("msg", "eva", "evd"))
    msg_st = [sem(f"up_mst{i}") for i in range(2)]
    NC_ = GROUP * P
    HN = NC_ // 2
    with ExitStack() as ctx:
        win = sb(ctx, "win", [P, KC, DFF])
        wout = sb(ctx, "wout", [P, FFC, FEAT])
        wrel = sb(ctx, "wrel", [P, KC, RELS, FEAT])
        wgate = sb(ctx, "wgate", [P, KC, RELS])
        bin_c = sb(ctx, "bin_c", [P, FFC])
        bout = sb(ctx, "bout", [P, FEAT])
        gb = sb(ctx, "res_gb", [P, 2, KC])
        h1 = sb(ctx, "up_h1", [P, GROUP, FEAT])
        agg = sb(ctx, "up_agg", [P, GROUP, AGGW])
        h0 = sb(ctx, "up_h0", [P, GROUP, FEAT])
        xg = sb(ctx, "up_x", [P, GROUP, FEAT])
        den = sb(ctx, "up_den", [P, GROUP, HEADS])
        x2 = sb(ctx, "up_x2", [P, GROUP, FEAT])
        res = sb(ctx, "up_res", [P, 2, GROUP, FEAT])
        yT = sb(ctx, "up_yT", [P, KC, NC_])
        hid = sb(ctx, "up_hid", [P, FFC, NC_])
        x1 = sb(ctx, "up_x1", [P, GROUP, FEAT])
        h1T = sb(ctx, "up_h1T", [P, KC, NC_])
        gate = sb(ctx, "up_gate", [P, GROUP, RELS])
        msg = sb(ctx, "up_msg", [P, 2, RELS * FEAT])
        st6 = sb(ctx, "up_st6", [P, 2, GROUP, 6])
        mv = sb(ctx, "up_mv", [P, 2, GROUP, 2])
        veps = sb(ctx, "up_veps", [P, 2, GROUP])
        rstd = sb(ctx, "up_rstd_t", [P, 2, GROUP])
        tr_ps = [ps(ctx, f"up_tr{i}", [P, KC, P]) for i in range(2)]
        gate_ps = tr_ps[0][:].rearrange("p k n -> p (k n)")[:, 0:GROUP * RELS]
        mm_ps = [ps(ctx, f"up_mm{i}", [P, 512]) for i in range(6)]
        rows = lambda d: d.rearrange("(g t p) f -> g p t f", t=GROUP, p=P)

        def tr_of_x2(g):
            return 0 if g == 0 else GROUP * (2 * g - 1)

        def tr_of_h1(g):
            return GROUP * (2 * g + 2) if g < GROUPS - 1 else GROUP * (2 * g + 1)

        with nc.Block() as block:
            @block.sync
            def _(sp):
                sp.dma_start(win[:], w_in.rearrange("(k p) n -> p k n", p=P)).then_inc(w_ld, 16)
                sp.dma_start(wout[:], w_out.rearrange("(k p) n -> p k n", p=P)).then_inc(w_ld, 16)
                for k in range(KC):
                    sp.dma_start(wrel[:, k], w_rel.rearrange("r (k p) n -> k p r n", p=P)[k]).then_inc(w_ld, 16)
                sp.dma_start(bout[:], b_out.rearrange("(a n) -> a n", a=1).to_broadcast([P, FEAT])).then_inc(w_ld, 16)
                with nc.allow_non_contiguous_dma("small columns of parameters"):
                    for k in range(KC):
                        sp.dma_start(wgate[:, k], w_gate.rearrange("r (k p) a -> k p (r a)", p=P)[k]).then_inc(w_ld, 16)
                    sp.dma_start(bin_c[:], b_in.rearrange("(k p) -> p k", p=P)).then_inc(w_ld, 16)
                    sp.dma_start(gb[:, 0], g_res.rearrange("(k p) -> p k", p=P)).then_inc(w_ld, 16)
                    sp.dma_start(gb[:, 1], b_res.rearrange("(k p) -> p k", p=P)).then_inc(w_ld, 16)
                def load(g):
                    if g >= 1:
                        sp.wait_ge(yn_ok, GROUP * g)
                    sp.dma_start(agg[:], rows(agg_d)[g]).then_inc(in_ld, 16)
                    sp.dma_start(h0[:], rows(h0_d)[g]).then_inc(in_ld, 16)
                    sp.dma_start(xg[:], rows(x)[g]).then_inc(in_ld, 16)

                def store_x1(g):
                    sp.wait_ge(x1_ok, GROUP * (g + 1))
                    sp.dma_start(rows(x1_d)[g], x1[:]).then_inc(x1_st, 16)

                load(0)
                load(1)
                store_x1(0)
                for g in range(GROUPS):
                    if g + 2 < GROUPS:
                        load(g + 2)
                    if g + 1 < GROUPS:
                        store_x1(g + 1)
                    for t in range(GROUP):
                        n_t = GROUP * g + t
                        sp.wait_ge(ev_act, PAIRS * (n_t + 1))
                        sp.wait_ge(ev_dve, (PAIRS // 2) * (n_t + 1))
                        sp.dma_start(msg_d[n_t * P * RELS:(n_t + 1) * P * RELS, :].rearrange("(p r) f -> p (r f)", r=RELS),
                                     msg[:, n_t % 2, :]).then_inc(msg_st[n_t % 2], 16)
                sp.wait_ge(x1_st, 16 * GROUPS)
                for n in range(2):
                    sp.wait_ge(msg_st[n], 16 * ((NODE_TILES + 1 - n) // 2))

            @block.vector
            def _(dve):
                n = [0]

                def own_wait(ins):
                    n[0] += 1
                    ins.then_inc(own, 1)
                    dve.wait_ge(own, n[0])

                def x2_tile(g, t):
                    if t == 0:
                        dve.wait_ge(in_ld, 48 * (g + 1))
                        own_wait(nc.vector.tensor_scalar(den[:], agg[:, :, FEAT:], 1e-30, None, ALU.max))
                        own_wait(nc.vector.reciprocal(den[:], den[:]))
                        if g >= 1:
                            dve.wait_ge(tr_ok, tr_of_x2(g - 1) + GROUP)
                    nc.vector.tensor_tensor(res[:, g % 2, t, :], xg[:, t, :], bout[:], ALU.add)
                    own_wait(nc.vector.tensor_tensor(x2[:, t, :].rearrange("p (h d) -> p h d", h=HEADS),
                                                     agg[:, t, 0:FEAT].rearrange("p (h d) -> p h d", h=HEADS),
                                                     den[:, t, :].rearrange("p (h o) -> p h o", o=1).to_broadcast([P, HEADS, HEAD_DIM]),
                                                     ALU.mult))
                    own_wait(nc.vector.tensor_tensor(x2[:, t, :], x2[:, t, :], h0[:, t, :], ALU.add))
                    nc.vector.bn_stats(st6[:, 0, t, :], x2[:, t, :])
                    own_wait(nc.vector.tensor_tensor(res[:, g % 2, t, :], res[:, g % 2, t, :], x2[:, t, :], ALU.add))

                def variance(which):
                    for t in range(GROUP):
                        last = nc.vector.bn_aggr(mv[:, which, t, :], st6[:, which, t, :])
                    own_wait(last)
                    nc.vector.tensor_scalar(veps[:, which, :], mv[:, which, :, 1], EPS, None, ALU.add).then_inc(stat[which], 1)

                def normalise(g, which, src_t, dst_t, ok):
                    dve.wait_ge(rstd_ok[which], g + 1)
                    for t in range(GROUP):
                        nc.vector.tensor_scalar(dst_t[:, t, :], src_t[:, t, :], mv[:, which, t, 0:1], rstd[:, which, t:t + 1],
                                                ALU.subtract, ALU.mult).then_inc(ok, 1)

                def x1_tiles(g):
                    if g >= 1:
                        dve.wait_ge(x1_st, 16 * g)
                    for t in range(GROUP):
                        dve.wait_ge(out_mm, GROUP * g + t + 1)
                        nc.vector.tensor_tensor(x1[:, t, :], mm_ps[t % 6][:, 0:FEAT], res[:, g % 2, t, :], ALU.add).then_inc(x1_ok, 1)
                        dve.wait_ge(x1_ok, GROUP * g + t + 1)
                        last = nc.vector.bn_stats(st6[:, 1, t, :], x1[:, t, :])
                    own_wait(last)
                    variance(1)

                dve.wait_ge(w_ld, 16 * 10)
                for t in range(GROUP):
                    x2_tile(0, t)
                variance(0)
                normalise(0, 0, x2, x2, yn_ok)
                for t in range(GROUP):
                    x2_tile(1, t)
                variance(0)
                x1_tiles(0)
                for g in range(GROUPS):
                    normalise(g, 1, x1, h1, h1_ok)
                    if g + 1 < GROUPS:
                        normalise(g + 1, 0, x2, x2, yn_ok)
                        x1_tiles(g + 1)
                    dve.wait_ge(gate_ok, g + 1)
                    for t in range(GROUP):
                        n_t = GROUP * g + t
                        if n_t >= 2:
                            dve.wait_ge(msg_st[n_t % 2], 16 * (n_t // 2))
                        for c in range(0, PAIRS, 2):
                            dve.wait_ge(msg_mm, PAIRS * n_t + c + 1)
                            nc.vector.tensor_tensor(
                                msg[:, n_t % 2, c * 512:(c + 1) * 512].rearrange("p (r f) -> p r f", r=2),
                                mm_ps[(PAIRS * n_t + c) % 6][:].rearrange("p (r f) -> p r f", r=2),
                                gate[:, t, 2 * c:2 * c + 2].rearrange("p (r o) -> p r o", o=1).to_broadcast([P, 2, FEAT]),
                                ALU.mult).then_inc(ev_dve, 1)
                        if g + 2 < GROUPS:
                            x2_tile(g + 2, t)
                    if g + 2 < GROUPS:
                        variance(0)

            @block.gpsimd
            def _(pool):
                def power(g, which):
                    pool.wait_ge(stat[which], g + 1)
                    nc.gpsimd.tensor_tensor(rstd[:, which, :], veps[:, which, :], neg_half[:], ALU.pow).then_inc(rstd_ok[which], 1)

                power(0, 0)
                for g in range(GROUPS):
                    if g + 1 < GROUPS:
                        power(g + 1, 0)
                    power(g, 1)

            @block.scalar
            def _(act):
                act.wait_ge(w_ld, 16 * 10)

                def mlp(g):
                    for t in range(GROUP):
                        act.wait_ge(tr_ok, tr_of_x2(g) + t + 1)
                        for k in range(KC):
                            last = nc.scalar.activation(yT[:, k, t * P:(t + 1) * P], tr_ps[t % 2][:, k, :], ACT.Identity,
                                                        scale=gb[:, 0, k:k + 1], bias=gb[:, 1, k:k + 1])
                        last.then_inc(yt_ok, 1)
                    for m in range(2 * FFC):
                        act.wait_ge(hid_mm, 2 * FFC * g + m + 1)
                        nc.scalar.activation(hid[:, m // 2, (m % 2) * HN:(m % 2 + 1) * HN], mm_ps[m % 6][:, 0:HN], ACT.Gelu,
                                             bias=bin_c[:, m // 2:m // 2 + 1]).then_inc(hid_ok, 1)

                mlp(0)
                for g in range(GROUPS):
                    if g + 1 < GROUPS:
                        mlp(g + 1)
                    for t in range(GROUP):
                        act.wait_ge(tr_ok, tr_of_h1(g) + t + 1)
                        nc.scalar.activation(h1T[:, :, t * P:(t + 1) * P], tr_ps[(t + 1) % 2][:], ACT.Relu).then_inc(h1t_ok, 1)
                    act.wait_ge(gate_mm, g + 1)
                    if g >= 1:
                        act.wait_ge(ev_dve, (PAIRS // 2) * GROUP * g)
                        act.wait_ge(ev_act, PAIRS * GROUP * g)
                    nc.scalar.activation(gate[:].rearrange("p t r -> p (t r)"), gate_ps, ACT.Sigmoid).then_inc(gate_ok, 1)
                    act.wait_ge(gate_ok, g + 1)
                    for t in range(GROUP):
                        n_t = GROUP * g + t
                        if n_t >= 2:
                            act.wait_ge(msg_st[n_t % 2], 16 * (n_t // 2))
                        for c in range(1, PAIRS, 2):
                            act.wait_ge(msg_mm, PAIRS * n_t + c + 1)
                            for r in range(2):
                                nc.scalar.mul(msg[:, n_t % 2, c * 512 + r * FEAT:c * 512 + (r + 1) * FEAT],
                                              mm_ps[(PAIRS * n_t + c) % 6][:, r * FEAT:(r + 1) * FEAT],
                                              gate[:, t, 2 * c + r:2 * c + r + 1]).then_inc(ev_act, 1)

            @block.tensor
            def _(pe):
                pe.wait_ge(w_ld, 16 * 10)

                def mlp(g):
                    for t in range(GROUP):
                        pe.wait_ge(yn_ok, GROUP * g + t + 1)
                        if t >= 2:
                            pe.wait_ge(yt_ok, GROUP * g + t - 1)
                        elif g >= 2:
                            pe.wait_ge(gate_ok, g - 1)
                        elif g == 1:
                            pe.wait_ge(yt_ok, GROUP)
                        for k in range(KC):
                            last = nc.tensor.transpose(tr_ps[t % 2][:, k, :], x2[:, t, k * P:(k + 1) * P], ident[:])
                        last.then_inc(tr_ok, 1)
                    if g >= 2:
                        pe.wait_ge(ev_act, PAIRS * GROUP * (g - 1))
                        pe.wait_ge(ev_dve, (PAIRS // 2) * GROUP * (g - 1))
                    elif g == 1:
                        pe.wait_ge(x1_ok, GROUP)
                    pe.wait_ge(yt_ok, GROUP * (g + 1))
                    for m in range(2 * FFC):
                        if m >= 6:
                            pe.wait_ge(hid_ok, 2 * FFC * g + m - 5)
                        for k in range(KC):
                            last = nc.tensor.matmul(mm_ps[m % 6][:, 0:HN], win[:, k, (m // 2) * P:(m // 2 + 1) * P],
                                                    yT[:, k, (m % 2) * HN:(m % 2 + 1) * HN], start=(k == 0), stop=(k == KC - 1))
                        last.then_inc(hid_mm, 1)
                    pe.wait_ge(hid_ok, 2 * FFC * (g + 1))
                    for t in range(GROUP):
                        if t >= 6:
                            pe.wait_ge(x1_ok, GROUP * g + t - 5)
                        for m in range(FFC):
                            last = nc.tensor.matmul(mm_ps[t % 6][:, 0:FEAT], hid[:, m, t * P:(t + 1) * P], wout[:, m, :],
                                                    start=(m == 0), stop=(m == FFC - 1))
                        last.then_inc(out_mm, 1)

                mlp(0)
                for g in range(GROUPS):
                    if g + 1 < GROUPS:
                        mlp(g + 1)
                    for t in range(GROUP):
                        pe.wait_ge(h1_ok, GROUP * g + t + 1)
                        if t >= 2:
                            pe.wait_ge(h1t_ok, GROUP * g + t - 1)
                        for k in range(KC):
                            last = nc.tensor.transpose(tr_ps[(t + 1) % 2][:, k, :], h1[:, t, k * P:(k + 1) * P], ident[:])
                        last.then_inc(tr_ok, 1)
                    pe.wait_ge(h1t_ok, GROUP * (g + 1))
                    for t in range(GROUP):
                        for k in range(KC):
                            last = nc.tensor.matmul(gate_ps[:, t * RELS:(t + 1) * RELS], h1T[:, k, t * P:(t + 1) * P], wgate[:, k, :],
                                                    start=(k == 0), stop=(k == KC - 1))
                    last.then_inc(gate_mm, 1)
                    for t in range(GROUP):
                        n_t = GROUP * g + t
                        for c in range(PAIRS):
                            m = PAIRS * n_t + c
                            if c >= 6 or t >= 1 or g == GROUPS - 1:
                                old = m - 6
                                if old % 2 == 0:
                                    pe.wait_ge(ev_dve, old // 2 + 1)
                                else:
                                    pe.wait_ge(ev_act, old + 1)
                            else:
                                pe.wait_ge(x1_ok, GROUP * min(g + 2, GROUPS))
                            for k in range(KC):
                                last = nc.tensor.matmul(mm_ps[m % 6][:], h1T[:, k, t * P:(t + 1) * P],
                                                        wrel[:, k, 2 * c:2 * c + 2, :].rearrange("p r f -> p (r f)"),
                                                        start=(k == 0), stop=(k == KC - 1))
                            last.then_inc(msg_mm, 1)


def finish(nc, sb, sem, x1_d, agg1_d, out):
    ld, dve_did, st = [sem(f"fin_ld{i}") for i in range(2)], sem("fin_dve"), sem("fin_st")
    with ExitStack() as ctx:
        a = sb(ctx, "fin_a", [P, GROUPS, GROUP, FEAT])
        b = sb(ctx, "fin_b", [P, 2, GROUP, FEAT])
        rows = lambda d: d.rearrange("(g t p) f -> g p t f", t=GROUP, p=P)
        with nc.Block() as block:
            @block.sync
            def _(sp):
                def load(g):
                    sp.dma_start(a[:, g], rows(x1_d)[g]).then_inc(ld[g % 2], 16)
                    sp.dma_start(b[:, g % 2], rows(agg1_d)[g]).then_inc(ld[g % 2], 16)

                def store(g):
                    sp.wait_ge(dve_did, g + 1)
                    last = g == GROUPS - 1
                    tiles = GROUP - 1 if last else GROUP
                    r0 = g * GROUP * P
                    sp.dma_start(out[r0:r0 + tiles * P, :].rearrange("(t p) f -> p t f", p=P), a[:, g, 0:tiles]).then_inc(st, 16)
                    if last:
                        sp.dma_start(out[NODES - LAST_ROWS:, :], a[0:LAST_ROWS, g, tiles]).then_inc(st, 16)

                load(0)
                load(1)
                for g in range(GROUPS):
                    store(g)
                    if g + 2 < GROUPS:
                        load(g + 2)
                sp.wait_ge(st, 16 * (GROUPS + 1))

            @block.vector
            def _(dve):
                for g in range(GROUPS):
                    dve.wait_ge(ld[g % 2], 32 * (g // 2 + 1))
                    nc.vector.scalar_tensor_tensor(out=a[:, g], in0=b[:, g % 2], scalar=0.0, in1=a[:, g],
                                                   op0=ALU.max, op1=ALU.add).then_inc(dve_did, 1)


_OUT = ((NODES, FEAT), "float32")
_NAMES = ["x", "src", "dst", "edge_type_16", "edge_weight1", "L0_gnn_Wqkv", "L0_gnn_bqkv", "L0_gnn_ln_attn_g",
          "L0_gnn_ln_attn_b", "L0_gnn_ln_res_g", "L0_gnn_ln_res_b", "L0_gnn_W_in", "L0_gnn_b_in", "L0_gnn_W_out",
          "L0_gnn_b_out", "L1_gnn_weight", "L1_gnn_gate_weight"]


def kernel(**inputs):
    import numpy as _np
    import concourse.bacc as _bacc
    from concourse import mybir as _mybir
    from concourse.bass_utils import run_bass_kernel_spmd as _run

    nc = _bacc.Bacc("TRN2", target_bir_lowering=False, num_devices=1)
    arrays, args = {}, []
    for name in _NAMES:
        a = _np.asarray(inputs[name])
        if name == "x":
            a = _np.pad(a, ((0, NODES_PAD - NODES), (0, 0)))
        if name in ("src", "edge_type_16"):
            a = _np.pad(a, (0, EDGES_PAD - EDGES))
        if name == "dst":
            a = _np.pad(a, (0, EDGES_PAD - EDGES), constant_values=DST_PAD)
        if name == "edge_weight1":
            a = _np.pad(a.reshape(EDGES), (0, EDGES_PAD - EDGES))
        a = _np.ascontiguousarray(a)
        arrays[f"in_{name}_dram"] = a
        args.append(nc.dram_tensor(f"in_{name}_dram", a.shape, _mybir.dt.from_np(a.dtype), kind="ExternalInput").ap())
    args.append(nc.dram_tensor("out_0_dram", _OUT[0], _mybir.dt.from_np(_np.dtype(_OUT[1])), kind="ExternalOutput").ap())
    gnn_program(nc, *args)
    r = _run(nc, [arrays], core_ids=[0])
    return r.results[0]["out_0_dram"]
```

```python
from contextlib import ExitStack

import concourse.bass as bass
from concourse import mybir

F32 = mybir.dt.float32
F32R = mybir.dt.float32r
BF16 = mybir.dt.bfloat16
I32 = mybir.dt.int32
ALU = mybir.AluOpType
ACT = mybir.ActivationFunctionType
AX_X = mybir.AxisListType.X

P = 128
NODES, FEAT = 6250, 256
EDGES = 100000
HEADS = 8
HEAD_DIM = FEAT // HEADS
DFF = 4 * FEAT
RELS = 16
EPS = 1e-5
ATT_SCALE = float(FEAT) ** -0.5
KC = FEAT // P
FFC = DFF // P

NODE_TILES = -(-NODES // P)
NODES_PAD = NODE_TILES * P
LAST_ROWS = NODES - (NODE_TILES - 1) * P
GROUP = 7
GROUPS = NODE_TILES // GROUP
EDGE_TILES = -(-EDGES // P)
IC = 112
ICN = 7
EDGE_TILES_PAD = IC * ICN
EDGES_PAD = EDGE_TILES_PAD * P
UNROLL = 16
AHEAD = 6
HALF = UNROLL // 2
STEPS = 832
assert EDGE_TILES + NODE_TILES - 1 <= STEPS and STEPS % UNROLL == 0
ROUNDS = STEPS // UNROLL
SH = STEPS // 2
DST_PAD = 6400
NOT_LAST = 4096
QUAD = 4
CHUNKS = P // HEADS
CHUNK_STEPS = STEPS // CHUNKS
CHUNK = CHUNK_STEPS * P
BIG = 1.0e30
AGGW = FEAT + HEADS
ACC_RING = 8
PAIRS = RELS // 2
MSG_WC = 8


def gnn_program(nc, x, src, dst, rel, norm, wqkv, bqkv, g_attn, b_attn, g_res, b_res,
                w_in, b_in, w_out, b_out, w_rel, w_gate, out):
    def dram(name, shape, dt=F32):
        return nc.dram_tensor(name, shape, dt, kind="Internal").ap()

    h0_d = dram("h0_d", [NODES_PAD, FEAT])
    q_d = dram("q_d", [NODES_PAD, FEAT])
    v_d = dram("v_d", [NODES_PAD, FEAT])
    x1_d = dram("x1_d", [NODES_PAD, FEAT])
    h1_d = dram("h1_d", [NODES_PAD, FEAT])
    msg_d = dram("msg_d", [NODES_PAD * RELS, FEAT])
    agg_d = dram("agg_d", [NODES_PAD, AGGW])
    scores_d = dram("scores_d", [HEADS, HALF + STEPS, P])
    probs_d = dram("probs_d", [HEADS, STEPS + UNROLL, P])
    key_d = dram("key_d", [STEPS * P + 2 * P])

    with ExitStack() as whole:
        def sb(ctx, name, shape, dt=F32):
            return ctx.enter_context(nc.sbuf_tensor(name, shape, dt))

        def ps(ctx, name, shape, dt=F32):
            return ctx.enter_context(nc.psum_tensor(name, shape, dt))

        def sem(name):
            return whole.enter_context(nc.semaphore(name))

        iota_n = sb(whole, "iota_n", [P, P])
        ident = sb(whole, "ident", [P, P])
        ident_b = sb(whole, "ident_b", [P, P], BF16)
        part = sb(whole, "part", [P, 1])
        ones = sb(whole, "ones", [P, P])
        neg_half = sb(whole, "neg_half", [P, GROUP])
        dloc = sb(whole, "dloc", [P, STEPS + AHEAD])
        keep = sb(whole, "keep", [P, STEPS])
        norm_s = sb(whole, "norm_s", [P, STEPS])
        src_i = sb(whole, "src_i", [P, STEPS], I32)
        msg_i = sb(whole, "msg_i", [P, STEPS], I32)
        tile_i = sb(whole, "tile_i", [P, STEPS], I32)
        ends_i = sb(whole, "ends_i", [P, STEPS // QUAD], I32)
        store_i = sb(whole, "store_i", [P, STEPS], I32)
        idx_now = sb(whole, "idx_now", [P, 2, HALF], I32)

        got = [sem(f"got{b}") for b in range(UNROLL)]

        build_steps(nc, sb, ps, sem, src, dst, rel, norm, key_d, iota_n, ident, ident_b, part, ones,
                    neg_half, dloc, keep, norm_s, src_i, msg_i, tile_i, store_i, ends_i)
        with ExitStack() as soft:
            key = sb(soft, "sm_key", [P, CHUNK + 2])
            brk = sb(soft, "sm_brk", [P, CHUNK + 1], BF16)
            s_all = sb(soft, "sm_s", [P, CHUNK])
            with ExitStack() as att:
                k_all = sb(att, "k_all", [P, (NODE_TILES + 1) * FEAT])
                node_inputs(nc, sb, ps, sem, x, wqkv, bqkv, g_attn, b_attn, ident, neg_half,
                            h0_d, q_d, v_d, k_all, key_d, key, brk, s_all)
                edge_scores(nc, sb, ps, sem, q_d, scores_d, k_all, iota_n, ident, ident_b, dloc, src_i, tile_i,
                            idx_now, got, s_all)
            v_rows = sb(soft, "v_rows", [P, UNROLL, FEAT])
            v_idx_ld = [sem(f"att_idx{h}") for h in range(2)]
            softmax_numerators(nc, sb, ps, sem, scores_d, probs_d, key, brk, s_all, ident, ones,
                               v_d, v_rows, src_i, idx_now, got, v_idx_ld)
            edge_sum(nc, sb, ps, sem, "att", v_d, agg_d, AGGW, probs_d, iota_n, ident, dloc, None, keep,
                     src_i, store_i, ends_i, idx_now, got, 1, first_round=(v_rows, v_idx_ld))
        node_mlp(nc, sb, ps, sem, x, g_res, b_res, w_in, b_in, w_out, b_out, ident, neg_half,
                 h0_d, agg_d, x1_d, h1_d)
        messages(nc, sb, ps, sem, w_rel, w_gate, ident, h1_d, msg_d)
        with ExitStack() as last:
            x1_all = sb(last, "x1_all", [P, GROUPS, GROUP, FEAT])
            sums_all = sb(last, "sums_all", [P, NODE_TILES * FEAT])
            edge_sum(nc, sb, ps, sem, "rel", msg_d, sums_all, FEAT, None, iota_n, ident, dloc, norm_s, keep,
                     msg_i, store_i, ends_i, idx_now, got, 2, (x1_d, x1_all))
            finish(nc, sb, sem, x1_all, sums_all, out)


def build_steps(nc, sb, ps, sem, src, dst, rel, norm, key_d, iota_n, ident, ident_b, part, ones,
                neg_half, dloc, keep, norm_s, src_i, msg_i, tile_i, store_i, ends_i):
    loaded = sem("steps_loaded")
    consts = sem("consts_made")
    dve_did = sem("steps_dve")
    pe_did = sem("steps_pe")
    sel_free = sem("steps_sel_free")
    key_out = sem("key_out")
    split = sem("steps_split")
    with ExitStack() as ctx:
        cols_i = sb(ctx, "cols_i", [IC, 3, ICN, P], I32)
        cols = sb(ctx, "cols", [IC, 4, ICN, P])
        cols_cut = sb(ctx, "cols_cut", [IC, 4, ICN, P])
        cols_hi = sb(ctx, "cols_hi", [IC, 4, ICN, P], F32R)
        cols_lo = sb(ctx, "cols_lo", [IC, 4, ICN, P], F32R)
        last_i = sb(ctx, "last_i", [1, EDGE_TILES_PAD], I32)
        last_f = sb(ctx, "last_f", [1, EDGE_TILES_PAD])
        step_no = sb(ctx, "step_no", [P, STEPS])
        bound = sb(ctx, "bound", [P, 1])
        full = sb(ctx, "full", [P, 1])
        pos = sb(ctx, "pos", [P, 1])
        scratch = sb(ctx, "steps_scratch", [P, STEPS])
        before = sb(ctx, "before", [P, STEPS])
        node_tile = sb(ctx, "node_tile", [P, STEPS + QUAD])
        edge_tile = sb(ctx, "edge_tile", [P, STEPS])
        part_c = sb(ctx, "part_c", [P, ICN])
        sel = sb(ctx, "sel", [IC, 2, STEPS], F32R)
        src_f = sb(ctx, "src_f", [P, STEPS])
        valid = sb(ctx, "valid", [P, STEPS])
        key = sb(ctx, "key", [P, STEPS])
        key_t = sb(ctx, "key_t", [P, ICN, P])
        guard = sb(ctx, "guard", [1, 2 * P])
        pb = [ps(ctx, f"steps_ps{b}", [P, 512]) for b in range(8)]

        with nc.Block() as block:
            @block.sync
            def _(sp):
                for n, a in enumerate((src, dst, rel)):
                    sp.dma_start(cols_i[:, n], a.rearrange("(c i p) -> i c p", i=IC, p=P)).then_inc(loaded, 16)
                sp.dma_start(cols[:, 3], norm.rearrange("(c i p) -> i c p", i=IC, p=P)).then_inc(loaded, 16)
                with nc.allow_non_contiguous_dma("one dst of each edge tile"):
                    sp.dma_start(last_i[:], dst.rearrange("(a i p) -> a i p", a=1, p=P)[:, :, P - 1]).then_inc(loaded, 16)
                sp.wait_ge(dve_did, 30)
                kd = key_d[P:P + STEPS * P].rearrange("(s p) -> s p", p=P)
                for c in range(ICN):
                    n = min(P, STEPS - c * P)
                    sp.dma_start(kd[c * P:c * P + n, :], key_t[0:n, c, :]).then_inc(key_out, 16)
                gd = key_d[:].rearrange("(a n) -> a n", a=1)
                sp.dma_start(gd[:, 0:P], guard[:, 0:P]).then_inc(key_out, 16)
                sp.dma_start(gd[:, P + STEPS * P:], guard[:, P:]).then_inc(key_out, 16)
                sp.wait_ge(key_out, 16 * (ICN + 2))

            @block.gpsimd
            def _(pool):
                nc.gpsimd.iota(iota_n[:], [[1, P]], base=0, channel_multiplier=0,
                               allow_small_or_imprecise_dtypes=True).then_inc(consts, 1)
                nc.gpsimd.iota(step_no[:], [[1, STEPS]], base=0, channel_multiplier=0,
                               allow_small_or_imprecise_dtypes=True).then_inc(consts, 1)
                nc.gpsimd.iota(part[:], [[1, 1]], base=0, channel_multiplier=1,
                               allow_small_or_imprecise_dtypes=True).then_inc(consts, 1)
                nc.gpsimd.iota(bound[:], [[1, 1]], base=P, channel_multiplier=P,
                               allow_small_or_imprecise_dtypes=True).then_inc(consts, 1)
                nc.gpsimd.iota(part_c[:], [[IC, ICN]], base=0, channel_multiplier=1,
                               allow_small_or_imprecise_dtypes=True).then_inc(consts, 1)
                nc.gpsimd.memset(ones[:], 1.0).then_inc(consts, 1)
                nc.gpsimd.memset(neg_half[:], -0.5).then_inc(consts, 1)
                nc.gpsimd.memset(guard[:], -2.0).then_inc(consts, 1)

            @block.vector
            def _(dve):
                done = [0]

                def did(ins):
                    done[0] += 1
                    ins.then_inc(dve_did, 1)
                    dve.wait_ge(dve_did, done[0])
                    return done[0]

                dve.wait_ge(consts, 8)
                nc.vector.memset(dloc[:, STEPS:], -1.0)
                did(nc.vector.tensor_scalar(ident[:], iota_n[:], part[:], None, ALU.is_equal))
                did(nc.vector.tensor_copy(ident_b[:], ident[:]))
                dve.wait_ge(loaded, 80)
                did(nc.vector.tensor_copy(last_f[:], last_i[:]))
                did(nc.vector.tensor_copy(cols[:, 0:3], cols_i[:]))
                nc.vector.tensor_scalar(cols_cut[:].bitcast(I32), cols[:].bitcast(I32), -4096, None, ALU.bitwise_and).then_inc(split, 1)
                dve.wait_ge(split, 1)
                nc.vector.tensor_tensor(cols_lo[:], cols[:], cols_cut[:], ALU.subtract).then_inc(split, 1)
                n = EDGE_TILES_PAD // 2
                dve.wait_ge(pe_did, 2)
                did(nc.vector.tensor_scalar(scratch[:, 0:n], pb[0][:, 0:n], bound[:], 0.0, ALU.is_lt, ALU.add,
                                            accum_out=full[:]))
                did(nc.vector.tensor_scalar(scratch[:, 0:n], pb[1][:, 0:n], bound[:], full[:], ALU.is_lt, ALU.add,
                                            accum_out=pos[:]))
                did(nc.vector.tensor_tensor(pos[:], pos[:], part[:], ALU.add))
                did(nc.vector.tensor_scalar(before[:], step_no[:], pos[:], None, ALU.is_gt))
                dve.wait_ge(pe_did, 4)
                did(nc.vector.tensor_copy(node_tile[:, 0:SH], pb[2][:, 0:SH]))
                did(nc.vector.tensor_copy(node_tile[:, SH:STEPS], pb[3][:, 0:SH]))
                did(nc.vector.tensor_copy(node_tile[:, STEPS:], node_tile[:, STEPS - 1:STEPS].to_broadcast([P, QUAD])))
                did(nc.vector.tensor_tensor(edge_tile[:], step_no[:], node_tile[:, 0:STEPS], ALU.subtract))
                for c in range(ICN):
                    if c >= 2:
                        dve.wait_ge(sel_free, c - 1)
                    did(nc.vector.tensor_scalar(sel[:, c % 2], edge_tile[0:IC, :], part_c[0:IC, c:c + 1], None,
                                                ALU.is_equal))
                dve.wait_ge(pe_did, 5)
                for h in range(2):
                    a, b = h * SH, (h + 1) * SH
                    nc.vector.tensor_copy(src_f[:, a:b], pb[h][:, 0:SH])
                    nc.vector.tensor_copy(src_i[:, a:b], pb[h][:, 0:SH])
                    nc.vector.scalar_tensor_tensor(out=dloc[:, a:b], in0=node_tile[:, a:b], scalar=-float(P),
                                                   in1=pb[2 + h][:, 0:SH], op0=ALU.mult, op1=ALU.add)
                    nc.vector.tensor_copy(scratch[:, a:b], pb[4 + h][:, 0:SH])
                    did(nc.vector.tensor_copy(norm_s[:, a:b], pb[6 + h][:, 0:SH]))
                did(nc.vector.scalar_tensor_tensor(out=msg_i[:], in0=src_f[:], scalar=float(RELS), in1=scratch[:],
                                                   op0=ALU.mult, op1=ALU.add))
                nc.vector.tensor_copy(tile_i[:], node_tile[:, 0:STEPS])
                quad = node_tile[:].rearrange("p (n q) -> p n q", q=QUAD)
                nc.vector.tensor_tensor(ends_i[:], quad[:, 1:, 0], quad[:, 0:STEPS // QUAD, 0], ALU.not_equal)
                did(nc.vector.tensor_tensor(before[:], node_tile[:, 1:STEPS + 1], node_tile[:, 0:STEPS], ALU.is_equal))
                nc.vector.memset(keep[:, 0:1], 0.0)
                nc.vector.tensor_copy(keep[:, 1:], before[:, 0:STEPS - 1])
                did(nc.vector.scalar_tensor_tensor(out=store_i[:], in0=before[:], scalar=float(NOT_LAST),
                                                   in1=node_tile[:, 0:STEPS], op0=ALU.mult, op1=ALU.add))
                did(nc.vector.tensor_scalar(valid[:], dloc[:, 0:STEPS], 0.0, None, ALU.is_ge))
                did(nc.vector.scalar_tensor_tensor(out=valid[:], in0=dloc[:, 0:STEPS], scalar=float(P), in1=valid[:],
                                                   op0=ALU.is_lt, op1=ALU.mult))
                did(nc.vector.scalar_tensor_tensor(out=key[:], in0=node_tile[:, 0:STEPS], scalar=float(P), in1=dloc[:, 0:STEPS],
                                                   op0=ALU.mult, op1=ALU.add))
                did(nc.vector.scalar_tensor_tensor(out=key[:], in0=key[:], scalar=1.0, in1=valid[:],
                                                   op0=ALU.add, op1=ALU.mult))
                did(nc.vector.tensor_scalar(key[:], key[:], -1.0, None, ALU.add))
                dve.wait_ge(pe_did, 6)
                for c in range(ICN):
                    n = min(P, STEPS - c * P)
                    last = nc.vector.tensor_copy(key_t[0:n, c, :], pb[c // 4][0:n, (c % 4) * P:(c % 4 + 1) * P])
                did(last)

            @block.scalar
            def _(act):
                act.wait_ge(split, 1)
                nc.scalar.copy(cols_hi[:], cols_cut[:]).then_inc(split, 1)

            @block.tensor
            def _(pe):
                n = EDGE_TILES_PAD // 2
                pe.wait_ge(dve_did, 3)
                for h in range(2):
                    nc.tensor.matmul(pb[h][:, 0:n], ones[0:1, :], last_f[:, h * n:(h + 1) * n],
                                     start=True, stop=True).then_inc(pe_did, 1)
                pe.wait_ge(dve_did, 8)
                for h in range(2):
                    nc.tensor.matmul(pb[2 + h][:, 0:SH], ones[0:NODE_TILES, :], before[0:NODE_TILES, h * SH:(h + 1) * SH],
                                     start=True, stop=True).then_inc(pe_did, 1)
                pe.wait_ge(split, 3)
                for c in range(ICN):
                    pe.wait_ge(dve_did, 13 + c)
                    for n in range(4):
                        for h in range(2):
                            for part_of in (cols_hi, cols_lo):
                                mm = nc.tensor.matmul(pb[2 * n + h][:, 0:SH], part_of[:, n, c, :],
                                                      sel[:, c % 2, h * SH:(h + 1) * SH],
                                                      start=(c == 0 and part_of is cols_hi),
                                                      stop=(c == ICN - 1 and part_of is cols_lo))
                    mm.then_inc(sel_free, 1)
                pe.wait_ge(sel_free, ICN)
                pe.sem_inc(pe_did, 1)
                pe.wait_ge(dve_did, 29)
                for c in range(ICN):
                    n = min(P, STEPS - c * P)
                    tr = nc.tensor.transpose(pb[c // 4][0:n, (c % 4) * P:(c % 4 + 1) * P], key[:, c * P:c * P + n], ident[:])
                tr.then_inc(pe_did, 1)


def node_inputs(nc, sb, ps, sem, x, wqkv, bqkv, g_attn, b_attn, ident, neg_half, h0_d, q_d, v_d, k_all,
                key_d, key, brk, s_all):
    w_ld = sem("in_w")
    x_ld = [sem(f"in_x{i}") for i in range(2)]
    x_free = sem("in_x_free")
    stat = sem("in_stat")
    rstd_ok = sem("in_rstd")
    h0_ok = sem("in_h0")
    hn_ok = sem("in_hn")
    tr_ok = sem("in_tr")
    ht_ok = sem("in_ht")
    mm_ok = sem("in_mm")
    ev_ok = sem("in_ev")
    st_h0 = [sem(f"in_st_h0{i}") for i in range(2)]
    st_qv = [sem(f"in_st_qv{i}") for i in range(2)]
    own, key_ld = sem("in_own"), sem("in_key")
    with ExitStack() as ctx:
        wq = sb(ctx, "wq", [P, KC, 3 * FEAT])
        bias = sb(ctx, "qkv_bias", [P, 3 * FEAT])
        gb = sb(ctx, "attn_gb", [P, 2, KC])
        xg = sb(ctx, "xg", [P, 2, GROUP, FEAT])
        h0 = s_all[:, 0:2 * GROUP * FEAT].rearrange("p (b t f) -> p b t f", b=2, t=GROUP)
        hn = s_all[:, 2 * GROUP * FEAT:3 * GROUP * FEAT].rearrange("p (t f) -> p t f", t=GROUP)
        hT = sb(ctx, "hT", [P, 2, KC, P])
        qv = sb(ctx, "qv", [P, 2, 2, GROUP, FEAT])
        st6 = sb(ctx, "st6", [P, 2, GROUP, 6])
        mv = sb(ctx, "mv", [P, 2, GROUP, 2])
        veps = sb(ctx, "veps", [P, 2, GROUP])
        rstd = sb(ctx, "rstd", [P, 2, GROUP])
        shift = sb(ctx, "shift", [P, GROUP])
        tr_ps = [ps(ctx, f"in_tr{i}", [P, KC, P]) for i in range(2)]
        qk_ps = [ps(ctx, f"in_qk{i}", [P, 512]) for i in range(2)]
        v_ps = [ps(ctx, f"in_v{i}", [P, FEAT]) for i in range(2)]
        rows = lambda d: d.rearrange("(g t p) f -> g p t f", t=GROUP, p=P)

        def next_tiles(t):
            return range(max(0, 2 * t - 2), min(GROUP, 2 * t)) if 1 <= t <= (GROUP + 1) // 2 else range(0)

        with nc.Block() as block:
            @block.sync
            def _(sp):
                def store_h0(g):
                    sp.wait_ge(h0_ok, GROUP * (g + 1))
                    sp.dma_start(rows(h0_d)[g], h0[:, g % 2]).then_inc(st_h0[g % 2], 16)

                def store_qv(g):
                    sp.wait_ge(ev_ok, GROUP * (g + 1))
                    sp.dma_start(rows(q_d)[g], qv[:, g % 2, 0]).then_inc(st_qv[g % 2], 16)
                    sp.dma_start(rows(v_d)[g], qv[:, g % 2, 1]).then_inc(st_qv[g % 2], 16)

                def load(g):
                    if g >= 2:
                        sp.wait_ge(h0_ok, GROUP * (g - 1))
                    sp.dma_start(xg[:, g % 2], rows(x)[g]).then_inc(x_ld[g % 2], 16)

                load(0)
                sp.dma_start(wq[:], wqkv.rearrange("(k p) n -> p k n", p=P)).then_inc(w_ld, 16)
                sp.dma_start(bias[:], bqkv.rearrange("(a n) -> a n", a=1).to_broadcast([P, 3 * FEAT])).then_inc(w_ld, 16)
                with nc.allow_non_contiguous_dma("two columns of LN parameters"):
                    sp.dma_start(gb[:, 0], g_attn.rearrange("(k p) -> p k", p=P)).then_inc(w_ld, 16)
                    sp.dma_start(gb[:, 1], b_attn.rearrange("(k p) -> p k", p=P)).then_inc(w_ld, 16)
                load(1)
                for h in range(HEADS):
                    sp.dma_start(key[h * CHUNKS:(h + 1) * CHUNKS, :],
                                 bass.AP(key_d.tensor, P - 1, [[CHUNK, CHUNKS], [1, CHUNK + 2]])).then_inc(key_ld, 16)
                store_h0(0)
                for g in range(GROUPS):
                    if g + 2 < GROUPS:
                        load(g + 2)
                    if g + 1 < GROUPS:
                        store_h0(g + 1)
                    store_qv(g)
                for n in range(2):
                    sp.wait_ge(st_h0[n], 16 * ((GROUPS + 1 - n) // 2))
                    sp.wait_ge(st_qv[n], 32 * ((GROUPS + 1 - n) // 2))

            @block.vector
            def _(dve):
                n = [0]

                def own_wait(ins):
                    n[0] += 1
                    ins.then_inc(own, 1)
                    dve.wait_ge(own, n[0])

                def variance(which):
                    for t in range(GROUP):
                        last = nc.vector.bn_aggr(mv[:, which, t, :], st6[:, which, t, :])
                    own_wait(last)
                    nc.vector.tensor_scalar(veps[:, which, :], mv[:, which, :, 1], EPS, None, ALU.add).then_inc(stat, 1)

                def stats_of_x(g):
                    dve.wait_ge(x_ld[g % 2], 16 * (g // 2 + 1))
                    for t in range(GROUP):
                        last = nc.vector.bn_stats(st6[:, 0, t, :], xg[:, g % 2, t, :])
                    own_wait(last)
                    variance(0)
                    dve.wait_ge(rstd_ok, 2 * g + 1)
                    nc.vector.scalar_tensor_tensor(out=shift[:], in0=mv[:, 0, :, 0], scalar=-1.0, in1=rstd[:, 0, :],
                                                   op0=ALU.mult, op1=ALU.mult).then_inc(stat, 1)

                def stats_of_h0(g, t):
                    dve.wait_ge(h0_ok, GROUP * g + t + 1)
                    last = nc.vector.bn_stats(st6[:, 1, t, :], h0[:, g % 2, t, :])
                    if t == GROUP - 1:
                        own_wait(last)
                        variance(1)

                def normalise(g):
                    dve.wait_ge(rstd_ok, 2 * g + 2)
                    if g >= 1:
                        dve.wait_ge(tr_ok, GROUP * g)
                    for t in range(GROUP):
                        nc.vector.tensor_scalar(hn[:, t, :], h0[:, g % 2, t, :], mv[:, 1, t, 0:1], rstd[:, 1, t:t + 1],
                                                ALU.subtract, ALU.mult).then_inc(hn_ok, 1)

                own_wait(nc.vector.memset(k_all[:, NODE_TILES * FEAT:], 0.0))
                stats_of_x(0)
                for t in range(GROUP):
                    stats_of_h0(0, t)
                normalise(0)
                stats_of_x(1)
                dve.wait_ge(w_ld, 64)
                for g in range(GROUPS):
                    if g >= 2:
                        dve.wait_ge(st_qv[g % 2], 32 * (g // 2))
                    for t in range(GROUP):
                        n_t = GROUP * g + t
                        if t == GROUP - 1 and g + 1 < GROUPS:
                            normalise(g + 1)
                        dve.wait_ge(mm_ok, n_t + 1)
                        nc.vector.tensor_tensor(qv[:, g % 2, 0, t, :], qk_ps[n_t % 2][:, 0:FEAT], bias[:, 0:FEAT], ALU.add)
                        nc.vector.tensor_tensor(k_all[:, n_t * FEAT:(n_t + 1) * FEAT], qk_ps[n_t % 2][:, FEAT:], bias[:, FEAT:2 * FEAT], ALU.add)
                        nc.vector.tensor_tensor(qv[:, g % 2, 1, t, :], v_ps[n_t % 2][:], bias[:, 2 * FEAT:], ALU.add).then_inc(ev_ok, 1)
                        if g + 1 < GROUPS:
                            for u in next_tiles(t - 1):
                                stats_of_h0(g + 1, u)
                    if g + 2 < GROUPS:
                        stats_of_x(g + 2)
                dve.wait_ge(key_ld, 16 * HEADS)
                own_wait(nc.vector.tensor_tensor(brk[:], key[:, 1:], key[:, 0:CHUNK + 1], ALU.not_equal))
                own_wait(nc.vector.tensor_scalar(brk[:], brk[:], -BIG, None, ALU.mult))

            @block.gpsimd
            def _(pool):
                for g in range(GROUPS):
                    for which in range(2):
                        pool.wait_ge(stat, 3 * g + 1 + 2 * which)
                        nc.gpsimd.tensor_tensor(rstd[:, which, :], veps[:, which, :], neg_half[:], ALU.pow).then_inc(rstd_ok, 1)

            @block.scalar
            def _(act):
                def relu(g, t):
                    if t == 0:
                        act.wait_ge(stat, 3 * g + 2)
                        if g >= 2:
                            act.wait_ge(st_h0[g % 2], 16 * (g // 2))
                            act.wait_ge(hn_ok, GROUP * (g - 1))
                    nc.scalar.activation(h0[:, g % 2, t, :], xg[:, g % 2, t, :], ACT.Relu,
                                         scale=rstd[:, 0, t:t + 1], bias=shift[:, t:t + 1]).then_inc(h0_ok, 1)

                for t in range(GROUP):
                    relu(0, t)
                act.wait_ge(w_ld, 64)
                for g in range(GROUPS):
                    for t in range(GROUP):
                        n_t = GROUP * g + t
                        act.wait_ge(tr_ok, n_t + 1)
                        if n_t >= 2:
                            act.wait_ge(mm_ok, n_t - 1)
                        for k in range(KC):
                            last = nc.scalar.activation(hT[:, n_t % 2, k, :], tr_ps[n_t % 2][:, k, :], ACT.Identity,
                                                        scale=gb[:, 0, k:k + 1], bias=gb[:, 1, k:k + 1])
                        last.then_inc(ht_ok, 1)
                        if g + 1 < GROUPS:
                            for u in next_tiles(t):
                                relu(g + 1, u)

            @block.tensor
            def _(pe):
                def products(m):
                    pe.wait_ge(ht_ok, m + 1)
                    if m >= 2:
                        pe.wait_ge(ev_ok, m - 1)
                    for k in range(KC):
                        nc.tensor.matmul(qk_ps[m % 2][:], hT[:, m % 2, k, :], wq[:, k, 0:512], start=(k == 0), stop=(k == KC - 1))
                    for k in range(KC):
                        last = nc.tensor.matmul(v_ps[m % 2][:], hT[:, m % 2, k, :], wq[:, k, 512:], start=(k == 0), stop=(k == KC - 1))
                    last.then_inc(mm_ok, 1)

                pe.wait_ge(w_ld, 64)
                for g in range(GROUPS):
                    for t in range(GROUP):
                        n_t = GROUP * g + t
                        pe.wait_ge(hn_ok, n_t + 1)
                        if n_t >= 2:
                            pe.wait_ge(ht_ok, n_t - 1)
                        for k in range(KC):
                            last = nc.tensor.transpose(tr_ps[n_t % 2][:, k, :], hn[:, t, k * P:(k + 1) * P], ident[:])
                        last.then_inc(tr_ok, 1)
                        if t >= 1:
                            products(n_t - 1)
                    products(GROUP * g + GROUP - 1)


def load_indices(eng, idx_now, idx_all, columns, half, idx_ld):
    eng.dma_start(idx_now[:, half, :], idx_all[:, columns]).then_inc(idx_ld[half], 16)


def next_indices(eng, idx_now, idx_all, t0, half, got, landed, idx_ld):
    for b in range(half * HALF, (half + 1) * HALF):
        eng.wait_ge(got[b], t0 + landed)
    load_indices(eng, idx_now, idx_all, bass.ds(t0 + (UNROLL + HALF * half), HALF), half, idx_ld)


def gather_rows(nc, pool, t0, b, rows, table, idx_now, got, used, idx_ld, turn):
    if b % HALF == 0:
        pool.wait_ge(idx_ld[b // HALF], t0 + 16)
        pool.sem_inc(turn, 1)
    pool.wait_ge(used, t0 + (b + 1))
    pool.sem_inc(turn, 1)
    start_gather(nc, b, rows, table, idx_now, got)


def start_gather(nc, b, rows, table, idx_now, got):
    nc.gpsimd.indirect_dma_start(rows[:, b, :], None, table,
                                 bass.IndirectOffsetOnAxis(ap=idx_now[:, b // HALF, b % HALF:b % HALF + 1], axis=0)
                                 ).then_inc(got[b], 16)


def by_chunk(scores_d, head):
    return scores_d[head, HALF:, :].rearrange("(c s) p -> c (s p)", c=CHUNKS)


def edge_scores(nc, sb, ps, sem, q_d, scores_d, k_all, iota_n, ident, ident_b, dloc, src_i, tile_i, idx_now, got,
                s_all):
    idx_ld = [sem(f"sc_idx{h}") for h in range(2)]
    landed = 16
    used = sem("sc_used")
    turn = sem("sc_turn")
    hot_ok, turned, hott_ok, expanded, prod_ok = (sem(f"sc_{n}") for n in ("hot", "turned", "hott", "exp", "prod"))
    t_ok, c_ok, st = ([sem(f"sc_{n}{h}") for h in range(2)] for n in ("t", "c", "st"))
    HAD_TURNED = (1, 0)
    EARLY_ROUNDS = -(-((CHUNKS - 1) * CHUNK_STEPS + HALF) // UNROLL)
    assert EARLY_ROUNDS < ROUNDS - 1
    s_ld = sem("sc_s")
    SLOTS = 4
    with ExitStack() as ctx:
        rows = sb(ctx, "q_rows", [P, UNROLL, FEAT])
        scores = sb(ctx, "scores", [P, 2, P])
        hot = sb(ctx, "hot_b", [P, 2 * SLOTS, P], BF16)
        hot_t = sb(ctx, "hot_t", [P, SLOTS, P])
        prod = sb(ctx, "prod", [P, 2, HEADS, HEAD_DIM])
        turned_sb = sb(ctx, "scores_t", [HALF * HEADS, 2, P])
        hot_ps = [ps(ctx, f"hot_ps{i}", [P, P], BF16) for i in range(2)]
        k_ps = [ps(ctx, f"k_ps{i}", [P, FEAT]) for i in range(SLOTS)]
        out_ps = [ps(ctx, f"sco_ps{i}", [P, P]) for i in range(2)]

        with nc.Block() as block:
            @block.sync
            def _(sp):
                by_step = scores_d.rearrange("h s p -> s h p")

                def store_scores(round_no, t0, h):
                    sp.wait_ge(c_ok[h], round_no + 2)
                    first = t0 + HALF * (1 - h)
                    sp.dma_start(by_step[bass.ds(first, HALF)], turned_sb[:, h]).then_inc(st[h], 16)

                for h in range(2):
                    load_indices(sp, idx_now, src_i, slice(h * HALF, (h + 1) * HALF), h, idx_ld)
                def next_and_store(round_no, t0):
                    for h in range(2):
                        next_indices(sp, idx_now, src_i, t0, h, got, landed, idx_ld)
                        store_scores(round_no, t0, 1 - h)

                with sp.Fori(0, EARLY_ROUNDS) as round_no:
                    next_and_store(round_no, sp.snap(round_no * UNROLL))
                for h in range(2):
                    sp.wait_ge(st[h], 16 * (EARLY_ROUNDS + 1))
                for h in range(HEADS):
                    sp.dma_start(s_all[h * CHUNKS:(h + 1) * CHUNKS - 1, :], by_chunk(scores_d, h)[0:CHUNKS - 1]).then_inc(s_ld, 16)
                for round_no in range(EARLY_ROUNDS, ROUNDS - 1):
                    next_and_store(round_no, round_no * UNROLL)
                store_scores(ROUNDS - 1, STEPS - UNROLL, 1)
                store_scores(ROUNDS - 1, STEPS - UNROLL, 0)
                sp.wait_ge(c_ok[1], ROUNDS + 2)
                sp.dma_start(by_step[STEPS:], turned_sb[:, 1]).then_inc(st[1], 16)
                sp.wait_ge(st[0], 16 * (ROUNDS + 1))
                sp.wait_ge(st[1], 16 * (ROUNDS + 2))
                sp.wait_ge(s_ld, 16 * HEADS)

            @block.gpsimd
            def _(pool):
                with pool.Fori(0, ROUNDS) as round_no:
                    t0 = pool.snap(round_no * UNROLL)
                    for b in range(UNROLL):
                        gather_rows(nc, pool, t0, b, rows, q_d, idx_now, got, used, idx_ld, turn)

            @block.scalar
            def _(act):
                def copy_scores(round_no, t0, h):
                    act.wait_ge(t_ok[h], round_no + 1 + HAD_TURNED[h])
                    act.wait_ge(st[h], t0 + 16)
                    nc.scalar.copy(turned_sb[:, h], out_ps[h][0:HALF * HEADS, :]).then_inc(c_ok[h], 1)

                act.sem_inc(hott_ok, SLOTS)
                for h in range(2):
                    act.sem_inc(c_ok[h], 1)
                    act.sem_inc(st[h], 16)
                with act.Fori(0, ROUNDS) as round_no:
                    t0 = act.snap(round_no * UNROLL)
                    for b in range(UNROLL):
                        act.wait_ge(turned, t0 + (b + 1))
                        act.wait_ge(expanded, t0 + (b + 1))
                        nc.scalar.copy(hot_t[:, b % SLOTS, :], hot_ps[b % 2][:]).then_inc(hott_ok, 1)
                        if b in (5, 13):
                            copy_scores(round_no, t0, 1 - b // HALF)
                copy_scores(ROUNDS, STEPS, 1)

            @block.tensor
            def _(pe):
                def turn_scores(h):
                    nc.tensor.transpose(out_ps[h][:], scores[:, h, :], ident[:]).then_inc(t_ok[h], 1)

                pe.sem_inc(expanded, SLOTS)
                pe.sem_inc(t_ok[0], HAD_TURNED[0])

                def turn_hot(slot):
                    nc.tensor.transpose(hot_ps[slot % 2][:], hot[:, slot % (2 * SLOTS), :], ident_b[:]).then_inc(turned, 1)

                pe.wait_ge(hot_ok, 2)
                turn_hot(0)
                turn_hot(1)
                with pe.Fori(0, ROUNDS) as round_no:
                    t0 = pe.snap(round_no * UNROLL)
                    for b in range(UNROLL):
                        tile = pe.value_load(tile_i[0:1, bass.ds(t0 + b, 1)], min_val=0, max_val=NODE_TILES)
                        if b % 2 == 0:
                            pe.wait_ge(hot_ok, t0 + (b + 4))
                            pe.wait_ge(hott_ok, t0 + (b + 2 + SLOTS))
                            turn_hot(b + 2)
                            turn_hot(b + 3)
                        nc.tensor.matmul(k_ps[b % SLOTS][:], hot_t[:, b % SLOTS, :], k_all[:, bass.ds(tile * FEAT, FEAT)],
                                         start=True, stop=True).then_inc(expanded, 1)
                        if b in (4, 12):
                            turn_scores(1 - b // HALF)
                pe.wait_ge(used, STEPS + UNROLL)
                pe.wait_ge(c_ok[1], ROUNDS + 1)
                turn_scores(1)

            @block.vector
            def _(dve):
                dve.sem_inc(prod_ok, SLOTS)
                nc.vector.memset(scores[:], 0.0).then_inc(used, UNROLL)

                def make_hot(column, slot):
                    nc.vector.tensor_scalar(hot[:, slot % (2 * SLOTS), :], iota_n[:], column, None, ALU.is_equal).then_inc(hot_ok, 1)

                for n in range(AHEAD):
                    make_hot(dloc[:, n:n + 1], n)
                with dve.Fori(0, ROUNDS) as round_no:
                    t0 = dve.snap(round_no * UNROLL)
                    for b in range(UNROLL):
                        dve.wait_ge(got[b], t0 + landed)
                        dve.wait_ge(expanded, t0 + (b + 1 + SLOTS))
                        nc.vector.tensor_tensor(prod[:, b % 2].rearrange("p h d -> p (h d)"), rows[:, b, :], k_ps[b % SLOTS][:],
                                                ALU.mult).then_inc(prod_ok, 1)
                        make_hot(dloc[:, bass.ds(t0 + (b + AHEAD), 1)], b + AHEAD)
                        dve.wait_ge(prod_ok, t0 + (b + 1 + SLOTS))
                        if b % HALF == 0:
                            dve.wait_ge(t_ok[b // HALF], round_no + 1)
                        nc.vector.tensor_reduce(scores[:, b // HALF, b % HALF * HEADS:(b % HALF + 1) * HEADS], prod[:, b % 2], AX_X, ALU.add).then_inc(used, 1)


def softmax_numerators(nc, sb, ps, sem, scores_d, probs_d, key, brk, s, ident, ones,
                       v_d, v_rows, src_i, idx_now, got, v_idx_ld):
    ld, dve_did, pe_did, exp_ok, st, zero_ok = (sem(f"sm_{n}") for n in ("ld", "dve", "pe", "exp", "st", "zero"))
    with ExitStack() as ctx:
        fwd = sb(ctx, "sm_fwd", [P, CHUNK])
        bwd = sb(ctx, "sm_bwd", [P, CHUNK])
        ends = sb(ctx, "sm_ends", [P, 4])
        rows_sb = sb(ctx, "sm_rows", [1, 4, P])
        carry = sb(ctx, "sm_carry", [1, 2, P])
        carry_c = sb(ctx, "sm_carry_c", [P, 2])
        zeros = sb(ctx, "sm_zeros", [P, P])
        row_ps = ps(ctx, "sm_row_ps", [1, 4 * P])
        col_ps = ps(ctx, "sm_col_ps", [P, 2])

        part_of = lambda n: slice(n * CHUNK // SM_PARTS, (n + 1) * CHUNK // SM_PARTS)

        with nc.Block() as block:
            @block.sync
            def _(sp):
                for h in range(HEADS):
                    sp.dma_start(s[(h + 1) * CHUNKS - 1:(h + 1) * CHUNKS, :], by_chunk(scores_d, h)[CHUNKS - 1:]).then_inc(ld, 16)
                sp.wait_ge(zero_ok, 1)
                sp.dma_start(probs_d[:, STEPS:, :], zeros[:]).then_inc(st, 16)
                for n in range(SM_PARTS):
                    sp.wait_ge(exp_ok, n + 1)
                    for h in range(HEADS):
                        sp.dma_start(probs_d[h, 0:STEPS, :].rearrange("(c s) p -> c (s p)", c=CHUNKS)[:, part_of(n)],
                                     s[h * CHUNKS:(h + 1) * CHUNKS, part_of(n)]).then_inc(st, 16)
                sp.wait_ge(st, 16 * (SM_PARTS * HEADS + 1))

            @block.gpsimd
            def _(pool):
                nc.gpsimd.memset(zeros[:], 0.0).then_inc(zero_ok, 1)
                for b in range(UNROLL):
                    if b % HALF == 0:
                        pool.wait_ge(v_idx_ld[b // HALF], 16)
                    start_gather(nc, b, v_rows, v_d, idx_now, got)

            @block.vector
            def _(dve):
                done = [0]

                def did(ins):
                    done[0] += 1
                    ins.then_inc(dve_did, 1)
                    dve.wait_ge(dve_did, done[0])

                dve.wait_ge(ld, 16 * HEADS)
                did(nc.vector.tensor_tensor_scan(fwd[:], brk[:, 0:CHUNK], s[:], -BIG, ALU.add, ALU.max))
                did(nc.vector.tensor_tensor_scan(bwd[:, ::-1], brk[:, CHUNK:0:-1], s[:, ::-1], -BIG, ALU.add, ALU.max))
                nc.vector.tensor_copy(ends[:, 0:1], fwd[:, CHUNK - 1:])
                nc.vector.tensor_copy(ends[:, 2:3], bwd[:, 0:1])
                nc.vector.tensor_tensor(ends[:, 1:2], key[:, 0:1], key[:, CHUNK:CHUNK + 1], ALU.not_equal)
                did(nc.vector.tensor_tensor(ends[:, 3:4], key[:, 1:2], key[:, CHUNK + 1:], ALU.not_equal))
                dve.wait_ge(pe_did, 1)
                did(nc.vector.tensor_copy(rows_sb[:].rearrange("a n p -> a (n p)"), row_ps[:]))
                for n in (1, 3):
                    last = nc.vector.tensor_scalar(rows_sb[:, n, :], rows_sb[:, n, :], -BIG, None, ALU.mult)
                did(last)
                nc.vector.memset(carry[:], -BIG)
                did(nc.vector.tensor_copy(ends[:, 0:1], ends[:, 0:1]))
                did(nc.vector.tensor_tensor_scan(carry[:, 0, 1:], rows_sb[:, 1, 0:P - 1], rows_sb[:, 0, 0:P - 1], -BIG,
                                                 ALU.add, ALU.max))
                did(nc.vector.tensor_tensor_scan(carry[:, 1, P - 2::-1], rows_sb[:, 3, P - 1:0:-1], rows_sb[:, 2, P - 1:0:-1],
                                                 -BIG, ALU.add, ALU.max))
                dve.wait_ge(pe_did, 2)
                did(nc.vector.tensor_copy(carry_c[:], col_ps[:]))
                did(nc.vector.tensor_tensor_scan(fwd[:], brk[:, 0:CHUNK], s[:], carry_c[:, 0:1], ALU.add, ALU.max))
                did(nc.vector.tensor_tensor_scan(bwd[:, ::-1], brk[:, CHUNK:0:-1], s[:, ::-1], carry_c[:, 1:2], ALU.add, ALU.max))
                for n in range(SM_PARTS):
                    did(nc.vector.tensor_tensor(fwd[:, part_of(n)], fwd[:, part_of(n)], bwd[:, part_of(n)], ALU.max))
                    did(nc.vector.tensor_tensor(s[:, part_of(n)], s[:, part_of(n)], fwd[:, part_of(n)], ALU.subtract))
                assert done[0] == SM_DVE + 2 * SM_PARTS

            @block.tensor
            def _(pe):
                pe.wait_ge(dve_did, 3)
                for n in range(4):
                    last = nc.tensor.transpose(row_ps[:, n * P:(n + 1) * P], ends[:, n:n + 1], ident[:])
                last.then_inc(pe_did, 1)
                pe.wait_ge(dve_did, 8)
                for n in range(2):
                    last = nc.tensor.matmul(col_ps[:, n:n + 1], carry[:, n, :], ones[0:1, 0:1], start=True, stop=True)
                last.then_inc(pe_did, 1)

            @block.scalar
            def _(act):
                for h in range(2):
                    load_indices(act, idx_now, src_i, slice(h * HALF, (h + 1) * HALF), h, v_idx_ld)
                for n in range(SM_PARTS):
                    act.wait_ge(dve_did, SM_DVE + 2 * (n + 1))
                    nc.scalar.activation(s[:, part_of(n)], s[:, part_of(n)], ACT.Exp, scale=ATT_SCALE).then_inc(exp_ok, 1)


SM_DVE = 11
SM_PARTS = 4


def edge_sum(nc, sb, ps, sem, name, table, sums, width, probs_d, iota_n, ident, dloc, norm_s, keep,
             row_i, store_i, ends_i, idx_now, got, gathers_before, beside=None,
             first_round=None):
    rows, idx_ld = first_round or (None, [sem(f"{name}_idx{h}") for h in range(2)])
    landed = gathers_before * ROUNDS * 16 + 16
    att = probs_d is not None
    summed = sem(f"{name}_sum")
    used = sem(f"{name}_used") if att else summed
    beside_ld = sem(f"{name}_beside") if beside else None
    credit = 4 if att else UNROLL
    turn = sem(f"{name}_turn")
    hot_ok, acc_ok, acc_free, acc_st = (sem(f"{name}_{n}") for n in ("hot", "acc", "accf", "accs"))
    if att:
        den_ok, p_ld, p_tr, p_ok = (sem(f"{name}_{n}") for n in ("den", "pld", "ptr", "pok"))
    with ExitStack() as ctx:
        if not first_round:
            rows = sb(ctx, f"{name}_rows", [P, UNROLL, FEAT])
        hot = sb(ctx, f"{name}_hot", [P, 4, P])
        acc = sb(ctx, f"{name}_acc", [P, ACC_RING, width])
        if att:
            probs = sb(ctx, "probs", [P, (STEPS + UNROLL) * HEADS])
            probs_t = sb(ctx, "probs_t", [P, P])
            val = sb(ctx, "val", [P, 4, AGGW])
        sum_ps = [ps(ctx, f"{name}_ps{i}", [P, width]) for i in range(4)]
        turn_ps = ps(ctx, f"{name}_tps", [P, P])

        with nc.Block() as block:
            @block.sync
            def _(sp):
                sp.sem_inc(acc_free, ACC_RING)
                if beside:
                    for g in range(GROUPS):
                        sp.dma_start(beside[1][:, g], beside[0].rearrange("(g t p) f -> g p t f", t=GROUP, p=P)[g]).then_inc(beside_ld, 16)

                def store_ended(t0, b):
                    code = sp.value_load(store_i[0:1, bass.ds(t0 + b, 1)], min_val=0, max_val=NOT_LAST + NODE_TILES)
                    sp.wait_ge(acc_ok, t0 + (b + 2))
                    sp.sem_inc(turn, 1)
                    with sp.If(code < NODE_TILES):
                        tile = nc.s_assert_within(
                            code, 0, NODE_TILES - 1,
                            skip_runtime_bounds_check_because="this branch is taken only for codes below NODE_TILES")
                        place = sums[bass.ds(tile * P, P), :] if att else sums[:, bass.ds(tile * width, width)]
                        sp.dma_start(place, acc[:, b % ACC_RING, :]).then_inc(acc_st, 16)
                        sp.wait_ge(acc_st, tile * 16 + 16)
                        sp.sem_inc(turn, 1)
                    sp.sem_inc(acc_free, 1)

                with sp.Fori(0, ROUNDS) as round_no:
                    t0 = sp.snap(round_no * UNROLL)
                    for b in range(0, UNROLL, QUAD):
                        any_ends = sp.value_load(ends_i[0:1, bass.ds(round_no * (UNROLL // QUAD) + b // QUAD, 1)],
                                                 min_val=0, max_val=1)
                        with sp.If(any_ends > 0):
                            for q in range(QUAD):
                                store_ended(t0, b + q)
                        with sp.Else():
                            sp.wait_ge(acc_ok, t0 + (b + QUAD + 1))
                            sp.sem_inc(acc_free, QUAD)
                sp.wait_ge(acc_st, 16 * NODE_TILES)
                if beside:
                    sp.wait_ge(beside_ld, 16 * GROUPS)

            @block.gpsimd
            def _(pool):
                start = 1 if first_round else 0
                with pool.Fori(0, ROUNDS - start) as round_no:
                    t0 = pool.snap((round_no + start) * UNROLL)
                    for b in range(UNROLL):
                        gather_rows(nc, pool, t0, b, rows, table, idx_now, got, used, idx_ld, turn)

            @block.scalar
            def _(act):
                if not first_round:
                    for h in range(2):
                        load_indices(act, idx_now, row_i, slice(h * HALF, (h + 1) * HALF), h, idx_ld)

                def load_numerators(steps):
                    act.dma_start(probs_t[:], probs_d.rearrange("h s p -> s h p")[steps]).then_inc(p_ld, 16)

                def copy_numerators(n, columns):
                    act.wait_ge(p_tr, n + 1)
                    nc.scalar.copy(probs[:, columns], turn_ps[:]).then_inc(p_ok, 1)

                if att:
                    load_numerators(slice(0, UNROLL))
                    copy_numerators(0, slice(0, P))
                    load_numerators(slice(UNROLL, 2 * UNROLL))

                def numerators(t0, b):
                    act.wait_ge(summed, t0 + (b + 1))
                    nc.scalar.copy(val[:, b % 4, FEAT:], probs[:, bass.ds((t0 + b) * HEADS, HEADS)]).then_inc(den_ok, 1)

                with act.Fori(0, ROUNDS - 1) as round_no:
                    t0 = act.snap(round_no * UNROLL)
                    for h in range(2):
                        if att:
                            if h == 0:
                                act.wait_ge(p_ok, round_no + 1)
                            else:
                                copy_numerators(round_no + 1, bass.ds(round_no * P + P, P))
                                load_numerators(bass.ds(t0 + 2 * UNROLL, UNROLL))
                            for b in range(h * HALF, (h + 1) * HALF):
                                numerators(t0, b)
                        next_indices(act, idx_now, row_i, t0, h, got, landed, idx_ld)
                if att:
                    act.wait_ge(p_ok, ROUNDS)
                    for b in range(UNROLL):
                        numerators(STEPS - UNROLL, b)

            @block.tensor
            def _(pe):
                def turn_numerators(n):
                    pe.wait_ge(p_ld, (n + 1) * 16)
                    nc.tensor.transpose(turn_ps[:], probs_t[:], ident[:]).then_inc(p_tr, 1)

                if att:
                    turn_numerators(0)
                pe.sem_inc(summed, credit)
                with pe.Fori(0, ROUNDS) as round_no:
                    t0 = pe.snap(round_no * UNROLL)
                    for b in range(UNROLL):
                        if att and b == 2:
                            pe.wait_ge(p_ok, round_no + 1)
                            turn_numerators(round_no + 1)
                        pe.wait_ge(hot_ok, t0 + (b + 1))
                        if b >= 4:
                            pe.wait_ge(acc_ok, t0 + (b - 2))
                        if att:
                            pe.wait_ge(used, t0 + (b + 1 + UNROLL))
                            pe.wait_ge(den_ok, t0 + (b + 1))
                            moving = val[:, b % 4, :]
                        else:
                            pe.wait_ge(got[b], t0 + landed)
                            moving = rows[:, b, :]
                        nc.tensor.matmul(sum_ps[b % 4][:], hot[:, b % 4, :], moving, start=True, stop=True).then_inc(summed, 1)

            @block.vector
            def _(dve):
                if att:
                    dve.sem_inc(used, UNROLL)
                nc.vector.memset(acc[:], 0.0).then_inc(acc_ok, 1)

                def feed(t0, b):
                    column = dloc[:, bass.ds(t0 + b, 1)]
                    dve.wait_ge(summed, t0 + (b - 3 + credit))
                    if att:
                        nc.vector.tensor_scalar(hot[:, b % 4, :], iota_n[:], column, None, ALU.is_equal).then_inc(hot_ok, 1)
                        dve.wait_ge(got[b], t0 + landed)
                        weights = probs[:, bass.ds((t0 + b) * HEADS, HEADS)]
                        nc.vector.tensor_tensor(val[:, b % 4, 0:FEAT].rearrange("p (h d) -> p h d", h=HEADS),
                                                rows[:, b, :].rearrange("p (h d) -> p h d", h=HEADS),
                                                weights.rearrange("p (h o) -> p h o", o=1).to_broadcast([P, HEADS, HEAD_DIM]),
                                                ALU.mult).then_inc(used, 1)
                    else:
                        nc.vector.tensor_scalar(hot[:, b % 4, :], iota_n[:], column, norm_s[:, bass.ds(t0 + b, 1)],
                                                ALU.is_equal, ALU.mult).then_inc(hot_ok, 1)

                def accumulate(t0, b):
                    dve.wait_ge(summed, t0 + (b + 1 + credit))
                    dve.wait_ge(acc_free, t0 + (b + 1))
                    dve.wait_ge(acc_ok, t0 + (b + 1))
                    nc.vector.scalar_tensor_tensor(out=acc[:, b % ACC_RING, :], in0=acc[:, (b - 1) % ACC_RING, :],
                                                   scalar=keep[:, bass.ds(t0 + b, 1)], in1=sum_ps[b % 4][:],
                                                   op0=ALU.mult, op1=ALU.add).then_inc(acc_ok, 1)

                with dve.Fori(0, ROUNDS) as round_no:
                    t0 = dve.snap(round_no * UNROLL)
                    if att:
                        dve.wait_ge(p_ok, round_no + 1)
                    for b in range(UNROLL):
                        feed(t0, b)
                        if b >= 2:
                            accumulate(t0, b - 2)
                    accumulate(t0, UNROLL - 2)
                    accumulate(t0, UNROLL - 1)


def node_mlp(nc, sb, ps, sem, x, g_res, b_res, w_in, b_in, w_out, b_out, ident, neg_half, h0_d, agg_d, x1_d, h1_d):
    w_ld, w_split = [sem(f"ml_w{i}") for i in range(2)], sem("ml_wsplit")
    p_ld, in_ld, own = sem("ml_par"), sem("ml_in"), sem("ml_own")
    stat, rstd_ok = [sem(f"ml_stat{i}") for i in range(2)], [sem(f"ml_rstd{i}") for i in range(2)]
    yn_ok, tr_ok, y_ok, ylo_ok = sem("ml_yn"), sem("ml_tr"), sem("ml_y"), sem("ml_ylo")
    hid_mm, gelu_ok, hi_ok, lo_ok, out_mm = (sem(f"ml_{n}") for n in ("hmm", "gelu", "hi", "lo", "omm"))
    x1_ok, x1_st, h1_ok, h1_st = (sem(f"ml_{n}") for n in ("x1", "x1s", "h1", "h1s"))
    NC_ = GROUP * P
    HN = NC_ // 2
    NM = 2 * FFC
    RING = 4
    with ExitStack() as ctx:
        win_raw = sb(ctx, "w_raw", [P, KC, DFF])
        win = sb(ctx, "win", [P, 2, KC, DFF], F32R)
        wout = sb(ctx, "wout", [P, 2, FFC, FEAT], F32R)
        bin_c = sb(ctx, "bin_c", [P, FFC])
        bout = sb(ctx, "bout", [P, FEAT])
        gb = sb(ctx, "res_gb", [P, 2, KC])
        agg = sb(ctx, "up_agg", [P, GROUP, AGGW])
        h0 = sb(ctx, "up_h0", [P, GROUP, FEAT])
        xg = sb(ctx, "up_x", [P, GROUP, FEAT])
        den = sb(ctx, "up_den", [P, GROUP, HEADS])
        x2 = sb(ctx, "up_x2", [P, GROUP, FEAT])
        res = sb(ctx, "up_res", [P, 2, GROUP, FEAT])
        y = sb(ctx, "up_y", [P, 2, KC, P])
        yT = sb(ctx, "up_yT", [P, 2, KC, NC_], F32R)
        gelu = sb(ctx, "up_gelu", [P, RING, HN])
        hid = sb(ctx, "up_hid", [P, 2, FFC, NC_], F32R)
        x1_h1 = sb(ctx, "up_x1_h1", [P, 2 * GROUP * FEAT])
        x1 = x1_h1[:, 0:GROUP * FEAT].rearrange("p (t f) -> p t f", t=GROUP)
        h1 = x1_h1[:, GROUP * FEAT:].rearrange("p (t f) -> p t f", t=GROUP)
        wout_raw = x1_h1[:, 0:FFC * FEAT].rearrange("p (k n) -> p k n", k=FFC)
        st6 = sb(ctx, "up_st6", [P, 2, GROUP, 6])
        mv = sb(ctx, "up_mv", [P, 2, GROUP, 2])
        veps = sb(ctx, "up_veps", [P, 2, GROUP])
        rstd = sb(ctx, "up_rstd_t", [P, 2, GROUP])
        tr_ps = [ps(ctx, f"up_tr{i}", [P, KC, P]) for i in range(2)]
        hid_ps = [ps(ctx, f"up_hid_ps{i}", [P, HN]) for i in range(RING)]
        out_ps = [ps(ctx, f"up_out_ps{i}", [P, FEAT]) for i in range(2)]
        rows = lambda d: d.rearrange("(g t p) f -> g p t f", t=GROUP, p=P)

        def powers_before(g, which):
            return g if which == 1 or g == 0 else GROUP + g - 1

        def hid_block(m):
            half, chunk = m // FFC, m % FFC
            return chunk, slice(half * HN, (half + 1) * HN)

        with nc.Block() as block:
            @block.sync
            def _(sp):
                def load(g):
                    if g >= 1:
                        sp.wait_ge(yn_ok, GROUP * g)
                    sp.dma_start(agg[:], rows(agg_d)[g]).then_inc(in_ld, 16)
                    sp.dma_start(h0[:], rows(h0_d)[g]).then_inc(in_ld, 16)
                    sp.dma_start(xg[:], rows(x)[g]).then_inc(in_ld, 16)

                sp.dma_start(bout[:], b_out.rearrange("(a n) -> a n", a=1).to_broadcast([P, FEAT])).then_inc(p_ld, 16)
                with nc.allow_non_contiguous_dma("small columns of parameters"):
                    sp.dma_start(bin_c[:], b_in.rearrange("(k p) -> p k", p=P)).then_inc(p_ld, 16)
                    sp.dma_start(gb[:, 0], g_res.rearrange("(k p) -> p k", p=P)).then_inc(p_ld, 16)
                    sp.dma_start(gb[:, 1], b_res.rearrange("(k p) -> p k", p=P)).then_inc(p_ld, 16)
                load(0)
                load(1)
                load(2)
                for g in range(GROUPS):
                    sp.wait_ge(x1_ok, GROUP * (g + 1))
                    sp.dma_start(rows(x1_d)[g], x1[:]).then_inc(x1_st, 16)
                    sp.wait_ge(h1_ok, GROUP * (g + 1))
                    sp.dma_start(rows(h1_d)[g], h1[:]).then_inc(h1_st, 16)
                    if g + 3 < GROUPS:
                        load(g + 3)
                sp.wait_ge(x1_st, 16 * GROUPS)
                sp.wait_ge(h1_st, 16 * GROUPS)

            @block.vector
            def _(dve):
                n = [0]

                def own_wait(ins):
                    n[0] += 1
                    ins.then_inc(own, 1)
                    dve.wait_ge(own, n[0])

                def x2_tile(g, t):
                    if t == 0:
                        dve.wait_ge(in_ld, 48 * (g + 1))
                        own_wait(nc.vector.tensor_scalar(den[:], agg[:, :, FEAT:], 1e-30, None, ALU.max))
                        own_wait(nc.vector.reciprocal(den[:], den[:]))
                    if g >= 1:
                        dve.wait_ge(tr_ok, GROUP * (g - 1) + t + 1)
                    nc.vector.tensor_tensor(res[:, g % 2, t, :], xg[:, t, :], bout[:], ALU.add)
                    own_wait(nc.vector.tensor_tensor(x2[:, t, :].rearrange("p (h d) -> p h d", h=HEADS),
                                                     agg[:, t, 0:FEAT].rearrange("p (h d) -> p h d", h=HEADS),
                                                     den[:, t, :].rearrange("p (h o) -> p h o", o=1).to_broadcast([P, HEADS, HEAD_DIM]),
                                                     ALU.mult))
                    own_wait(nc.vector.tensor_tensor(x2[:, t, :], x2[:, t, :], h0[:, t, :], ALU.add))
                    nc.vector.bn_stats(st6[:, 0, t, :], x2[:, t, :])
                    own_wait(nc.vector.tensor_tensor(res[:, g % 2, t, :], res[:, g % 2, t, :], x2[:, t, :], ALU.add))

                def x1_tile(g, t):
                    if t == 0 and g >= 1:
                        dve.wait_ge(x1_st, 16 * g)
                    dve.wait_ge(out_mm, GROUP * g + t + 1)
                    nc.vector.tensor_tensor(x1[:, t, :], out_ps[(GROUP * g + t) % 2][:], res[:, g % 2, t, :], ALU.add).then_inc(x1_ok, 1)

                def x1_stats(g, t):
                    dve.wait_ge(x1_ok, GROUP * g + t + 1)
                    nc.vector.bn_stats(st6[:, 1, t, :], x1[:, t, :]).then_inc(own, 1)
                    n[0] += 1

                def variance(which):
                    dve.wait_ge(own, n[0])
                    for t in range(GROUP):
                        last = nc.vector.bn_aggr(mv[:, which, t, :], st6[:, which, t, :])
                    own_wait(last)
                    nc.vector.tensor_scalar(veps[:, which, :], mv[:, which, :, 1], EPS, None, ALU.add).then_inc(stat[which], 1)

                def first_variance(t):
                    own_wait(nc.vector.bn_aggr(mv[:, 0, t, :], st6[:, 0, t, :]))
                    nc.vector.tensor_scalar(veps[:, 0, t:t + 1], mv[:, 0, t, 1:2], EPS, None, ALU.add).then_inc(stat[0], 1)

                def normalise(g, which, src_t, dst_t, ok, tiles=range(GROUP)):
                    for t in tiles:
                        if which == 0 and g == 0:
                            dve.wait_ge(rstd_ok[0], t + 1)
                        elif t == 0:
                            dve.wait_ge(rstd_ok[which], powers_before(g, which) + 1)
                        nc.vector.tensor_scalar(dst_t[:, t, :], src_t[:, t, :], mv[:, which, t, 0:1], rstd[:, which, t:t + 1],
                                                ALU.subtract, ALU.mult).then_inc(ok, 1)

                def y_low(g, t):
                    n_t = GROUP * g + t
                    dve.wait_ge(y_ok, n_t + 1)
                    cols = slice(t * P, (t + 1) * P)
                    nc.vector.tensor_tensor(yT[:, 1, :, cols], y[:, n_t % 2], yT[:, 0, :, cols].bitcast(F32),
                                            ALU.subtract).then_inc(ylo_ok, 1)

                def hid_low(g, m):
                    chunk, cols = hid_block(m)
                    dve.wait_ge(hi_ok, NM * g + m + 1)
                    nc.vector.tensor_tensor(hid[:, 1, chunk, cols], gelu[:, m % RING, :], hid[:, 0, chunk, cols].bitcast(F32),
                                            ALU.subtract).then_inc(lo_ok, 1)

                dve.wait_ge(p_ld, 16 * 4)
                for t in range(GROUP):
                    x2_tile(0, t)
                    first_variance(t)
                    if t >= 1:
                        normalise(0, 0, x2, x2, yn_ok, [t - 1])
                normalise(0, 0, x2, x2, yn_ok, [GROUP - 1])
                dve.wait_ge(w_split, 2)
                nc.vector.tensor_tensor(win[:, 1], win_raw[:], win[:, 0].bitcast(F32), ALU.subtract).then_inc(w_split, 1)
                for t in range(GROUP):
                    y_low(0, t)
                for t in range(GROUP):
                    x2_tile(1, t)
                    hid_low(0, t)
                variance(0)
                for m in range(GROUP, NM):
                    hid_low(0, m)
                    if m == GROUP + 2:
                        normalise(1, 0, x2, x2, yn_ok)
                nc.vector.tensor_tensor(wout[:, 1], wout_raw, wout[:, 0].bitcast(F32), ALU.subtract).then_inc(w_split, 1)
                for g in range(GROUPS):
                    if g + 1 < GROUPS:
                        y_low(g + 1, 0)
                        y_low(g + 1, 1)
                    for t in range(GROUP):
                        if g + 1 < GROUPS and t + 2 < GROUP:
                            y_low(g + 1, t + 2)
                        x1_tile(g, t)
                        x1_stats(g, t)
                        if g + 2 < GROUPS:
                            x2_tile(g + 2, t)
                    variance(1)
                    if g + 2 < GROUPS:
                        variance(0)
                    if g + 1 < GROUPS:
                        for m in range(NM):
                            hid_low(g + 1, m)
                            if m == 2:
                                if g >= 1:
                                    dve.wait_ge(h1_st, 16 * g)
                                normalise(g, 1, x1, h1, h1_ok)
                            if m == 5 and g + 2 < GROUPS:
                                normalise(g + 2, 0, x2, x2, yn_ok)
                    else:
                        dve.wait_ge(h1_st, 16 * g)
                        normalise(g, 1, x1, h1, h1_ok)

            @block.gpsimd
            def _(pool):
                def power(g, which):
                    pool.wait_ge(stat[which], powers_before(g, which) + 1)
                    nc.gpsimd.tensor_tensor(rstd[:, which, :], veps[:, which, :], neg_half[:], ALU.pow).then_inc(rstd_ok[which], 1)

                for t in range(GROUP):
                    pool.wait_ge(stat[0], t + 1)
                    nc.gpsimd.tensor_tensor(rstd[:, 0, t:t + 1], veps[:, 0, t:t + 1], neg_half[:, 0:1], ALU.pow).then_inc(rstd_ok[0], 1)
                power(1, 0)
                for g in range(GROUPS):
                    power(g, 1)
                    if g + 2 < GROUPS:
                        power(g + 2, 0)

            @block.scalar
            def _(act):
                def turned_y(g):
                    for t in range(GROUP):
                        n_t = GROUP * g + t
                        act.wait_ge(tr_ok, n_t + 1)
                        if n_t >= 2:
                            act.wait_ge(ylo_ok, n_t - 1)
                        if t == 0 and g >= 1:
                            act.wait_ge(hid_mm, NM * g)
                        for k in range(KC):
                            nc.scalar.activation(y[:, n_t % 2, k, :], tr_ps[n_t % 2][:, k, :], ACT.Identity,
                                                 scale=gb[:, 0, k:k + 1], bias=gb[:, 1, k:k + 1])
                            last = nc.scalar.activation(yT[:, 0, k, t * P:(t + 1) * P], tr_ps[n_t % 2][:, k, :], ACT.Identity,
                                                        scale=gb[:, 0, k:k + 1], bias=gb[:, 1, k:k + 1])
                        last.then_inc(y_ok, 1)

                def high(g, m):
                    chunk, cols = hid_block(m)
                    act.wait_ge(gelu_ok, NM * g + m + 1)
                    nc.scalar.copy(hid[:, 0, chunk, cols], gelu[:, m % RING, :]).then_inc(hi_ok, 1)

                def hidden(g):
                    for m in range(NM):
                        chunk, _ = hid_block(m)
                        act.wait_ge(hid_mm, NM * g + m + 1)
                        if NM * g + m >= RING:
                            act.wait_ge(lo_ok, NM * g + m + 1 - RING)
                        if m == 0 and g >= 1:
                            act.wait_ge(out_mm, GROUP * g)
                        nc.scalar.activation(gelu[:, m % RING, :], hid_ps[m % RING][:], ACT.Gelu,
                                             bias=bin_c[:, chunk:chunk + 1]).then_inc(gelu_ok, 1)
                        if m >= 1:
                            high(g, m - 1)
                    high(g, NM - 1)

                act.wait_ge(p_ld, 16 * 4)
                act.dma_start(win_raw[:], w_in.rearrange("(k p) n -> p k n", p=P)).then_inc(w_ld[0], 16)
                act.dma_start(wout_raw, w_out.rearrange("(k p) n -> p k n", p=P)).then_inc(w_ld[1], 16)
                act.wait_ge(w_ld[0], 16)
                nc.scalar.copy(win[:, 0], win_raw[:]).then_inc(w_split, 1)
                act.wait_ge(w_ld[1], 16)
                nc.scalar.copy(wout[:, 0], wout_raw).then_inc(w_split, 1)
                turned_y(0)
                hidden(0)
                for g in range(1, GROUPS):
                    turned_y(g)
                    hidden(g)

            @block.tensor
            def _(pe):
                PARTS = ((0, 0), (0, 1), (1, 0))

                def turn(g, t):
                    n_t = GROUP * g + t
                    pe.wait_ge(yn_ok, n_t + 1)
                    if n_t >= 2:
                        pe.wait_ge(y_ok, n_t - 1)
                    for k in range(KC):
                        last = nc.tensor.transpose(tr_ps[n_t % 2][:, k, :], x2[:, t, k * P:(k + 1) * P], ident[:])
                    last.then_inc(tr_ok, 1)

                def hidden(g):
                    for m in range(NM):
                        chunk, cols = hid_block(m)
                        if m % FFC == 0:
                            pe.wait_ge(ylo_ok, GROUP * g + (4 if m == 0 else GROUP))
                        if NM * g + m >= RING:
                            pe.wait_ge(gelu_ok, NM * g + m + 1 - RING)
                        parts = [(k, a, b) for k in range(KC) for a, b in PARTS]
                        for i, (k, a, b) in enumerate(parts):
                            last = nc.tensor.matmul(hid_ps[m % RING][:], win[:, a, k, chunk * P:(chunk + 1) * P],
                                                    yT[:, b, k, cols], start=(i == 0), stop=(i == len(parts) - 1))
                        last.then_inc(hid_mm, 1)

                def output(g):
                    for t in range(GROUP):
                        n_t = GROUP * g + t
                        if t == 0:
                            pe.wait_ge(lo_ok, NM * g + FFC)
                        elif t == 3:
                            pe.wait_ge(lo_ok, NM * (g + 1))
                        if n_t >= 2:
                            pe.wait_ge(x1_ok, n_t - 1)
                        parts = [(m, a, b) for m in range(FFC) for a, b in PARTS]
                        for i, (m, a, b) in enumerate(parts):
                            last = nc.tensor.matmul(out_ps[n_t % 2][:], hid[:, a, m, t * P:(t + 1) * P], wout[:, b, m, :],
                                                    start=(i == 0), stop=(i == len(parts) - 1))
                        last.then_inc(out_mm, 1)
                        if g + 1 < GROUPS and t + 2 < GROUP:
                            turn(g + 1, t + 2)

                for t in range(GROUP):
                    turn(0, t)
                pe.wait_ge(w_split, 3)
                hidden(0)
                for g in range(GROUPS):
                    if g + 1 < GROUPS:
                        turn(g + 1, 0)
                        turn(g + 1, 1)
                    if g == 0:
                        pe.wait_ge(w_split, 4)
                    output(g)
                    if g + 1 < GROUPS:
                        hidden(g + 1)


def messages(nc, sb, ps, sem, w_rel, w_gate, ident, h1_d, msg_d):
    w_ld, w_hi, w_lo, g_ld = [sem(f"ms_w{c}") for c in range(MSG_WC)], sem("ms_whi"), sem("ms_wlo"), sem("ms_g")
    h_ld = [sem(f"ms_h{i}") for i in range(2)]
    tr_ok, ht_ok, lo_ok, gate_mm, gate_ok = (sem(f"ms_{n}") for n in ("tr", "ht", "lo", "gmm", "gate"))
    msg_mm, ev_act, ev_dve = (sem(f"ms_{n}") for n in ("mm", "eva", "evd"))
    SLOTS = 3
    BANKS = 5
    msg_st = [sem(f"ms_st{i}") for i in range(SLOTS)]
    HALF_COLS = RELS * FEAT // 2
    HALVES = 2 * NODE_TILES
    with ExitStack() as ctx:
        raw = sb(ctx, "wrel_raw", [P, KC, RELS, FEAT])
        wrel = sb(ctx, "wrel", [P, 2, KC, RELS, FEAT], F32R)
        wgate = sb(ctx, "wgate", [P, KC, RELS])
        h1 = sb(ctx, "ms_h1", [P, 2, GROUP, FEAT])
        hT = sb(ctx, "ms_hT", [P, 2, KC, P])
        hTs = sb(ctx, "ms_hTs", [P, 2, 2, KC, P], F32R)
        gate = sb(ctx, "ms_gate", [P, 2, RELS])
        msg = sb(ctx, "msg", [P, SLOTS, HALF_COLS])
        tr_ps = [ps(ctx, f"ms_tr{i}", [P, KC, P]) for i in range(2)]
        gate_ps = ps(ctx, "ms_gate_ps", [P, RELS])
        mm_ps = [ps(ctx, f"ms_mm{i}", [P, 512]) for i in range(BANKS)]
        w_part = lambda c: slice(c * RELS // MSG_WC, (c + 1) * RELS // MSG_WC)

        with nc.Block() as block:
            @block.sync
            def _(sp):
                def load(g):
                    if g >= 2:
                        sp.wait_ge(tr_ok, GROUP * (g - 1))
                    sp.dma_start(h1[:, g % 2], h1_d.rearrange("(g t p) f -> g p t f", t=GROUP, p=P)[g]).then_inc(h_ld[g % 2], 16)

                load(0)
                with nc.allow_non_contiguous_dma("gate weights"):
                    for k in range(KC):
                        sp.dma_start(wgate[:, k], w_gate.rearrange("r (k p) a -> k p (r a)", p=P)[k]).then_inc(g_ld, 16)
                for c in range(0, MSG_WC, 2):
                    for k in range(KC):
                        sp.dma_start(raw[:, k, w_part(c)], w_rel.rearrange("r (k p) n -> k p r n", p=P)[k][:, w_part(c)]).then_inc(w_ld[c], 16)
                load(1)
                for u in range(HALVES):
                    sp.wait_ge(ev_act, 2 * (u + 1))
                    sp.wait_ge(ev_dve, 2 * (u + 1))
                    n_t, half = u // 2, u % 2
                    sp.dma_start(msg_d[n_t * P * RELS:(n_t + 1) * P * RELS, :].rearrange("(p q r) f -> q p (r f)", r=RELS // 2, q=2)[half],
                                 msg[:, u % SLOTS, :]).then_inc(msg_st[u % SLOTS], 16)
                    if half == 1 and n_t % GROUP == GROUP - 2 and n_t // GROUP + 2 < GROUPS:
                        load(n_t // GROUP + 2)
                for n in range(SLOTS):
                    sp.wait_ge(msg_st[n], 16 * ((HALVES + SLOTS - 1 - n) // SLOTS))

            @block.scalar
            def _(act):
                def turned_h(n):
                    act.wait_ge(tr_ok, n + 1)
                    if n >= 2:
                        act.wait_ge(msg_mm, PAIRS * (n - 1))
                    nc.scalar.activation(hT[:, n % 2], tr_ps[n % 2][:], ACT.Relu)
                    nc.scalar.activation(hTs[:, n % 2, 0], tr_ps[n % 2][:], ACT.Relu).then_inc(ht_ok, 1)

                for c in range(1, MSG_WC, 2):
                    for k in range(KC):
                        act.dma_start(raw[:, k, w_part(c)], w_rel.rearrange("r (k p) n -> k p r n", p=P)[k][:, w_part(c)]).then_inc(w_ld[c], 16)
                turned_h(0)
                for c in range(MSG_WC):
                    act.wait_ge(w_ld[c], 16 * KC)
                    nc.scalar.copy(wrel[:, 0, :, w_part(c)], raw[:, :, w_part(c)]).then_inc(w_hi, 1)
                for n in range(NODE_TILES):
                    if n + 1 < NODE_TILES:
                        turned_h(n + 1)
                    act.wait_ge(gate_mm, n + 1)
                    if n >= 2:
                        act.wait_ge(ev_dve, (PAIRS // 2) * (n - 1))
                        act.wait_ge(ev_act, (PAIRS // 2) * (n - 1))
                    nc.scalar.activation(gate[:, n % 2], gate_ps[:], ACT.Sigmoid).then_inc(gate_ok, 1)
                    act.wait_ge(gate_ok, n + 1)
                    for c in range(1, PAIRS, 2):
                        u = 2 * n + c // (PAIRS // 2)
                        if u >= SLOTS:
                            act.wait_ge(msg_st[u % SLOTS], 16 * (u // SLOTS))
                        act.wait_ge(msg_mm, PAIRS * n + c + 1)
                        c0 = (c % (PAIRS // 2)) * 2 * FEAT
                        for r in range(2):
                            last = nc.scalar.mul(msg[:, u % SLOTS, c0 + r * FEAT:c0 + (r + 1) * FEAT],
                                                 mm_ps[(PAIRS * n + c) % BANKS][:, r * FEAT:(r + 1) * FEAT],
                                                 gate[:, n % 2, 2 * c + r:2 * c + r + 1])
                        last.then_inc(ev_act, 1)

            @block.vector
            def _(dve):
                def low(n):
                    dve.wait_ge(ht_ok, n + 1)
                    nc.vector.tensor_tensor(hTs[:, n % 2, 1], hT[:, n % 2], hTs[:, n % 2, 0].bitcast(F32), ALU.subtract).then_inc(lo_ok, 1)

                low(0)
                for c in range(MSG_WC):
                    dve.wait_ge(w_hi, c + 1)
                    nc.vector.tensor_tensor(wrel[:, 1, :, w_part(c)], raw[:, :, w_part(c)], wrel[:, 0, :, w_part(c)].bitcast(F32),
                                            ALU.subtract).then_inc(w_lo, 1)
                for n in range(NODE_TILES):
                    if n + 1 < NODE_TILES:
                        low(n + 1)
                    dve.wait_ge(gate_ok, n + 1)
                    for c in range(0, PAIRS, 2):
                        u = 2 * n + c // (PAIRS // 2)
                        if u >= SLOTS:
                            dve.wait_ge(msg_st[u % SLOTS], 16 * (u // SLOTS))
                        dve.wait_ge(msg_mm, PAIRS * n + c + 1)
                        c0 = (c % (PAIRS // 2)) * 2 * FEAT
                        nc.vector.tensor_tensor(
                            msg[:, u % SLOTS, c0:c0 + 2 * FEAT].rearrange("p (r f) -> p r f", r=2),
                            mm_ps[(PAIRS * n + c) % BANKS][:].rearrange("p (r f) -> p r f", r=2),
                            gate[:, n % 2, 2 * c:2 * c + 2].rearrange("p (r o) -> p r o", o=1).to_broadcast([P, 2, FEAT]),
                            ALU.mult).then_inc(ev_dve, 1)

            @block.tensor
            def _(pe):
                PARTS = ((0, 0), (0, 1), (1, 0))

                def turn(n):
                    if n % GROUP == 0:
                        g = n // GROUP
                        pe.wait_ge(h_ld[g % 2], 16 * (g // 2 + 1))
                    if n >= 2:
                        pe.wait_ge(ht_ok, n - 1)
                    for k in range(KC):
                        last = nc.tensor.transpose(tr_ps[n % 2][:, k, :], h1[:, n // GROUP % 2, n % GROUP, k * P:(k + 1) * P], ident[:])
                    last.then_inc(tr_ok, 1)

                turn(0)
                pe.wait_ge(g_ld, 16 * KC)
                for n in range(NODE_TILES):
                    if n + 1 < NODE_TILES:
                        turn(n + 1)
                    pe.wait_ge(ht_ok, n + 1)
                    if n >= 1:
                        pe.wait_ge(gate_ok, n)
                    for k in range(KC):
                        last = nc.tensor.matmul(gate_ps[:], hT[:, n % 2, k, :], wgate[:, k, :], start=(k == 0), stop=(k == KC - 1))
                    last.then_inc(gate_mm, 1)
                    pe.wait_ge(lo_ok, n + 1)
                    for c in range(PAIRS):
                        if n == 0 and c % (PAIRS // MSG_WC) == 0:
                            pe.wait_ge(w_lo, c // (PAIRS // MSG_WC) + 1)
                        m = PAIRS * n + c
                        old = m - BANKS
                        if old >= 0:
                            pe.wait_ge(ev_act if old % 2 else ev_dve, old // 2 + 1)
                        parts = [(k, a, b) for k in range(KC) for a, b in PARTS]
                        for i, (k, a, b) in enumerate(parts):
                            last = nc.tensor.matmul(mm_ps[m % BANKS][:], hTs[:, n % 2, a, k, :],
                                                    wrel[:, b, k, 2 * c:2 * c + 2, :].rearrange("p r f -> p (r f)"),
                                                    start=(i == 0), stop=(i == len(parts) - 1))
                        last.then_inc(msg_mm, 1)


def finish(nc, sb, sem, x1, sums, out):
    dve_did, st = sem("fin_dve"), sem("fin_st")
    sums = sums[:].rearrange("p (g t f) -> p g t f", g=GROUPS, t=GROUP)
    with nc.Block() as block:
        @block.sync
        def _(sp):
            for g in range(GROUPS):
                sp.wait_ge(dve_did, g + 1)
                last = g == GROUPS - 1
                tiles = GROUP - 1 if last else GROUP
                r0 = g * GROUP * P
                sp.dma_start(out[r0:r0 + tiles * P, :].rearrange("(t p) f -> p t f", p=P), x1[:, g, 0:tiles]).then_inc(st, 16)
                if last:
                    sp.dma_start(out[NODES - LAST_ROWS:, :], x1[0:LAST_ROWS, g, tiles]).then_inc(st, 16)
            sp.wait_ge(st, 16 * (GROUPS + 1))

        @block.vector
        def _(dve):
            for g in range(GROUPS):
                nc.vector.scalar_tensor_tensor(out=x1[:, g], in0=sums[:, g], scalar=0.0, in1=x1[:, g],
                                               op0=ALU.max, op1=ALU.add).then_inc(dve_did, 1)


_OUT = ((NODES, FEAT), "float32")
_NAMES = ["x", "src", "dst", "edge_type_16", "edge_weight1", "L0_gnn_Wqkv", "L0_gnn_bqkv", "L0_gnn_ln_attn_g",
          "L0_gnn_ln_attn_b", "L0_gnn_ln_res_g", "L0_gnn_ln_res_b", "L0_gnn_W_in", "L0_gnn_b_in", "L0_gnn_W_out",
          "L0_gnn_b_out", "L1_gnn_weight", "L1_gnn_gate_weight"]


def kernel(**inputs):
    import numpy as _np
    import concourse.bacc as _bacc
    from concourse import mybir as _mybir
    from concourse.bass_utils import run_bass_kernel_spmd as _run

    nc = _bacc.Bacc("TRN2", target_bir_lowering=False, num_devices=1)
    arrays, args = {}, []
    for name in _NAMES:
        a = _np.asarray(inputs[name])
        if name == "x":
            a = _np.pad(a, ((0, NODES_PAD - NODES), (0, 0)))
        if name in ("src", "edge_type_16"):
            a = _np.pad(a, (0, EDGES_PAD - EDGES))
        if name == "dst":
            a = _np.pad(a, (0, EDGES_PAD - EDGES), constant_values=DST_PAD)
        if name == "edge_weight1":
            a = _np.pad(a.reshape(EDGES), (0, EDGES_PAD - EDGES))
        a = _np.ascontiguousarray(a)
        arrays[f"in_{name}_dram"] = a
        args.append(nc.dram_tensor(f"in_{name}_dram", a.shape, _mybir.dt.from_np(a.dtype), kind="ExternalInput").ap())
    args.append(nc.dram_tensor("out_0_dram", _OUT[0], _mybir.dt.from_np(_np.dtype(_OUT[1])), kind="ExternalOutput").ap())
    gnn_program(nc, *args)
    r = _run(nc, [arrays], core_ids=[0])
    return r.results[0]["out_0_dram"]
```
